# Optimizing a Trainium2 kernel written in Bass

```python
import numpy as np
import jax
import jax.numpy as jnp

def _softmax(x, axis=-1):
    return jax.nn.softmax(x, axis=axis)

def _gelu(x):
    return jax.nn.gelu(x, approximate=True)

def _silu(x):
    return jax.nn.silu(x)

def _sigmoid(x):
    return jax.nn.sigmoid(x)

def _layernorm(x, axis=-1, eps=1e-05):
    m = jnp.mean(x, axis=axis, keepdims=True)
    v = jnp.var(x, axis=axis, keepdims=True)
    return (x - m) / jnp.sqrt(v + eps)

def _scatter_add(tgt, idx, src, axis=0):
    return tgt.at[idx].add(src)

def _segment_sum(src, seg, n):
    return jax.ops.segment_sum(src, seg, n)
kernel_name = 'mk_xattn_ffn_d4_seqx_r8_2ee006'

def setup_inputs(seed: int=0):
    np.random.seed(seed)
    _w = jnp.asarray

    def _rec_inputs():
        import jax
        import jax.numpy as jnp
        _rk = jax.random.key(seed)
        x = -0.0002928 + 1 * jax.random.normal(jax.random.fold_in(_rk, 1), (16, 128, 128), jnp.float32)
        _lenS = 128 - jax.random.randint(jax.random.fold_in(_rk, 7), (16,), 0, max(1, 128 // 4) + 1, jnp.int32)
        _lenS2 = 128 - jax.random.randint(jax.random.fold_in(_rk, 8), (16,), 0, max(1, 128 // 4) + 1, jnp.int32)
        _ctx_1024P = jax.random.normal(jax.random.fold_in(_rk, 11), (16, 16, 128), jnp.float32)
        _ctx_1024c = jax.random.dirichlet(jax.random.fold_in(_rk, 511), 0.3 * jnp.ones((16,), jnp.float32), (16, 128))
        _ctx_1024t = jnp.einsum('bsk,bkd->bsd', _ctx_1024c, _ctx_1024P)
        _ctx_1024t = _ctx_1024t * jax.lax.rsqrt(jnp.mean(jnp.square(_ctx_1024t)) + 1e-12) * 0.953939
        ctx_1024 = -1.52775e-05 + 0.999936 * (_ctx_1024t + 0.3 * jax.random.normal(jax.random.fold_in(_rk, 611), (16, 128, 128), jnp.float32))
        pos_1xS2 = jnp.broadcast_to(jnp.arange(128, dtype=jnp.int32), (1, 128))
        _validS = jnp.arange(128)[None, :] < _lenS[:, None]
        _validS2 = jnp.arange(128)[None, :] < _lenS2[:, None]
        _causal = jnp.tril(jnp.ones((128, 128), dtype=bool))
        mask_BxS2_bf1 = jnp.ones((16, 128), dtype=bool)
        return (x, ctx_1024, pos_1xS2, mask_BxS2_bf1)
    x, ctx_1024, pos_1xS2, mask_BxS2_bf1 = _rec_inputs()

    def _L0_xattn_setup():
        import jax, jax.numpy as jnp
        import numpy as np
        DIM = 128
        NUM_HEADS = 8
        HEAD_DIM = 64
        INNER = NUM_HEADS * HEAD_DIM
        key = jax.random.key(seed)
        ks = jax.random.split(key, 7)
        B, N, M = (8, 64, 512)
        x = jax.random.normal(ks[0], (B, N, DIM), dtype=jnp.float32)
        context = jax.random.normal(ks[1], (B, M, DIM), dtype=jnp.float32)
        s_in = 1.0 / np.sqrt(DIM)
        s_inner = 1.0 / np.sqrt(INNER)
        Wq = jax.random.normal(ks[2], (DIM, INNER), dtype=jnp.float32) * s_in
        Wk = jax.random.normal(ks[3], (DIM, INNER), dtype=jnp.float32) * s_in
        Wv = jax.random.normal(ks[4], (DIM, INNER), dtype=jnp.float32) * s_in
        Wo = jax.random.normal(ks[5], (INNER, DIM), dtype=jnp.float32) * s_inner
        bo = jax.random.normal(ks[6], (DIM,), dtype=jnp.float32) * 0.01
        return {'x': x, 'context': context, 'Wq': Wq, 'Wk': Wk, 'Wv': Wv, 'Wo': Wo, 'bo': bo}
    _L0_xattn_all = _L0_xattn_setup()
    _L0_xattn_in = {k: v for k, v in _L0_xattn_all.items() if k in ('Wq', 'Wk', 'Wv', 'Wo', 'bo')}
    del _L0_xattn_all

    def _L0_ffn_setup():
        import jax, jax.numpy as jnp
        import numpy as np
        B, S, D = (2, 128, 128)
        H, HD = (16, 64)
        E_R = 31
        K_ACT = 3
        INTER = 128
        EPS = 1e-05
        BASE = 10000.0

        def _rmsnorm(x, gamma):
            rms = jnp.sqrt(jnp.mean(x * x, axis=-1, keepdims=True) + EPS)
            return x / rms * gamma

        def _rope(x, theta):
            seq = x.shape[2]
            angles = jnp.arange(seq, dtype=theta.dtype)[:, None] * theta
            cos = jnp.cos(angles)[None, None]
            sin = jnp.sin(angles)[None, None]
            x1, x2 = (x[..., 0::2], x[..., 1::2])
            return jnp.concatenate([x1 * cos - x2 * sin, x1 * sin + x2 * cos], axis=-1)

        def _forward(x, theta, gamma1, gamma2, q_w, q_b, k_w, k_b, v_w, v_b, o_w, o_b, router_w, router_b, sh_w1, sh_b1, sh_w2, sh_b2, re_w1, re_b1, re_w2, re_b2):
            b, s, d = x.shape
            xn = _rmsnorm(x, gamma1)
            q = (xn @ q_w + q_b).reshape(b, s, H, HD).transpose(0, 2, 1, 3)
            k = (xn @ k_w + k_b).reshape(b, s, H, HD).transpose(0, 2, 1, 3)
            v = (xn @ v_w + v_b).reshape(b, s, H, HD).transpose(0, 2, 1, 3)
            q = _rope(q, theta)
            k = _rope(k, theta)
            scale = 1.0 / np.sqrt(HD)
            scores = jnp.einsum('bhqd,bhkd->bhqk', q, k) * scale
            causal = jnp.tril(jnp.ones((s, s), dtype=bool))
            scores = jnp.where(causal, scores, -jnp.inf)
            attn = jax.nn.softmax(scores, axis=-1)
            ctx = jnp.einsum('bhqk,bhkd->bhqd', attn, v)
            ctx = ctx.transpose(0, 2, 1, 3).reshape(b, s, H * HD)
            attn_out = ctx @ o_w + o_b + xn
            an = _rmsnorm(attn_out, gamma2)
            shared = jax.nn.gelu(an @ sh_w1 + sh_b1, approximate=False) @ sh_w2 + sh_b2
            logits = an @ router_w + router_b
            aff = jax.nn.softmax(logits, axis=-1)
            topv, topi = jax.lax.top_k(aff, K_ACT)
            gates = jnp.sum(jax.nn.one_hot(topi, E_R, dtype=aff.dtype) * topv[..., None], axis=-2)
            h = jax.nn.gelu(jnp.einsum('bsd,edh->besh', an, re_w1) + re_b1[None, :, None, :], approximate=False)
            routed = jnp.einsum('bse,besh,ehd->bsd', gates, h, re_w2) + jnp.einsum('bse,ed->bsd', gates, re_b2)
            return shared + routed + an + attn_out
        key = jax.random.key(seed)
        ks = jax.random.split(key, 24)
        s = 0.02
        theta = BASE ** (-jnp.arange(HD // 2, dtype=jnp.float32) * 2.0 / HD)
        inp = {'x': jax.random.normal(ks[0], (B, S, D), jnp.float32), 'positions': jnp.arange(S, dtype=jnp.int32), 'theta': theta, 'gamma1': jnp.ones((D,), jnp.float32), 'gamma2': jnp.ones((D,), jnp.float32), 'q_w': jax.random.normal(ks[1], (D, H * HD), jnp.float32) * s, 'q_b': jnp.zeros((H * HD,), jnp.float32), 'k_w': jax.random.normal(ks[2], (D, H * HD), jnp.float32) * s, 'k_b': jnp.zeros((H * HD,), jnp.float32), 'v_w': jax.random.normal(ks[3], (D, H * HD), jnp.float32) * s, 'v_b': jnp.zeros((H * HD,), jnp.float32), 'o_w': jax.random.normal(ks[4], (H * HD, D), jnp.float32) * s, 'o_b': jnp.zeros((D,), jnp.float32), 'router_w': jax.random.normal(ks[5], (D, E_R), jnp.float32) * s, 'router_b': jnp.zeros((E_R,), jnp.float32), 'sh_w1': jax.random.normal(ks[6], (D, INTER), jnp.float32) * s, 'sh_b1': jnp.zeros((INTER,), jnp.float32), 'sh_w2': jax.random.normal(ks[7], (INTER, D), jnp.float32) * s, 'sh_b2': jnp.zeros((D,), jnp.float32), 're_w1': jax.random.normal(ks[8], (E_R, D, INTER), jnp.float32) * s, 're_b1': jnp.zeros((E_R, INTER), jnp.float32), 're_w2': jax.random.normal(ks[9], (E_R, INTER, D), jnp.float32) * s, 're_b2': jnp.zeros((E_R, D), jnp.float32)}
        return inp
    _L0_ffn_all = _L0_ffn_setup()
    _L0_ffn_in = {k: v for k, v in _L0_ffn_all.items() if k in ('positions', 'theta', 'gamma1', 'gamma2', 'q_w', 'q_b', 'k_w', 'k_b', 'v_w', 'v_b', 'o_w', 'o_b', 'router_w', 'router_b', 'sh_w1', 'sh_b1', 'sh_w2', 'sh_b2', 're_w1', 're_b1', 're_w2', 're_b2')}
    del _L0_ffn_all

    def _L1_xattn_setup():
        import jax, jax.numpy as jnp
        import numpy as np
        EMB = 128
        HEADS = 16
        HEAD_DIM = EMB // HEADS
        EPS = 1e-05

        def _layer_norm(x, gamma, beta):
            m = jnp.mean(x, axis=-1, keepdims=True)
            v = jnp.mean(jnp.square(x - m), axis=-1, keepdims=True)
            return (x - m) / jnp.sqrt(v + EPS) * gamma + beta
        key = jax.random.key(seed)
        ks = jax.random.split(key, 8)
        B, Tx, Tc = (2, 128, 1024)
        scale = 1.0 / np.sqrt(EMB)
        return {'x': jax.random.normal(ks[0], (B, Tx, EMB), dtype=jnp.float32), 'context': jax.random.normal(ks[1], (B, Tc, EMB), dtype=jnp.float32), 'context_mask': jnp.ones((B, Tc), dtype=bool), 'Wq': jax.random.normal(ks[2], (EMB, EMB), dtype=jnp.float32) * scale, 'Wk': jax.random.normal(ks[3], (EMB, EMB), dtype=jnp.float32) * scale, 'Wv': jax.random.normal(ks[4], (EMB, EMB), dtype=jnp.float32) * scale, 'Wo': jax.random.normal(ks[5], (EMB, EMB), dtype=jnp.float32) * scale, 'bo': jnp.zeros((EMB,), dtype=jnp.float32), 'g1': jnp.ones((EMB,), dtype=jnp.float32), 'b1': jnp.zeros((EMB,), dtype=jnp.float32), 'g2': jnp.ones((EMB,), dtype=jnp.float32), 'b2': jnp.zeros((EMB,), dtype=jnp.float32)}
    _L1_xattn_all = _L1_xattn_setup()
    _L1_xattn_in = {k: v for k, v in _L1_xattn_all.items() if k in ('Wq', 'Wk', 'Wv', 'Wo', 'bo', 'g1', 'b1', 'g2', 'b2')}
    del _L1_xattn_all

    def _L1_ffn_setup():
        import jax, jax.numpy as jnp
        import numpy as np
        HID = 128
        NH = 16
        NKV = 4
        HD = HID // NH
        E = 8
        TOPK = 2
        FFN = 256
        EPS = 1e-05
        THETA = 10000.0

        def _rmsnorm(x, w):
            var = jnp.mean(x * x, axis=-1, keepdims=True)
            return x * jax.lax.rsqrt(var + EPS) * w

        def _rope_tables(S):
            inv_freq = 1.0 / THETA ** (jnp.arange(0, HD, 2, dtype=jnp.float32) / HD)
            freqs = jnp.arange(S, dtype=jnp.float32)[:, None] * inv_freq[None, :]
            emb = jnp.concatenate([freqs, freqs], axis=-1)
            return (jnp.cos(emb), jnp.sin(emb))

        def _apply_rope(t, cos, sin):
            t1, t2 = jnp.split(t, 2, axis=-1)
            rot = jnp.concatenate([-t2, t1], axis=-1)
            return t * cos[None, :, None, :] + rot * sin[None, :, None, :]
        key = jax.random.key(seed)
        ks = jax.random.split(key, 6)
        B, S = (1, 256)
        x = jax.random.normal(ks[0], (B, S, HID), dtype=jnp.float32)
        wqkv = jax.random.normal(ks[1], ((NH + 2 * NKV) * HD, HID), dtype=jnp.float32) * 0.02
        wo = jax.random.normal(ks[2], (HID, NH * HD), dtype=jnp.float32) * 0.02
        gate_w = jax.random.normal(ks[3], (E, HID), dtype=jnp.float32) * 0.02
        w13 = jax.random.normal(ks[4], (E, 2 * FFN, HID), dtype=jnp.float32) * 0.02
        w2 = jax.random.normal(ks[5], (E, HID, FFN), dtype=jnp.float32) * 0.02
        return {'x': x, 'ln1_w': jnp.ones((HID,), jnp.float32), 'ln2_w': jnp.ones((HID,), jnp.float32), 'wqkv': wqkv, 'wo': wo, 'gate_w': gate_w, 'w13': w13, 'w2': w2}
    _L1_ffn_all = _L1_ffn_setup()
    _L1_ffn_in = {k: v for k, v in _L1_ffn_all.items() if k in ('ln1_w', 'ln2_w', 'wqkv', 'wo', 'gate_w', 'w13', 'w2')}
    del _L1_ffn_all

    def _L2_xattn_setup():
        import jax, jax.numpy as jnp
        import numpy as np
        D1, D2, D3 = (128, 128, 128)
        key = jax.random.key(seed)
        k1, k2, kw, kb = jax.random.split(key, 4)
        x1 = jax.random.normal(k1, (8, 256, D1), dtype=jnp.float32)
        x2 = jax.random.normal(k2, (8, 256, D2), dtype=jnp.float32)
        bound = 1.0 / np.sqrt(D1 + D2)
        W = jax.random.uniform(kw, (D3, D1 + D2), minval=-bound, maxval=bound, dtype=jnp.float32)
        b = jax.random.uniform(kb, (D3,), minval=-bound, maxval=bound, dtype=jnp.float32)
        return {'x1': x1, 'x2': x2, 'W': W, 'b': b}
    _L2_xattn_all = _L2_xattn_setup()
    _L2_xattn_in = {k: v for k, v in _L2_xattn_all.items() if k in ('W', 'b')}
    del _L2_xattn_all

    def _L2_ffn_setup():
        import jax, jax.numpy as jnp
        import numpy as np
        D = 128
        I = 64
        E = 32
        K = 4
        T = 2 * 256
        C = 2 * T * K // E
        key = jax.random.key(seed)
        ks = jax.random.split(key, 9)
        bf = jnp.bfloat16
        std = 0.02
        x = jax.random.normal(ks[0], (2, 256, D), dtype=jnp.float32).astype(bf)
        gate_w = (std * jax.random.normal(ks[1], (E, D), dtype=jnp.float32)).astype(bf)
        bias = jnp.zeros((E,), jnp.float32)
        W1 = (std * jax.random.normal(ks[2], (E, D, I), dtype=jnp.float32)).astype(bf)
        W3 = (std * jax.random.normal(ks[3], (E, D, I), dtype=jnp.float32)).astype(bf)
        W2 = (std * jax.random.normal(ks[4], (E, I, D), dtype=jnp.float32)).astype(bf)
        sw1 = (std * jax.random.normal(ks[5], (I, D), dtype=jnp.float32)).astype(bf)
        sw3 = (std * jax.random.normal(ks[6], (I, D), dtype=jnp.float32)).astype(bf)
        sw2 = (std * jax.random.normal(ks[7], (D, I), dtype=jnp.float32)).astype(bf)
        return {'x': x, 'gate_w': gate_w, 'bias': bias, 'W1': W1, 'W3': W3, 'W2': W2, 'sw1': sw1, 'sw3': sw3, 'sw2': sw2}
    _L2_ffn_all = _L2_ffn_setup()
    _L2_ffn_in = {k: v for k, v in _L2_ffn_all.items() if k in ('gate_w', 'bias', 'W1', 'W3', 'W2', 'sw1', 'sw3', 'sw2')}
    del _L2_ffn_all

    def _L3_xattn_setup():
        import jax, jax.numpy as jnp
        import numpy as np
        import math
        G_SIZE = 16
        W_SIZE = 64

        def _pos_encoding(seq_len, dim, dtype):
            position = jnp.arange(seq_len, dtype=dtype)[:, None]
            div_term = jnp.exp(jnp.arange(0, dim, 2, dtype=dtype) * -(math.log(10000.0) / dim))
            ang = position * div_term
            return jnp.stack([jnp.sin(ang), jnp.cos(ang)], axis=-1).reshape(seq_len, dim)
        key = jax.random.key(seed)
        kq, kk, kv = jax.random.split(key, 3)
        B, S, D = (2, 512, 128)
        q = jax.random.normal(kq, (B, S, D), jnp.float32)
        k = jax.random.normal(kk, (B, S, D), jnp.float32)
        v = jax.random.normal(kv, (B, S, D), jnp.float32)
        pos = jnp.arange(S, dtype=jnp.int32)[None, :]
        return {'q': q, 'k': k, 'v': v, 'pos': pos}
    _L3_xattn_all = _L3_xattn_setup()
    _L3_xattn_in = {k: v for k, v in _L3_xattn_all.items() if k in ()}
    del _L3_xattn_all

    def _L3_ffn_setup():
        import jax, jax.numpy as jnp
        import numpy as np
        BLOCK = 32
        W_BITS = 4
        ACT_BITS = 16

        def act_qdq(x):
            qmax = 2.0 ** (ACT_BITS - 1) - 1.0
            scale = jnp.maximum(jnp.max(jnp.abs(x)) / qmax, 1e-12)
            return jnp.clip(jnp.round(x / scale), -qmax - 1.0, qmax) * scale

        def fixed_qdq_u16(x):
            scale = 1.0 / 65536.0
            return jnp.clip(jnp.round(x / scale), 0.0, 65535.0) * scale

        def lpbq_dequant(w):
            O, I = w.shape
            qmax = 2.0 ** (W_BITS - 1) - 1.0
            wb = w.reshape(O, I // BLOCK, BLOCK)
            s = jnp.maximum(jnp.max(jnp.abs(wb), axis=-1, keepdims=True) / qmax, 1e-12)
            wq = jnp.clip(jnp.round(wb / s), -qmax - 1.0, qmax) * s
            return wq.reshape(O, I)
        key = jax.random.key(seed)
        k1, k2, k3, k4 = jax.random.split(key, 4)
        B, S, H, I = (2, 512, 128, 384)
        x = jax.random.normal(k1, (B, S, H), jnp.float32)
        w_gate = jax.random.normal(k2, (I, H), jnp.float32) * 0.02
        w_up = jax.random.normal(k3, (I, H), jnp.float32) * 0.02
        w_down = jax.random.normal(k4, (H, I), jnp.float32) * 0.02
        return {'x': x, 'w_gate': w_gate, 'w_up': w_up, 'w_down': w_down}
    _L3_ffn_all = _L3_ffn_setup()
    _L3_ffn_in = {k: v for k, v in _L3_ffn_all.items() if k in ('w_gate', 'w_up', 'w_down')}
    del _L3_ffn_all
    return {'x': x, 'ctx_1024': ctx_1024, 'pos_1xS2': pos_1xS2, 'mask_BxS2_bf1': mask_BxS2_bf1, 'L0_xattn_Wq': _L0_xattn_in['Wq'], 'L0_xattn_Wk': _L0_xattn_in['Wk'], 'L0_xattn_Wv': _L0_xattn_in['Wv'], 'L0_xattn_Wo': _L0_xattn_in['Wo'], 'L0_xattn_bo': _L0_xattn_in['bo'], 'L0_ffn_positions': _L0_ffn_in['positions'], 'L0_ffn_theta': _L0_ffn_in['theta'], 'L0_ffn_gamma1': _L0_ffn_in['gamma1'], 'L0_ffn_gamma2': _L0_ffn_in['gamma2'], 'L0_ffn_q_w': _L0_ffn_in['q_w'], 'L0_ffn_q_b': _L0_ffn_in['q_b'], 'L0_ffn_k_w': _L0_ffn_in['k_w'], 'L0_ffn_k_b': _L0_ffn_in['k_b'], 'L0_ffn_v_w': _L0_ffn_in['v_w'], 'L0_ffn_v_b': _L0_ffn_in['v_b'], 'L0_ffn_o_w': _L0_ffn_in['o_w'], 'L0_ffn_o_b': _L0_ffn_in['o_b'], 'L0_ffn_router_w': _L0_ffn_in['router_w'], 'L0_ffn_router_b': _L0_ffn_in['router_b'], 'L0_ffn_sh_w1': _L0_ffn_in['sh_w1'], 'L0_ffn_sh_b1': _L0_ffn_in['sh_b1'], 'L0_ffn_sh_w2': _L0_ffn_in['sh_w2'], 'L0_ffn_sh_b2': _L0_ffn_in['sh_b2'], 'L0_ffn_re_w1': _L0_ffn_in['re_w1'], 'L0_ffn_re_b1': _L0_ffn_in['re_b1'], 'L0_ffn_re_w2': _L0_ffn_in['re_w2'], 'L0_ffn_re_b2': _L0_ffn_in['re_b2'], 'L1_xattn_Wq': _L1_xattn_in['Wq'], 'L1_xattn_Wk': _L1_xattn_in['Wk'], 'L1_xattn_Wv': _L1_xattn_in['Wv'], 'L1_xattn_Wo': _L1_xattn_in['Wo'], 'L1_xattn_bo': _L1_xattn_in['bo'], 'L1_xattn_g1': _L1_xattn_in['g1'], 'L1_xattn_b1': _L1_xattn_in['b1'], 'L1_xattn_g2': _L1_xattn_in['g2'], 'L1_xattn_b2': _L1_xattn_in['b2'], 'L1_ffn_ln1_w': _L1_ffn_in['ln1_w'], 'L1_ffn_ln2_w': _L1_ffn_in['ln2_w'], 'L1_ffn_wqkv': _L1_ffn_in['wqkv'], 'L1_ffn_wo': _L1_ffn_in['wo'], 'L1_ffn_gate_w': _L1_ffn_in['gate_w'], 'L1_ffn_w13': _L1_ffn_in['w13'], 'L1_ffn_w2': _L1_ffn_in['w2'], 'L2_xattn_W': _L2_xattn_in['W'], 'L2_xattn_b': _L2_xattn_in['b'], 'L2_ffn_gate_w': _L2_ffn_in['gate_w'], 'L2_ffn_bias': _L2_ffn_in['bias'], 'L2_ffn_W1': _L2_ffn_in['W1'], 'L2_ffn_W3': _L2_ffn_in['W3'], 'L2_ffn_W2': _L2_ffn_in['W2'], 'L2_ffn_sw1': _L2_ffn_in['sw1'], 'L2_ffn_sw3': _L2_ffn_in['sw3'], 'L2_ffn_sw2': _L2_ffn_in['sw2'], 'L3_ffn_w_gate': _L3_ffn_in['w_gate'], 'L3_ffn_w_up': _L3_ffn_in['w_up'], 'L3_ffn_w_down': _L3_ffn_in['w_down']}

def reference(x, ctx_1024, pos_1xS2, mask_BxS2_bf1, L0_xattn_Wq, L0_xattn_Wk, L0_xattn_Wv, L0_xattn_Wo, L0_xattn_bo, L0_ffn_positions, L0_ffn_theta, L0_ffn_gamma1, L0_ffn_gamma2, L0_ffn_q_w, L0_ffn_q_b, L0_ffn_k_w, L0_ffn_k_b, L0_ffn_v_w, L0_ffn_v_b, L0_ffn_o_w, L0_ffn_o_b, L0_ffn_router_w, L0_ffn_router_b, L0_ffn_sh_w1, L0_ffn_sh_b1, L0_ffn_sh_w2, L0_ffn_sh_b2, L0_ffn_re_w1, L0_ffn_re_b1, L0_ffn_re_w2, L0_ffn_re_b2, L1_xattn_Wq, L1_xattn_Wk, L1_xattn_Wv, L1_xattn_Wo, L1_xattn_bo, L1_xattn_g1, L1_xattn_b1, L1_xattn_g2, L1_xattn_b2, L1_ffn_ln1_w, L1_ffn_ln2_w, L1_ffn_wqkv, L1_ffn_wo, L1_ffn_gate_w, L1_ffn_w13, L1_ffn_w2, L2_xattn_W, L2_xattn_b, L2_ffn_gate_w, L2_ffn_bias, L2_ffn_W1, L2_ffn_W3, L2_ffn_W2, L2_ffn_sw1, L2_ffn_sw3, L2_ffn_sw2, L3_ffn_w_gate, L3_ffn_w_up, L3_ffn_w_down):
    import jax
    import jax.numpy as jnp

    def _L0_xattn_ref(x, context, Wq, Wk, Wv, Wo, bo):
        import jax, jax.numpy as jnp
        import numpy as np
        DIM = 128
        NUM_HEADS = 8
        HEAD_DIM = 64
        INNER = NUM_HEADS * HEAD_DIM
        B, N, _ = x.shape
        M = context.shape[1]
        scale = HEAD_DIM ** (-0.5)
        q = (x @ Wq).reshape(B, N, NUM_HEADS, HEAD_DIM).transpose(0, 2, 1, 3)
        k = (context @ Wk).reshape(B, M, NUM_HEADS, HEAD_DIM).transpose(0, 2, 1, 3)
        v = (context @ Wv).reshape(B, M, NUM_HEADS, HEAD_DIM).transpose(0, 2, 1, 3)
        attn = jax.nn.softmax(jnp.einsum('bhnd,bhmd->bhnm', q, k) * scale, axis=-1)
        out = jnp.einsum('bhnm,bhmd->bhnd', attn, v)
        out = out.transpose(0, 2, 1, 3).reshape(B, N, INNER)
        return out @ Wo + bo

    def _L0_ffn_ref(x, positions, theta, gamma1, gamma2, q_w, q_b, k_w, k_b, v_w, v_b, o_w, o_b, router_w, router_b, sh_w1, sh_b1, sh_w2, sh_b2, re_w1, re_b1, re_w2, re_b2):
        import jax, jax.numpy as jnp
        import numpy as np
        B, S, D = (2, 128, 128)
        H, HD = (16, 64)
        E_R = 31
        K_ACT = 3
        INTER = 128
        EPS = 1e-05
        BASE = 10000.0

        def _rmsnorm(x, gamma):
            rms = jnp.sqrt(jnp.mean(x * x, axis=-1, keepdims=True) + EPS)
            return x / rms * gamma

        def _rope(x, theta):
            seq = x.shape[2]
            angles = jnp.arange(seq, dtype=theta.dtype)[:, None] * theta
            cos = jnp.cos(angles)[None, None]
            sin = jnp.sin(angles)[None, None]
            x1, x2 = (x[..., 0::2], x[..., 1::2])
            return jnp.concatenate([x1 * cos - x2 * sin, x1 * sin + x2 * cos], axis=-1)

        def _forward(x, theta, gamma1, gamma2, q_w, q_b, k_w, k_b, v_w, v_b, o_w, o_b, router_w, router_b, sh_w1, sh_b1, sh_w2, sh_b2, re_w1, re_b1, re_w2, re_b2):
            b, s, d = x.shape
            xn = _rmsnorm(x, gamma1)
            q = (xn @ q_w + q_b).reshape(b, s, H, HD).transpose(0, 2, 1, 3)
            k = (xn @ k_w + k_b).reshape(b, s, H, HD).transpose(0, 2, 1, 3)
            v = (xn @ v_w + v_b).reshape(b, s, H, HD).transpose(0, 2, 1, 3)
            q = _rope(q, theta)
            k = _rope(k, theta)
            scale = 1.0 / np.sqrt(HD)
            scores = jnp.einsum('bhqd,bhkd->bhqk', q, k) * scale
            causal = jnp.tril(jnp.ones((s, s), dtype=bool))
            scores = jnp.where(causal, scores, -jnp.inf)
            attn = jax.nn.softmax(scores, axis=-1)
            ctx = jnp.einsum('bhqk,bhkd->bhqd', attn, v)
            ctx = ctx.transpose(0, 2, 1, 3).reshape(b, s, H * HD)
            attn_out = ctx @ o_w + o_b + xn
            an = _rmsnorm(attn_out, gamma2)
            shared = jax.nn.gelu(an @ sh_w1 + sh_b1, approximate=False) @ sh_w2 + sh_b2
            logits = an @ router_w + router_b
            aff = jax.nn.softmax(logits, axis=-1)
            topv, topi = jax.lax.top_k(aff, K_ACT)
            gates = jnp.sum(jax.nn.one_hot(topi, E_R, dtype=aff.dtype) * topv[..., None], axis=-2)
            h = jax.nn.gelu(jnp.einsum('bsd,edh->besh', an, re_w1) + re_b1[None, :, None, :], approximate=False)
            routed = jnp.einsum('bse,besh,ehd->bsd', gates, h, re_w2) + jnp.einsum('bse,ed->bsd', gates, re_b2)
            return shared + routed + an + attn_out
        del positions
        return _forward(x, theta, gamma1, gamma2, q_w, q_b, k_w, k_b, v_w, v_b, o_w, o_b, router_w, router_b, sh_w1, sh_b1, sh_w2, sh_b2, re_w1, re_b1, re_w2, re_b2)

    def _L1_xattn_ref(x, context, context_mask, Wq, Wk, Wv, Wo, bo, g1, b1, g2, b2):
        import jax, jax.numpy as jnp
        import numpy as np
        EMB = 128
        HEADS = 16
        HEAD_DIM = EMB // HEADS
        EPS = 1e-05

        def _layer_norm(x, gamma, beta):
            m = jnp.mean(x, axis=-1, keepdims=True)
            v = jnp.mean(jnp.square(x - m), axis=-1, keepdims=True)
            return (x - m) / jnp.sqrt(v + EPS) * gamma + beta
        B, Tx, C = x.shape
        Tc = context.shape[1]
        xn = _layer_norm(x, g1, b1)
        cn = _layer_norm(context, g2, b2)
        q = (xn @ Wq.T).reshape(B, Tx, HEADS, HEAD_DIM)
        k = (cn @ Wk.T).reshape(B, Tc, HEADS, HEAD_DIM)
        v = (cn @ Wv.T).reshape(B, Tc, HEADS, HEAD_DIM)
        scores = jnp.einsum('bqhs,bkhs->bhqk', q, k) / np.sqrt(HEAD_DIM)
        scores = jnp.where(context_mask[:, None, None, :], scores, -jnp.inf)
        attn = jax.nn.softmax(scores, axis=-1)
        out = jnp.einsum('bhqk,bkhs->bqhs', attn, v).reshape(B, Tx, C)
        return out @ Wo.T + bo

    def _L1_ffn_ref(x, ln1_w, ln2_w, wqkv, wo, gate_w, w13, w2):
        import jax, jax.numpy as jnp
        import numpy as np
        HID = 128
        NH = 16
        NKV = 4
        HD = HID // NH
        E = 8
        TOPK = 2
        FFN = 256
        EPS = 1e-05
        THETA = 10000.0

        def _rmsnorm(x, w):
            var = jnp.mean(x * x, axis=-1, keepdims=True)
            return x * jax.lax.rsqrt(var + EPS) * w

        def _rope_tables(S):
            inv_freq = 1.0 / THETA ** (jnp.arange(0, HD, 2, dtype=jnp.float32) / HD)
            freqs = jnp.arange(S, dtype=jnp.float32)[:, None] * inv_freq[None, :]
            emb = jnp.concatenate([freqs, freqs], axis=-1)
            return (jnp.cos(emb), jnp.sin(emb))

        def _apply_rope(t, cos, sin):
            t1, t2 = jnp.split(t, 2, axis=-1)
            rot = jnp.concatenate([-t2, t1], axis=-1)
            return t * cos[None, :, None, :] + rot * sin[None, :, None, :]
        B, S, _ = x.shape
        h = _rmsnorm(x, ln1_w)
        qkv = jnp.einsum('bsh,oh->bso', h, wqkv)
        q = qkv[..., :NH * HD].reshape(B, S, NH, HD)
        k = qkv[..., NH * HD:(NH + NKV) * HD].reshape(B, S, NKV, HD)
        v = qkv[..., (NH + NKV) * HD:].reshape(B, S, NKV, HD)
        cos, sin = _rope_tables(S)
        q = _apply_rope(q, cos, sin)
        k = _apply_rope(k, cos, sin)
        groups = NH // NKV
        k = jnp.repeat(k, groups, axis=2)
        v = jnp.repeat(v, groups, axis=2)
        scale = HD ** (-0.5)
        scores = jnp.einsum('bqhd,bkhd->bhqk', q, k) * scale
        causal = jnp.tril(jnp.ones((S, S), dtype=bool))
        scores = jnp.where(causal[None, None], scores, jnp.finfo(scores.dtype).min)
        probs = jax.nn.softmax(scores, axis=-1)
        attn = jnp.einsum('bhqk,bkhd->bqhd', probs, v).reshape(B, S, NH * HD)
        x = x + jnp.einsum('bso,ho->bsh', attn, wo)
        h = _rmsnorm(x, ln2_w).reshape(-1, HID)
        T = h.shape[0]
        logits = jnp.einsum('th,eh->te', h, gate_w)
        rprobs = jax.nn.softmax(logits.astype(jnp.float32), axis=-1)
        topw, topi = jax.lax.top_k(rprobs, TOPK)
        topw = topw / jnp.sum(topw, axis=-1, keepdims=True)
        wfull = jnp.zeros((T, E), jnp.float32).at[jnp.arange(T)[:, None], topi].set(topw)
        wfull = wfull.astype(h.dtype)
        out = jnp.zeros((T, HID), h.dtype)
        for e in range(E):
            w1 = w13[e, :FFN]
            w3 = w13[e, FFN:]
            g = jax.nn.silu(h @ w1.T) * (h @ w3.T)
            out = out + jnp.einsum('tf,hf->th', g, w2[e]) * wfull[:, e:e + 1]
        return x + out.reshape(B, S, HID)

    def _L2_xattn_ref(x1, x2, W, b):
        import jax, jax.numpy as jnp
        import numpy as np
        D1, D2, D3 = (128, 128, 128)
        d1 = x1.shape[-1]
        W1 = W[:, :d1]
        W2 = W[:, d1:]
        part1 = jnp.einsum('bld,ed->ble', x1, W1)
        part2 = jnp.einsum('bld,ed->be', x2, W2) / x2.shape[1]
        return part1 + part2[:, None, :] + b

    def _L2_ffn_ref(x, gate_w, bias, W1, W3, W2, sw1, sw3, sw2):
        import jax, jax.numpy as jnp
        import numpy as np
        D = 128
        I = 64
        E = 32
        K = 4
        T = 2 * 256
        C = 2 * T * K // E
        X = x.reshape(-1, D)
        logits = (X @ gate_w.T).astype(jnp.float32)
        scores = jax.nn.sigmoid(logits)
        _, idx = jax.lax.top_k(scores + bias[None, :], K)
        w = jnp.take_along_axis(scores, idx, axis=-1)
        w = w / jnp.clip(jnp.sum(w, axis=-1, keepdims=True), 1e-12, None)
        w = w.astype(x.dtype)
        eid = idx.reshape(-1)
        onehot = (eid[:, None] == jnp.arange(E)[None, :]).astype(jnp.int32)
        pos = jnp.take_along_axis(jnp.cumsum(onehot, axis=0) - 1, eid[:, None], axis=1)[:, 0]
        valid = pos < C
        posc = jnp.minimum(pos, C - 1)
        Xrep = jnp.repeat(X, K, axis=0)
        xe = jnp.zeros((E, C, D), x.dtype).at[eid, posc].add(jnp.where(valid[:, None], Xrep, jnp.zeros((), x.dtype)))
        h = jax.nn.silu(jnp.einsum('ecd,edi->eci', xe, W1)) * jnp.einsum('ecd,edi->eci', xe, W3)
        ye = jnp.einsum('eci,eid->ecd', h, W2)
        gflat = jnp.where(valid, w.reshape(-1), jnp.zeros((), x.dtype))
        yrows = ye[eid, posc] * gflat[:, None]
        out = yrows.reshape(-1, K, D).sum(axis=1)
        out = out + jax.nn.silu(X @ sw1.T) * (X @ sw3.T) @ sw2.T
        return out.reshape(x.shape)

    def _L3_xattn_ref(q, k, v, pos):
        import jax, jax.numpy as jnp
        import numpy as np
        import math
        G_SIZE = 16
        W_SIZE = 64

        def _pos_encoding(seq_len, dim, dtype):
            position = jnp.arange(seq_len, dtype=dtype)[:, None]
            div_term = jnp.exp(jnp.arange(0, dim, 2, dtype=dtype) * -(math.log(10000.0) / dim))
            ang = position * div_term
            return jnp.stack([jnp.sin(ang), jnp.cos(ang)], axis=-1).reshape(seq_len, dim)
        B, S, D = q.shape
        pe = _pos_encoding(S, D, q.dtype)
        neg = jnp.asarray(-jnp.inf, q.dtype)
        causal = jnp.tril(jnp.ones((S, S), bool))
        ngb_q = q + pe[pos]
        ngb_k = k + pe[pos]
        ngb_attn = jnp.where(causal, jnp.einsum('bqd,bkd->bqk', ngb_q, ngb_k), neg)
        g_pos = pos // G_SIZE
        s_g_pos = g_pos + (W_SIZE - W_SIZE // G_SIZE)
        g_q = q + pe[s_g_pos]
        g_k = k + pe[g_pos]
        g_attn = jnp.where(causal, jnp.einsum('bqd,bkd->bqk', g_q, g_k), neg)
        mask = jnp.ones((S, S), q.dtype)
        g_mask = jnp.tril(jnp.ones((S - W_SIZE, S - W_SIZE), q.dtype))
        mask = mask.at[W_SIZE:, :S - W_SIZE].add(-g_mask)
        attn = jnp.where(mask.astype(bool), ngb_attn, g_attn)
        w = jax.nn.softmax(attn, axis=-1)
        return jnp.einsum('bqk,bkd->bqd', w, v)

    def _L3_ffn_ref(x, w_gate, w_up, w_down):
        import jax, jax.numpy as jnp
        import numpy as np
        BLOCK = 32
        W_BITS = 4
        ACT_BITS = 16

        def act_qdq(x):
            qmax = 2.0 ** (ACT_BITS - 1) - 1.0
            scale = jnp.maximum(jnp.max(jnp.abs(x)) / qmax, 1e-12)
            return jnp.clip(jnp.round(x / scale), -qmax - 1.0, qmax) * scale

        def fixed_qdq_u16(x):
            scale = 1.0 / 65536.0
            return jnp.clip(jnp.round(x / scale), 0.0, 65535.0) * scale

        def lpbq_dequant(w):
            O, I = w.shape
            qmax = 2.0 ** (W_BITS - 1) - 1.0
            wb = w.reshape(O, I // BLOCK, BLOCK)
            s = jnp.maximum(jnp.max(jnp.abs(wb), axis=-1, keepdims=True) / qmax, 1e-12)
            wq = jnp.clip(jnp.round(wb / s), -qmax - 1.0, qmax) * s
            return wq.reshape(O, I)
        x = act_qdq(x)
        up = act_qdq(x @ lpbq_dequant(w_up).T)
        gate = act_qdq(x @ lpbq_dequant(w_gate).T)
        sig = fixed_qdq_u16(jax.nn.sigmoid(gate))
        gate = act_qdq(gate * sig)
        o = act_qdq(gate * up)
        return o @ lpbq_dequant(w_down).T
    x = x + _L0_xattn_ref(_layernorm(x, axis=-1), ctx_1024, L0_xattn_Wq, L0_xattn_Wk, L0_xattn_Wv, L0_xattn_Wo, L0_xattn_bo)
    x = x + _L0_ffn_ref(_layernorm(x, axis=-1), L0_ffn_positions, L0_ffn_theta, L0_ffn_gamma1, L0_ffn_gamma2, L0_ffn_q_w, L0_ffn_q_b, L0_ffn_k_w, L0_ffn_k_b, L0_ffn_v_w, L0_ffn_v_b, L0_ffn_o_w, L0_ffn_o_b, L0_ffn_router_w, L0_ffn_router_b, L0_ffn_sh_w1, L0_ffn_sh_b1, L0_ffn_sh_w2, L0_ffn_sh_b2, L0_ffn_re_w1, L0_ffn_re_b1, L0_ffn_re_w2, L0_ffn_re_b2)
    x = x + _L1_xattn_ref(_layernorm(x, axis=-1), ctx_1024, mask_BxS2_bf1, L1_xattn_Wq, L1_xattn_Wk, L1_xattn_Wv, L1_xattn_Wo, L1_xattn_bo, L1_xattn_g1, L1_xattn_b1, L1_xattn_g2, L1_xattn_b2)
    x = x + _L1_ffn_ref(_layernorm(x, axis=-1), L1_ffn_ln1_w, L1_ffn_ln2_w, L1_ffn_wqkv, L1_ffn_wo, L1_ffn_gate_w, L1_ffn_w13, L1_ffn_w2)
    x = x + _L2_xattn_ref(_layernorm(x, axis=-1), ctx_1024, L2_xattn_W, L2_xattn_b)
    x = x + _L2_ffn_ref(_layernorm(x, axis=-1), L2_ffn_gate_w, L2_ffn_bias, L2_ffn_W1, L2_ffn_W3, L2_ffn_W2, L2_ffn_sw1, L2_ffn_sw3, L2_ffn_sw2)
    x = x + _L3_xattn_ref(_layernorm(x, axis=-1), ctx_1024, ctx_1024, pos_1xS2)
    x = x + _L3_ffn_ref(_layernorm(x, axis=-1), L3_ffn_w_gate, L3_ffn_w_up, L3_ffn_w_down)
    return x

_drawn_inputs = setup_inputs


def setup_inputs(seed=0):
    import zlib

    import numpy as np

    out = dict(_drawn_inputs(seed))
    spreads = {'L0_ffn_gamma1': (1.0, 0.2),
     'L0_ffn_gamma2': (1.0, 0.2),
     'L0_ffn_q_b': (0.0, 0.8),
     'L0_ffn_k_b': (0.0, 0.8),
     'L0_ffn_v_b': (0.0, 0.1),
     'L0_ffn_o_b': (0.0, 0.1),
     'L0_ffn_router_b': (0.0, 0.8),
     'L0_ffn_sh_b1': (0.0, 0.8),
     'L0_ffn_sh_b2': (0.0, 0.1),
     'L0_ffn_re_b1': (0.0, 0.8),
     'L0_ffn_re_b2': (0.0, 0.8),
     'L1_xattn_bo': (0.0, 0.1),
     'L1_xattn_g1': (1.0, 0.6),
     'L1_xattn_b1': (0.0, 0.8),
     'L1_xattn_g2': (1.0, 0.2),
     'L1_xattn_b2': (0.0, 0.308),
     'L1_ffn_ln1_w': (1.0, 0.6),
     'L1_ffn_ln2_w': (1.0, 0.6),
     'L2_ffn_bias': (0.0, 0.8)}
    factors = {'L0_xattn_bo': 5.928,
     'L0_ffn_theta': 8.0,
     'L0_ffn_q_w': 8.0,
     'L0_ffn_k_w': 8.0,
     'L0_ffn_router_w': 8.0,
     'L0_ffn_sh_w1': 6.257,
     'L0_ffn_sh_w2': 5.758,
     'L0_ffn_re_w1': 8.0,
     'L0_ffn_re_w2': 8.0,
     'L1_ffn_wqkv': 8.0,
     'L1_ffn_wo': 8.0,
     'L1_ffn_gate_w': 8.0,
     'L1_ffn_w13': 8.0,
     'L1_ffn_w2': 8.0,
     'L2_xattn_b': 6.438,
     'L2_ffn_gate_w': 8.0,
     'L2_ffn_W1': 8.0,
     'L2_ffn_W3': 8.0,
     'L2_ffn_W2': 8.0,
     'L2_ffn_sw1': 8.0,
     'L2_ffn_sw3': 8.0,
     'L2_ffn_sw2': 8.0,
     'L3_ffn_w_gate': 8.0,
     'L3_ffn_w_up': 8.0,
     'L3_ffn_w_down': 8.0}
    for name, (base, spread) in spreads.items():
        noise = np.random.default_rng([zlib.crc32(name.encode()), seed]).standard_normal(out[name].shape)
        drawn = base * np.exp(spread * noise) if base else spread * noise
        out[name] = jnp.asarray(drawn.astype(out[name].dtype))
    for name, factor in factors.items():
        out[name] = (out[name] * factor).astype(out[name].dtype)
    return out
```

```python
from contextlib import ExitStack
import math

import concourse.bass as bass
from concourse import mybir
from concourse.alu_op_type import AluOpType as ALU

ACT = mybir.ActivationFunctionType
AX_X = mybir.AxisListType.X
F32 = mybir.dt.float32
BF16 = mybir.dt.bfloat16
I32 = mybir.dt.int32
U32 = mybir.dt.uint32
U8 = mybir.dt.uint8

P = 128
B = 16
BANK = 512
PAIRS = B // 2
HEADS = 4
EPS = 1e-5
NEG = -1e30
MAGIC = 1.5 * 2.0 ** 23
QMAX = 32767.0

LAYERS = [
    dict(name="l0x", units=2, heads=8, dim=64, scale=64 ** -0.5, front=4, back=4, turns=1),
    dict(name="l0f", units=4, heads=16, dim=64, scale=64 ** -0.5, front=11, back=7, turns=2),
    dict(name="l1x", units=4, heads=16, dim=8, scale=8 ** -0.5, front=4, back=3, turns=1),
    dict(name="l1f", units=4, heads=16, dim=8, scale=8 ** -0.5, front=4, back=3, turns=1),
    dict(name="l3x", units=1, heads=1, dim=128, scale=1.0, front=1, back=1, turns=0),
]


def schedule(L):
    units, wide = L["units"], L["dim"] == 64
    slots = units + 2 + 2
    parts, done = [("Y", 0)], 0

    def front(slot):
        nonlocal done
        upto = (L["front"] * (slot + 1) + slots - 1) // slots
        while done < min(upto, L["front"]):
            parts.append(("F", done))
            done += 1

    for t in range(units + 2):
        if t < units:
            parts.append(("S", t))
        if 1 <= t <= units:
            parts.append(("T", t - 1))
        if t < units:
            parts.append(("E", t))
        front(t)
        if t >= 2:
            parts.append(("V", t - 2))
    for n in range(L["turns"]):
        parts.append(("OT", n))
    front(units + 2)
    if L["turns"]:
        parts.append(("OP", 0))
    front(units + 3)
    assert done == L["front"]
    return parts


EXPERTS = [
    dict(name="l0m", steps=32, halves=1, gated=False, downs=[(0, P)], up=P, wcols=2 * P + 1),
    dict(name="l1m", steps=8, halves=2, gated=True, downs=[(0, P)], up=4 * P, wcols=6 * P),
    dict(name="l2m", steps=17, halves=1, gated=True, downs=[(0, 64), (64, P)], up=2 * P, wcols=3 * P),
]
CHUNKS = B * P // BANK
GCOLS = 34
CAPACITY = 2 * 512 * 4 // 32


def build(nc, a, out):
    ctx = ExitStack()
    with ctx:
        def sb(name, shape, dt=F32):
            return ctx.enter_context(nc.sbuf_tensor(name, shape, dt))

        def sem(name):
            return ctx.enter_context(nc.semaphore(name))

        def pair(name):
            return [sem(f"{name}{s}") for s in range(2)]

        def bank(name):
            return ctx.enter_context(nc.psum_tensor(name, [P, BANK], F32))

        s_bank = [bank(f"s_bank{s}") for s in range(2)]
        t_bank = [bank(f"t_bank{s}") for s in range(2)]
        v_bank = [bank(f"v_bank{s}") for s in range(2)]
        f_bank = [bank(f"f_bank{s}") for s in range(2)]

        X = sb("X", [P, B, P])
        AO = sb("AO", [P, B, P])
        Y = sb("Y", [P, B, P])
        YT = sb("YT", [P, B * P])
        CTX = sb("CTX", [P, B, P])
        big = sb("big", [P, 6 * 8 * P])
        work = sb("work", [P, 6 * 8 * P])
        qT = [work[:, 1024 * s:1024 * s + 1024] for s in range(2)]
        kT = [work[:, 1024 * s + 2048:1024 * s + 3072] for s in range(2)]
        o_tok = [work[:, 1024 * s + 4096:1024 * s + 5120] for s in range(2)]
        GT = work[0:32, 0:B * P]
        U3 = work[:, :].rearrange("p (m t) -> p m t", m=3)
        W0X = sb("W0X", [P, 4, 4 * P])
        W1X = sb("W1X", [P, 10 * P])
        W1F = sb("W1F", [P, 8 * P + 2 * P + 32 + P])
        WL2 = sb("WL2", [P, 2 * P])
        W3N = work[:, 1024:1024 + 9 * P]
        POSF = work[:, 0:3 * P].rearrange("p (m s) -> p m s", m=3)
        HOT = work[:, 3 * P:6 * P].rearrange("p (m s) -> p m s", m=3)
        W3T = sb("W3T", [P, 9 * P])
        W3M = sb("W3M", [P, 36])
        W3S = sb("W3S", [P, 36])
        W3R = sb("W3R", [P, 36])
        VEC = sb("VEC", [P, a["vec"].shape[1]])
        ROWS = sb("ROWS", [P, 3 * P])
        RB = sb("RB", [P, 31])
        LB = sb("LB", [P, 32])
        RW = sb("RW", [P, 31 + 8 + 32])
        RWB = sb("RWB", [P, 32], BF16)
        BROW = sb("BROW", [1, 4 * P])
        VB = sb("VB", [P, 8 * P])
        MASK = sb("MASK", [P, B, P], BF16)
        MASKU = sb("MASKU", [P, B * P], U8)
        NANF = sb("NANF", [P, B])
        POSI = sb("POSI", [P, P], I32)
        POSG = sb("POSG", [P, P], I32)
        PET = sb("PET", [P, 3 * P])
        CF = sb("CF", [P, a["cf"].shape[1]])
        CB = sb("CB", [P, a["cb"].shape[1]], BF16)
        ones_row = sb("ones_row", [1, P])
        half_neg = sb("half_neg", [P, B])
        B2 = sb("B2", [32, P])
        GATES = sb("GATES", [P, B, GCOLS])

        y_tok = [sb(f"y_tok{s}", [P, P]) for s in range(2)]
        y_aux = [sb(f"y_aux{s}", [P, P]) for s in range(2)]
        yT = [sb(f"yT{s}", [P, P]) for s in range(2)]
        cT = [sb(f"cT{s}", [P, P]) for s in range(2)]
        V64 = [sb(f"V64_{s}", [P, 16, 65]) for s in range(2)]
        V8 = [sb(f"V8_{s}", [P, 16, 9]) for s in range(2)]
        V128 = [sb(f"V128_{s}", [P, P + 1]) for s in range(2)]
        rope_a = [sb(f"rope_a{s}", [P, BANK]) for s in range(2)]
        rope_b = [sb(f"rope_b{s}", [P, BANK]) for s in range(2)]
        shifted = [sb(f"shifted{s}", [P, BANK]) for s in range(2)]
        h_all = sb("h_all", [P, 4 * BANK])
        hT = [h_all[:, BANK * s:BANK * s + BANK] for s in range(4)]
        probs, probsT = hT[0:2], hT[2:4]
        row_max = [sb(f"row_max{s}", [P, HEADS]) for s in range(2)]
        recips = [sb(f"recips{s}", [P, 16]) for s in range(2)]
        oT = sb("oT", [P, 8 * P])
        wset = [sb(f"wset{s}", [P, 6 * P]) for s in range(2)]
        wraw = [sb(f"wraw{s}", [P, 3 * P], BF16) for s in range(2)]
        act_sb = shifted
        st = sb("st", [P, B, 6])
        small = sb("small", [P, 12, B])
        cstat = sb("cstat", [P, 2, B])
        lg = sb("lg", [P, B, 32])
        ex = sb("ex", [P, B, 32])
        top8 = sb("top8", [P, B, 8])
        idx8 = sb("idx8", [P, B, 8], U32)
        idxf = sb("idxf", [P, B, 8])
        hits = h_all[:, :].rearrange("p (b k e) -> p b k e", b=B, k=4)
        sel = sb("sel", [P, B, 32])
        run = [rope_a[s][:, :].rearrange("p (b e) -> p b e", b=B) for s in range(2)]
        quant = sb("quant", [P, 5, 4])
        part_max = sb("part_max", [P, 24])
        sig = [CTX[:, 8 * s:8 * s + 8, :].rearrange("p b d -> p (b d)") for s in range(2)]
        csum = sb("csum", [P, B])
        tmpT = sb("tmpT", [P, 4, P])
        joined = [sb(f"joined{s}", [P, P]) for s in range(2)]

        mean, r1, r12, var, ve, t0, t1, ms = (small[:, n, :] for n in range(8))
        srow0, srow1, srow2, srow3 = (small[:, n, :] for n in range(8, 12))
        ident = CF[:, 0:P]
        before = CF[:, P:2 * P]
        iota_row = CF[:, 2 * P:3 * P]
        pe = CF[:, 3 * P:4 * P]
        cos1 = CF[:, 4 * P:5 * P]
        sin1 = CF[:, 5 * P:6 * P]
        part_no = CF[:, 6 * P:6 * P + 1]
        ones_at = CF[:, 6 * P + 1:6 * P + 2]
        sin_sign = CF[:, 6 * P + 2:6 * P + 3]
        magic = CF[:, 6 * P + 3:6 * P + 4]
        ones_sq = CF[:, 6 * P + 4:7 * P + 4]
        part_one = CF[:, 6 * P + 4:6 * P + 5]
        ident_bf = CB[:, 0:P]
        causal_bf = CB[:, P:P + BANK]
        own_bf = CB[:, P + BANK:P + BANK + 2 * P]
        names = ["l1x_g1", "l1x_b1", "l1x_g2", "l1x_b2", "l1f_ln1", "l1f_ln2", "theta", "gamma2"]
        vec = {n: VEC[:, j:j + 1] for j, n in enumerate(names)}
        qb_a = VEC[:, 8:16]
        qb_b = VEC[:, 16:24]
        kb_a = VEC[:, 24:32]
        kb_b = VEC[:, 32:40]
        gamma1_row = ROWS[:, 0:P]
        gamma2_row = ROWS[:, P:2 * P]
        bo = {"l0x": BROW[:, 0:P], "l0f": BROW[:, P:2 * P], "l1x": BROW[:, 2 * P:3 * P], "l2x": BROW[:, 3 * P:4 * P]}
        w0f = {n: big[:, 1024 * j:1024 * j + 1024] for j, n in enumerate(["qa", "qb", "ka", "kb", "v", "o"])}
        w1f = {"qa": W1F[:, 0:512], "qb": W1F[:, 512:1024], "ka": W1F[:, 1024:1152], "kb": W1F[:, 1152:1280],
               "v": W1F[:, 1280:1312], "o": W1F[:, 1312:1440]}
        w1x = {"q": W1X[:, 0:512], "k": W1X[:, 512:1024], "v": W1X[:, 1024:1152], "o": W1X[:, 1152:1280]}
        TAB = sb("TAB", [P, 2 * P + 16 * P])
        cos0, sin0 = TAB[:, 0:P], TAB[:, P:2 * P]
        tbq, tbk = TAB[:, 2 * P:10 * P], TAB[:, 10 * P:18 * P]
        G3 = big[:, :].rearrange("p (m t) -> p m t", m=3)

        in_x, in_ctx, in_c, in_w0x, in_w0f, in_w1, in_l3 = (sem(n) for n in (
            "in_x", "in_ctx", "in_c", "in_w0x", "in_w0f", "in_w1", "in_l3"))
        y_ready, aux_ready, cT_ready, v_dma = pair("y_ready"), pair("aux_ready"), pair("cT_ready"), pair("v_dma")
        f_full, f_drained = pair("f_full"), pair("f_drained")
        b_drained, turned, projected = pair("b_drained"), sem("turned"), sem("projected")
        s_full, shifted_ready, max_ready = pair("s_full"), pair("shifted_ready"), pair("max_ready")
        probs_ready, t_full, probsT_ready = pair("probs_ready"), pair("t_full"), pair("probsT_ready")
        pv_done, recip_ready = pair("pv_done"), pair("recip_ready")
        rope_sum, rope_done, k3_ready = pair("rope_sum"), pair("rope_done"), pair("k3_ready")
        grouped_ready, joined_ready = pair("grouped_ready"), pair("joined_ready")
        dve_chain, pool_chain = sem("dve_chain"), sem("pool_chain")
        w_loaded, w_cast = pair("w_loaded"), pair("w_cast")
        g_full, g_drained, u_full, h_ready = pair("g_full"), pair("g_drained"), pair("u_full"), pair("h_ready")
        d_full, d_drained = pair("d_full"), pair("d_drained")
        stored = sem("stored")
        step_sem = {}

        def step(name):
            if name not in step_sem:
                step_sem[name] = sem(name.replace(".", "_"))
            return step_sem[name]

        front_at, n = {}, 0
        for name, uses in [("setup", 4), ("l0x", 4 * B), ("l0f", 11 * B), ("l0m", 13), ("l1x", 4 * B), ("l1f", 4 * B),
                           ("l1m", 5), ("l2x", 9), ("l2m", 6), ("l3x", B), ("l3m", 32)]:
            front_at[name] = n
            n += uses
        unit_at, back_at, turn_at, proj_at = {}, {}, {}, {}
        nu = nb = nt = np_ = 0
        for j, L in enumerate(LAYERS):
            name = L["name"]
            L["no"] = j
            unit_at[name], back_at[name], turn_at[name], proj_at[name] = nu, nb, nt, np_
            nu, nb, nt = nu + L["units"] * B, nb + L["back"] * B, nt + L["turns"] * B
            np_ += B * (L["turns"] > 0)
        hid_at, sum_at, set_at = {}, {}, {}
        nh = nd = ns = 0
        for M in EXPERTS:
            hid_at[M["name"]], sum_at[M["name"]], set_at[M["name"]] = nh, nd, ns
            nh += M["steps"] * CHUNKS * M["halves"]
            nd += M["steps"] * CHUNKS * len(M["downs"])
            ns += M["steps"]
        ungated = hid_at["l1m"]
        ORDER = {L["name"]: schedule(L) for L in LAYERS}

        def place(at, per, i, s, c):
            c = at + per * s + c
            return c % 2, per * i + c // 2 + 1

        def front_use(name, c):
            c += front_at[name]
            return c % 2, c // 2 + 1

        def heads_of(L, u):
            if L["dim"] == 64:
                return [(8 * (u // 2) + u % 2 + 2 * m, 64 * (u % 2), 4 * (u // 2) + m, 4 * (u // 2) + m, 64,
                         8 * (u // 2) + u % 2 + 2 * m) for m in range(HEADS)]
            if L["name"] == "l1x":
                return [(4 * m + u, 32 * u, m, m, 32, 4 * m + u) for m in range(HEADS)]
            return [(4 * u + m, 32 * u, m, 0, 32, u) for m in range(HEADS)]

        recips_at, nr = {}, 0
        for L in LAYERS:
            recips_at[L["name"]] = nr
            nr += L["units"] * PAIRS if L["dim"] == 64 else PAIRS

        def batches(eng, part):
            part(0, 0, False, True, 0, 0)
            with eng.Fori(0, PAIRS - 1) as i:
                part(i, 0, True, True, i, 1)
                part(i, 1, True, True, i + 1, 0)
            part(PAIRS - 1, 0, True, True, PAIRS - 1, 1)
            part(PAIRS - 1, 1, True, False, 0, 0)

        def sets(eng, M, chunk):
            pairs, odd = M["steps"] // 2, M["steps"] % 2
            with eng.Fori(0, pairs - 1 + odd) as i:
                for s in range(2):
                    for c in range(CHUNKS):
                        chunk(i, s, c, False)
            for s in range(1 if odd else 2):
                for c in range(CHUNKS):
                    chunk(pairs - 1 + odd, s, c, s == (0 if odd else 1) and c == CHUNKS - 1)

        def after(i, s, c):
            return (i, s, c + 1) if c + 1 < CHUNKS else (i, 1, 0) if s == 0 else (i + 1, 0, 0)

        def last_sum(M, i, s):
            per = CHUNKS * len(M["downs"])
            return place(sum_at[M["name"]], per, i, s, per - 1)

        def col(ap, b):
            return ap[:, bass.ds(b, 1)]

        def tile(t, b):
            return t[:, bass.ds(b, 1), :].rearrange("p o d -> p (o d)")

        def wide(ap, n, m):
            return ap.unsqueeze(2).to_broadcast([P, n, m])

        def over(ap, n):
            return ap.unsqueeze(1).to_broadcast([P, n, ap.shape[1]])

        def split(ap, n):
            return ap.rearrange("p (n m) -> p n m", n=n)

        def rows_to_all(ap):
            return ap.partition_broadcast(P).rearrange("p o n -> p (o n)")

        block = ctx.enter_context(nc.Block())

        @block.sync
        def _(sp):
            def load(dst, src, s):
                sp.dma_start(dst, src).then_inc(s, 16)

            load(X[:, :, :], a["x"].rearrange("b s d -> s b d"), in_x)
            load(CF[:, :], a["cf"], in_c)
            load(CB[:, :], a["cb"], in_c)
            load(VEC[:, :], a["vec"], in_c)
            load(BROW[:, :], a["brow"], in_c)
            load(W0X[:, :, :], split(a["w0x"], 4), in_w0x)
            load(CTX[:, :, :], a["ctx"].rearrange("b s d -> s b d"), in_ctx)
            load(POSI[:, :], rows_to_all(a["pos"]), in_l3)
            load(MASKU[:, :], rows_to_all(a["mask"]), in_l3)
            load(W3N[:, :], a["w3"], in_l3)
            load(ROWS[:, 0:2 * P], rows_to_all(a["rows"]), in_l3)
            load(VB[:, :], rows_to_all(a["l0f_vb"]), in_l3)
            load(RB[:, :], rows_to_all(a["l0m_rb"]), in_l3)
            load(LB[:, :], rows_to_all(a["l2m_bias"]), in_l3)
            load(B2[:, :], a["b2"], in_l3)
            load(RW[:, 0:39], a["rw"], in_l3)
            load(RWB[:, :], a["rwb"], in_l3)

            def context0(i, s):
                sp.dma_start(cT[s][:, :], a["ctxT"][bass.ds(2 * i + s, 1), :, :].rearrange("o p n -> (o p) n")).then_inc(cT_ready[s], 16)

            for s in range(2):
                context0(0, s)
            load(big[:, :], a["w0f"], in_w0f)
            load(W1X[:, :], a["w1x"], in_w1)
            load(W1F[:, :], a["w1f"], in_w1)
            load(WL2[:, :], a["wl2"], in_w1)
            with sp.Fori(1, PAIRS) as i:
                for s in range(2):
                    for job in (2, 3):
                        r, k = place(front_at["l0x"], 4, i - 1, s, job)
                        sp.wait_ge(f_full[r], k + 1)
                    context0(i, s)

            def weights(M, dst, wait):
                def one(i, s):
                    wait(i, s)
                    sp.dma_start(dst[s][:, 0:M["wcols"]], a[M["name"]][bass.ds(2 * i + s, 1), :, :].rearrange("o p n -> (o p) n")).then_inc(w_loaded[s], 16)

                for s in range(2):
                    one(0, s)
                with sp.Fori(1, M["steps"] // 2) as i:
                    for s in range(2):
                        one(i, s)
                if M["steps"] % 2:
                    one(M["steps"] // 2, 0)

            def slot_free(M, prev):
                def wait(i, s):
                    if isinstance(i, int) and i == 0:
                        if prev is None:
                            return
                        r, k = last_sum(prev, prev["steps"] // 2 - 1, s)
                    else:
                        r, k = last_sum(M, i - 1, s)
                    sp.wait_ge(d_full[r], k + 1)
                return wait

            weights(EXPERTS[0], wset, slot_free(EXPERTS[0], None))
            weights(EXPERTS[1], wset, slot_free(EXPERTS[1], EXPERTS[0]))

            def raw_free(i, s):
                if isinstance(i, int) and i == 0:
                    sp.wait_ge(w_loaded[s], 16 * (set_at["l2m"] // 2))
                else:
                    sp.wait_ge(w_cast[s], i)

            weights(EXPERTS[2], wraw, raw_free)

            sp.wait_ge(step("l3x.begin"), 1)

            def context3(i, s):
                b = 2 * i + s
                if not (isinstance(i, int) and i == 0):
                    sp.wait_ge(k3_ready[s], 2 * i)
                sp.dma_start(cT[s][:, :], a["ctxT"][bass.ds(b, 1), :, :].rearrange("o p n -> (o p) n")).then_inc(cT_ready[s], 16)
                if not (isinstance(i, int) and i == 0):
                    r, k = place(unit_at["l3x"], 1, i - 1, s, 0)
                    sp.wait_ge(pv_done[r], k + 1)
                sp.dma_start(V128[s][:, 0:P], a["ctx"][bass.ds(b, 1), :, :].rearrange("o p n -> (o p) n")).then_inc(v_dma[s], 16)

            for s in range(2):
                context3(0, s)
            with sp.Fori(1, PAIRS) as i:
                for s in range(2):
                    context3(i, s)

            for g in range(4):
                r, k = front_use("l3m", 28 + g)
                sp.wait_ge(f_drained[r], k + 1)
                sp.dma_start(out[4 * g:4 * g + 4].rearrange("b s d -> s b d"), X[:, 4 * g:4 * g + 4, :]).then_inc(stored, 16)
            sp.wait_ge(stored, 4 * 16)

        @block.gpsimd
        def _(pool):
            links = [0]

            def link(ins):
                links[0] += 1
                ins.then_inc(pool_chain, 1)
                pool.wait_ge(pool_chain, links[0])

            for ring in (f_full, f_drained, b_drained, s_full, shifted_ready, max_ready, probs_ready, t_full, probsT_ready,
                         pv_done, rope_sum, rope_done, grouped_ready, joined_ready, g_full, g_drained, u_full, h_ready,
                         d_full, d_drained):
                for s in range(2):
                    pool.sem_inc(ring[s], 1)
            link(pool.memset(half_neg[:, :], -0.5))
            pool.memset(ones_row[:, :], 1.0)
            for s in range(2):
                pool.memset(V64[s][:, :, 64:65], 1.0)
                pool.memset(V8[s][:, :, 8:9], 1.0)
                pool.memset(V128[s][:, P:P + 1], 1.0)
            pool.memset(ex[:, :, :], -1.0)
            link(pool.memset(GATES[:, :, :], 0.0))
            pool.memset(GATES[:, :, 32:33], 1.0)
            pool.memset(GATES[:, :, 31:32], 1.0).then_inc(step("setup.ones"), 1)

            def power(name, src, dst):
                pool.wait_ge(step(name), 1)
                pool.tensor_tensor(dst, src, half_neg[:, :], ALU.pow).then_inc(step(name + "_pow"), 1)

            def attention(L):
                n = L["name"]

                def part(i, s, att, front, j, t):
                    for what, u in ORDER[n] if front else []:
                        if n == "l0f" and what == "Y":
                            pool.wait_ge(y_ready[t], PAIRS * L["no"] + j + 1)
                            pool.tensor_tensor(y_aux[t][:, :], y_tok[t][:, :], gamma1_row, ALU.mult).then_inc(aux_ready[t], 1)
                        if n == "l0f" and what == "F" and u in (2, 4, 6, 8):
                            piece = u // 2 - 1
                            half = slice(BANK * (piece % 2), BANK * (piece % 2) + BANK)
                            r, k = place(front_at[n], L["front"], j, t, u)
                            pool.wait_ge(f_drained[r], k + 1)
                            r, k = place(0, 4, j, t, piece)
                            pool.tensor_tensor(rope_a[r][:, :], rope_a[r][:, :], rope_b[r][:, :], ALU.add).then_inc(rope_sum[r], 1)
                            pool.wait_ge(rope_sum[r], k + 1)
                            pool.tensor_tensor((qT if piece < 2 else kT)[t][:, half], rope_a[r][:, :],
                                               (tbq if piece < 2 else tbk)[:, half], ALU.add).then_inc(rope_done[r], 1)
                        if n == "l1f" and what == "F" and u in (2, 3):
                            r, k = place(front_at[n], L["front"], j, t, u)
                            pool.wait_ge(f_drained[r], k + 1)
                            r, k = place(4 * B, 2, j, t, u - 2)
                            cols = BANK if u == 2 else P
                            pool.tensor_tensor((qT if u == 2 else kT)[t][:, 0:cols], rope_a[r][:, 0:cols],
                                               rope_b[r][:, 0:cols], ALU.add).then_inc(rope_done[r], 1)
                        if n == "l3x" and what == "F":
                            pool.wait_ge(cT_ready[t], 16 * (PAIRS + j + 1))
                            pool.wait_ge(y_ready[t], PAIRS * L["no"] + j + 1)
                            pool.tensor_tensor(kT[t][:, 0:P], cT[t][:, :], PET[:, 0:P], ALU.add).then_inc(k3_ready[t], 1)
                            pool.tensor_tensor(kT[t][:, P:2 * P], cT[t][:, :], PET[:, 2 * P:3 * P], ALU.add).then_inc(k3_ready[t], 1)
                batches(pool, part)

            def residual(name):
                pool.wait_ge(step(name + ".y"), 4)
                link(pool.tensor_tensor(X[:, :, :], X[:, :, :], AO[:, :, :], ALU.add))
                if name == "l0m":
                    pool.wait_ge(step("l0m.an"), 4)
                    link(pool.tensor_tensor(X[:, :, :], X[:, :, :], Y[:, :, :], ALU.add))
                pool.sem_inc(step(name + ".x_ready"), 1)

            power("ctx.stats", ve, r1)
            power("l0x.stats", ve, r1)
            pool.wait_ge(in_l3, 16 * 10)
            power("l0f.stats", ve, r1)
            power("l0f.stats2", t0, t1)
            pool.wait_ge(step("setup.tables"), 1)
            attention(LAYERS[1])
            power("l0m.stats", ve, r1)
            residual("l0m")
            power("l1x.stats", ve, r1)
            power("l1x.stats2", t0, t1)
            power("l1f.stats", ve, r1)
            power("l1f.stats2", t0, t1)
            attention(LAYERS[3])
            power("l1m.stats", ve, r1)
            residual("l1m")
            power("l2x.stats", ve, r1)
            power("l2m.stats", ve, r1)
            power("l3x.stats", ve, r1)
            attention(LAYERS[4])
            power("l3m.stats", ve, r1)
            largest = 0
            for n, count in enumerate([1, 2, 1, 1]):
                pool.wait_ge(step("l3m.part_max"), n + 1)
                for c in range(count):
                    pool.partition_all_reduce(quant[:, largest, 1:2], quant[:, largest, 0:1], P,
                                              bass.bass_isa.ReduceOp.max).then_inc(step("l3m.all_max"), 1)
                    largest += 1
                if n == 1:
                    for h in range(6):
                        pool.wait_ge(step("l3m.u_round"), h + 1)
                        u = U3[:, :, :].rearrange("p m t -> p (m t)")[:, 1024 * h:1024 * h + 1024]
                        pool.tensor_scalar(u, u, MAGIC, quant[:, 1, 2:3], ALU.subtract, ALU.mult).then_inc(step("l3m.u"), 1)

        @block.scalar
        def _(act):
            def attention(L):
                n, units = L["name"], L["units"]
                cols = BANK if units > 1 else P

                def part(i, s, att, front, j, t):
                    for what, u in ORDER[n]:
                        if what == "E" and att:
                            r, k = place(unit_at[n], units, i, s, u)
                            act.wait_ge(shifted_ready[r], k + 1)
                            act.wait_ge(t_full[r], k)
                            act.activation(probs[r][:, 0:cols], shifted[r][:, 0:cols], ACT.Exp, scale=L["scale"]).then_inc(probs_ready[r], 1)
                        if what == "T" and att:
                            r, k = place(unit_at[n], units, i, s, u)
                            act.wait_ge(t_full[r], k + 1)
                            act.wait_ge(pv_done[r], k)
                            act.activation(probsT[r][:, 0:cols], t_bank[r][:, 0:cols], ACT.Copy).then_inc(probsT_ready[r], 1)
                        if what == "OT" and att:
                            r, k = place(back_at[n], L["back"], i, s, (units if L["dim"] == 64 else 1) + u)
                            act.wait_ge(turned, turn_at[n] + L["turns"] * (2 * i + s) + u + 1)
                            c = BANK if L["dim"] == 64 else P
                            act.activation(oT[:, BANK * u:BANK * u + c], v_bank[r][:, 0:c], ACT.Copy).then_inc(b_drained[r], 1)
                        if what != "F" or not front:
                            continue
                        r, k = place(front_at[n], L["front"], j, t, u)
                        bk = f_bank[r]
                        if u == 0 and n != "l3x":
                            act.wait_ge(f_full[r], k + 1)
                            if n == "l1x":
                                act.activation(yT[t][:, :], bk[:, 0:P], ACT.Identity, scale=vec["l1x_g1"], bias=vec["l1x_b1"])
                                act.activation(cT[t][:, :], bk[:, P:2 * P], ACT.Identity, scale=vec["l1x_g2"],
                                               bias=vec["l1x_b2"]).then_inc(f_drained[r], 1)
                            elif n == "l1f":
                                act.activation(yT[t][:, :], bk[:, 0:P], ACT.Copy, scale=vec["l1f_ln1"]).then_inc(f_drained[r], 1)
                            else:
                                act.activation(yT[t][:, :], bk[:, 0:P], ACT.Copy).then_inc(f_drained[r], 1)
                        if n == "l0x" and u in (1, 2):
                            act.wait_ge(f_full[r], k + 1)
                            act.activation((qT if u == 1 else kT)[t][:, 0:BANK], bk[:, :], ACT.Copy).then_inc(f_drained[r], 1)
                        if n == "l1x" and u == 1:
                            act.wait_ge(f_full[r], k + 1)
                            act.activation(qT[t][:, 0:BANK], bk[:, :], ACT.Identity, bias=ones_at).then_inc(f_drained[r], 1)
                        if n == "l1x" and u == 3:
                            act.wait_ge(f_full[r], k + 1)
                            act.activation(V8[t][:, :, 0:8], split(bk[:, 0:P], 16), ACT.Copy).then_inc(f_drained[r], 1)
                batches(act, part)

            def turned_stream(n, **how):
                for g in range(4):
                    r, k = front_use(n, g)
                    act.wait_ge(f_full[r], k + 1)
                    act.activation(YT[:, BANK * g:BANK * g + BANK], f_bank[r][:, :], ACT.Copy, **how).then_inc(f_drained[r], 1)

            def experts(M):
                n, H = M["name"], M["halves"]

                def chunk(i, s, c, last):
                    for h in range(H):
                        r, k = place(hid_at[n], CHUNKS * H, i, s, c * H + h)
                        act.wait_ge(g_full[r], k + 1)
                        if M["gated"]:
                            act.wait_ge(h_ready[r], k)
                            act.activation(act_sb[r][:, :], s_bank[r][:, :], ACT.Silu).then_inc(g_drained[r], 1)
                        else:
                            act.activation(hT[(c * H + h) % 4][:, :], s_bank[r][:, :], ACT.Gelu,
                                           bias=wset[s][:, 2 * P:2 * P + 1]).then_inc(h_ready[r], 1)
                sets(act, M, chunk)

            act.wait_ge(step("setup.angles"), 1)
            act.activation(tmpT[:, 2:4, :], tmpT[:, 0:2, :], ACT.Sin).then_inc(step("setup.sin"), 1)
            for g, dst in enumerate([PET[:, 0:3 * P], W3T[:, 0:BANK], W3T[:, BANK:2 * BANK], W3T[:, 2 * BANK:9 * P]]):
                r, k = front_use("setup", g)
                act.wait_ge(f_full[r], k + 1)
                act.activation(dst, f_bank[r][:, 0:dst.shape[1]], ACT.Copy).then_inc(f_drained[r], 1)
            attention(LAYERS[0])
            attention(LAYERS[1])
            turned_stream("l0m", scale=vec["gamma2"])
            act.wait_ge(step("l0m.logits"), 1)
            act.activation(ex[:, :, 0:31], lg[:, :, 0:31], ACT.Exp).then_inc(step("l0m.exp"), 1)
            for g in range(4):
                r, k = front_use("l0m", 5 + g)
                act.wait_ge(f_full[r], k + 1)
                act.activation(GT[:, BANK * g:BANK * g + BANK], f_bank[r][0:32, :], ACT.Copy).then_inc(f_drained[r], 1)
            experts(EXPERTS[0])
            attention(LAYERS[2])
            attention(LAYERS[3])
            turned_stream("l1m", scale=vec["l1f_ln2"])
            act.wait_ge(step("l1m.logits"), 1)
            act.activation(ex[:, :, 0:8], lg[:, :, 0:8], ACT.Exp).then_inc(step("l1m.exp"), 1)
            experts(EXPERTS[1])
            turned_stream("l2x")
            r, k = front_use("l2x", 4)
            act.wait_ge(f_full[r], k + 1)
            act.activation(csum[:, :], f_bank[r][:, 0:B], ACT.Copy, scale=1.0 / P).then_inc(f_drained[r], 1)
            turned_stream("l2m")
            r, k = front_use("l2m", 4)
            act.wait_ge(f_full[r], k + 1)
            act.activation(ex[:, :, :], split(f_bank[r][:, :], B), ACT.Sigmoid).then_inc(f_drained[r], 1)
            experts(EXPERTS[2])
            attention(LAYERS[4])

            act.wait_ge(step("l3m.scale"), 1)
            for g in range(4):
                r, k = front_use("l3m", g)
                act.wait_ge(f_full[r], k + 1)
                act.activation(YT[:, BANK * g:BANK * g + BANK], f_bank[r][:, :], ACT.Identity, scale=quant[:, 0, 3:4],
                               bias=magic).then_inc(f_drained[r], 1)
            for e in range(24):
                r, k = front_use("l3m", 4 + e)
                c, w, m = e // 6, e % 6 // 3, e % 3
                act.wait_ge(f_full[r], k + 1)
                act.activation((U3, G3)[w][:, m, BANK * c:BANK * c + BANK], f_bank[r][:, :], ACT.Copy).then_inc(f_drained[r], 1)
            Uf = U3[:, :, :].rearrange("p m t -> p (m t)")
            act.wait_ge(step("l3m.scale"), 3)
            for h in range(6):
                part = big[:, 1024 * h:1024 * h + 1024]
                act.activation(part, part, ACT.Identity, scale=quant[:, 2, 3:4], bias=magic).then_inc(step("l3m.g_round"), 1)
            for h in range(6):
                part = Uf[:, 1024 * h:1024 * h + 1024]
                act.activation(part, part, ACT.Identity, scale=quant[:, 1, 3:4], bias=magic).then_inc(step("l3m.u_round"), 1)
            for h in range(6):
                act.wait_ge(step("l3m.g"), h + 1)
                if h >= 2:
                    act.wait_ge(step("l3m.gs"), h - 1)
                act.activation(sig[h % 2][:, :], big[:, 1024 * h:1024 * h + 1024], ACT.Sigmoid).then_inc(step("l3m.sig"), 1)
            for stage in (3, 4):
                act.wait_ge(step("l3m.scale"), stage + 1)
                for h in range(6):
                    part = big[:, 1024 * h:1024 * h + 1024]
                    act.activation(part, part, ACT.Identity, scale=quant[:, stage, 3:4], bias=magic).then_inc(step(f"l3m.round{stage}"), 1)

        @block.tensor
        def _(pe_):
            def front_begin(n, c):
                r, k = front_use(n, c)
                pe_.wait_ge(f_drained[r], k)
                return f_bank[r], f_full[r]

            def attention(L):
                n, units, F, U = L["name"], L["units"], L["front"], L["units"]
                causal = n in ("l0f", "l1f")

                def drained(i, s, job):
                    r, k = place(front_at[n], F, i, s, job)
                    pe_.wait_ge(f_drained[r], k + 1)

                def roped(i, s, piece):
                    at, per = (0, 4) if n == "l0f" else (4 * B, 2)
                    r, k = place(at, per, i, s, piece)
                    pe_.wait_ge(rope_done[r], k + 1)

                def front_job(j, t, u):
                    r, k = place(front_at[n], F, j, t, u)
                    pe_.wait_ge(f_drained[r], k)
                    bk = f_bank[r]

                    def product(cols, w, m, count, x):
                        for q in range(count):
                            last = pe_.matmul(bk[:, cols + P * q:cols + P * q + P], w[:, P * (m + q):P * (m + q) + P], x[:, :],
                                              start=True, stop=True)
                        return last

                    if u == 0:
                        if n == "l0f":
                            pe_.wait_ge(aux_ready[t], j + 1)
                            last = pe_.transpose(bk[:, 0:P], y_aux[t][:, :], ident)
                        else:
                            pe_.wait_ge(y_ready[t], PAIRS * L["no"] + j + 1)
                            last = pe_.transpose(bk[:, 0:P], y_tok[t][:, :], ident)
                            if n == "l1x":
                                last = pe_.transpose(bk[:, P:2 * P], y_aux[t][:, :], ident)
                    elif n == "l0x":
                        if u == 1:
                            drained(j, t, 0)
                            last = product(0, W0X[:, 0, :], 0, 4, yT[t])
                        if u == 2:
                            pe_.wait_ge(cT_ready[t], 16 * (j + 1))
                            last = product(0, W0X[:, 1, :], 0, 4, cT[t])
                        if u == 3:
                            last = pe_.matmul(bk[:, :], cT[t][:, :], W0X[:, 2, :], start=True, stop=True)
                    elif n == "l0f":
                        if u == 1:
                            drained(j, t, 0)
                        if u < 9:
                            piece = (u - 1) // 2
                            w = w0f[["qa", "qb", "ka", "kb"][2 * (piece // 2) + (u - 1) % 2]]
                            last = product(0, w, 4 * (piece % 2), 4, yT[t])
                        else:
                            last = pe_.matmul(bk[:, :], yT[t][:, :], w0f["v"][:, BANK * (u - 9):BANK * (u - 9) + BANK], start=True, stop=True)
                    elif n == "l1x":
                        if u == 1:
                            drained(j, t, 0)
                            last = product(0, w1x["q"], 0, 4, yT[t])
                        if u == 2:
                            last = product(0, w1x["k"], 0, 4, cT[t])
                        if u == 3:
                            last = pe_.matmul(bk[:, 0:P], cT[t][:, :], w1x["v"], start=True, stop=True)
                    elif n == "l1f":
                        if u == 1:
                            drained(j, t, 0)
                        if u < 3:
                            last = product(0, w1f[("qa", "qb")[u - 1]], 0, 4, yT[t])
                        else:
                            product(0, w1f["ka"], 0, 1, yT[t])
                            product(P, w1f["kb"], 0, 1, yT[t])
                            last = pe_.matmul(bk[:, 2 * P:2 * P + 32], yT[t][:, :], w1f["v"], start=True, stop=True)
                    last.then_inc(f_full[r], 1)

                def back_uses(i, s, uses):
                    for r0 in range(2):
                        mine = [c for c in uses if place(back_at[n], L["back"], i, s, c)[0] == r0]
                        if mine:
                            r, k = place(back_at[n], L["back"], i, s, max(mine))
                            pe_.wait_ge(b_drained[r], k + 1)

                def operands_ready(i, s, u):
                    if n in ("l0x", "l1x") and u == 0:
                        drained(i, s, 1)
                        drained(i, s, 2)
                    if n == "l0f" and u % 2 == 0:
                        roped(i, s, 2 + u // 2)
                    if n == "l1f" and u == 0:
                        roped(i, s, 0)
                        roped(i, s, 1)
                    if n == "l3x":
                        drained(i, s, 0)
                        pe_.wait_ge(k3_ready[s], 2 * i + 2)

                def part(i, s, att, front, j, t):
                    for what, u in ORDER[n]:
                        if what == "F" and front:
                            front_job(j, t, u)
                        if not att:
                            continue
                        if what in ("S", "T", "V"):
                            r, k = place(unit_at[n], units, i, s, u)
                        if what == "S":
                            pe_.wait_ge(shifted_ready[r], k)
                            operands_ready(i, s, u)
                            bk = s_bank[r]
                            if causal:
                                pe_.matmul(bk[:, :], ident_bf, causal_bf, start=True, stop=False, skip_group_check=True)
                            if n == "l3x":
                                pe_.matmul(bk[:, 0:2 * P], ident_bf, own_bf, start=True, stop=False, skip_group_check=True)
                                for m in range(2):
                                    last = pe_.matmul(bk[:, P * m:P * m + P], qT[s][:, P * m:P * m + P], kT[s][:, P * m:P * m + P],
                                                      start=False, stop=True, skip_group_check=True)
                            else:
                                for m, (_, row, tq, tk, rows, _) in enumerate(heads_of(L, u)):
                                    last = pe_.matmul(bk[:, P * m:P * m + P], qT[s][row:row + rows, P * tq:P * tq + P],
                                                      kT[s][row:row + rows, P * tk:P * tk + P],
                                                      start=not causal, stop=True, skip_group_check=causal)
                            last.then_inc(s_full[r], 1)
                        if what == "T":
                            pe_.wait_ge(probs_ready[r], k + 1)
                            pe_.wait_ge(probsT_ready[r], k)
                            for m in range(HEADS if units > 1 else 1):
                                last = pe_.transpose(t_bank[r][:, P * m:P * m + P], probs[r][:, P * m:P * m + P], ident)
                            last.then_inc(t_full[r], 1)
                        if what == "V":
                            pe_.wait_ge(probsT_ready[r], k + 1)
                            rb, kb = place(back_at[n], L["back"], i, s, u if L["dim"] == 64 else 0)
                            if L["dim"] == 64 or u == 0:
                                pe_.wait_ge(b_drained[rb], kb)
                            if n == "l0x" and u == 0:
                                drained(i, s, 3)
                            if n == "l0f" and u % 2 == 0:
                                drained(i, s, 9 + u // 2)
                            if n in ("l1x", "l1f") and u == 0:
                                drained(i, s, 3)
                            bk = v_bank[rb]
                            if n == "l3x":
                                pe_.wait_ge(v_dma[s], 16 * (i + 1))
                                last = pe_.matmul(bk[:, 0:P + 1], probsT[r][:, 0:P], V128[s][:, :], start=True, stop=True)
                            else:
                                for m, (h, _, _, _, _, hv) in enumerate(heads_of(L, u)):
                                    dst = bk[:, 65 * m:65 * m + 65] if L["dim"] == 64 else bk[:, 9 * h:9 * h + 9]
                                    last = pe_.matmul(dst, probsT[r][:, P * m:P * m + P], (V64 if L["dim"] == 64 else V8)[s][:, hv, :],
                                                      start=True, stop=True)
                            last.then_inc(pv_done[r], 1)
                        if what == "OT":
                            c = (units if L["dim"] == 64 else 1) + u
                            back_uses(i, s, ([2 * u, 2 * u + 1] if L["dim"] == 64 else [0]) + [c - 2])
                            rb, kb = place(back_at[n], L["back"], i, s, c)
                            for m in range(4 if L["dim"] == 64 else 1):
                                c = BANK * u + P * m
                                last = pe_.transpose(v_bank[rb][:, P * m:P * m + P], o_tok[s][:, c:c + P], ident)
                            last.then_inc(turned, 1)
                        if what == "OP":
                            first = units if L["dim"] == 64 else 1
                            c = first + L["turns"]
                            back_uses(i, s, list(range(first, c)) + [c - 2])
                            rb, kb = place(back_at[n], L["back"], i, s, c)
                            count = {"l0x": 4, "l0f": 8, "l1x": 1, "l1f": 1}[n]
                            w = {"l0x": W0X[:, 3, :], "l0f": w0f["o"], "l1x": w1x["o"], "l1f": w1f["o"]}[n]
                            for m in range(count):
                                last = pe_.matmul(v_bank[rb][:, 0:P], oT[:, P * m:P * m + P], w[:, P * m:P * m + P],
                                                  start=(m == 0), stop=(m == count - 1 and n == "l1f"))
                            if n != "l1f":
                                last = pe_.matmul(v_bank[rb][:, 0:P], ones_row[:, :], bo[n], start=False, stop=True)
                            last.then_inc(projected, 1)
                batches(pe_, part)

            def turn_stream(n, src=None):
                for g in range(4):
                    bk, full = front_begin(n, g)
                    pe_.wait_ge(step(n + ".y"), g + 1)
                    for m in range(4):
                        last = pe_.transpose(bk[:, P * m:P * m + P], Y[:, 4 * g + m, :], ident)
                    last.then_inc(full, 1)

            def stream_turned(n):
                for c in range(4):
                    r, k = front_use(n, c)
                    pe_.wait_ge(f_drained[r], k + 1)

            def router(n, w):
                stream_turned(n)
                bk, full = front_begin(n, 4)
                for b in range(B):
                    last = pe_.matmul(bk[:, 32 * b:32 * b + w.shape[1]], YT[:, P * b:P * b + P], w, start=True, stop=True)
                last.then_inc(full, 1)

            def experts(M):
                n, H, downs = M["name"], M["halves"], M["downs"]

                def hidden(i, s, c):
                    if c == 0:
                        if n == "l2m":
                            pe_.wait_ge(w_cast[s], i + 1)
                        else:
                            pe_.wait_ge(w_loaded[s], 16 * (set_at[n] // 2 + i + 1))
                    x = YT[:, BANK * c:BANK * c + BANK]
                    for h in range(H):
                        r, k = place(hid_at[n], CHUNKS * H, i, s, c * H + h)
                        if M["gated"]:
                            pe_.wait_ge(g_drained[r], k - ungated // 2)
                        pe_.wait_ge(h_ready[r], k)
                        pe_.matmul(s_bank[r][:, :], wset[s][:, P * h:P * h + P], x, start=True, stop=True).then_inc(g_full[r], 1)
                        if M["gated"]:
                            up = (M["up"] // 2) + P * h
                            pe_.matmul(t_bank[r][:, :], wset[s][:, up:up + P], x, start=True, stop=True).then_inc(u_full[r], 1)

                def sums(i, s, c):
                    for h in range(H):
                        r, k = place(hid_at[n], CHUNKS * H, i, s, c * H + h)
                        pe_.wait_ge(h_ready[r], k + 1)
                    for d, (lo, hi) in enumerate(downs):
                        r, k = place(sum_at[n], CHUNKS * len(downs), i, s, c * len(downs) + d)
                        pe_.wait_ge(d_drained[r], k)
                        for q in range(4):
                            for h in range(H):
                                last = pe_.matmul(v_bank[r][:, P * q:P * q + P], hT[(c * H + h) % 4][lo:hi, P * q:P * q + P],
                                                  wset[s][lo:hi, (M["up"] + P * h):(M["up"] + P * h) + P],
                                                  start=(h == 0), stop=(h == H - 1))
                        last.then_inc(d_full[r], 1)

                def chunk(i, s, c, last):
                    if not last:
                        hidden(*after(i, s, c))
                    sums(i, s, c)

                hidden(0, 0, 0)
                sets(pe_, M, chunk)

            pe_.wait_ge(in_c, 16 * 4)
            pe_.wait_ge(step("setup.hot"), 1)
            bk, full = front_begin("setup", 0)
            pe_.matmul(bk[:, 0:3 * P], pe, HOT[:, :, :].rearrange("p m s -> p (m s)"), start=True, stop=True).then_inc(full, 1)
            pe_.wait_ge(step("setup.w3"), 1)
            for g in range(3):
                bk, full = front_begin("setup", 1 + g)
                for m in range(4 * g, min(4 * g + 4, 9)):
                    last = pe_.transpose(bk[:, P * (m - 4 * g):P * (m - 4 * g) + P], W3N[:, P * m:P * m + P], ident)
                last.then_inc(full, 1)
            pe_.wait_ge(in_w0x, 16)
            pe_.wait_ge(step("setup.ones"), 1)
            attention(LAYERS[0])
            pe_.wait_ge(in_w0f, 16)
            attention(LAYERS[1])
            turn_stream("l0m")
            pe_.wait_ge(in_l3, 16 * 10)
            router("l0m", RW[:, 0:31])
            pe_.wait_ge(step("l0m.gates"), 1)
            for g in range(4):
                bk, full = front_begin("l0m", 5 + g)
                for m in range(4):
                    last = pe_.transpose(bk[0:32, P * m:P * m + P], GATES[:, 4 * g + m, 0:32], ident)
                last.then_inc(full, 1)
            for g in range(4):
                r, k = front_use("l0m", 5 + g)
                pe_.wait_ge(f_drained[r], k + 1)
            for g in range(4):
                bk, full = front_begin("l0m", 9 + g)
                for m in range(4):
                    b = 4 * g + m
                    last = pe_.matmul(bk[:, P * m:P * m + P], GT[:, P * b:P * b + P], B2[:, :], start=True, stop=True)
                last.then_inc(full, 1)
            experts(EXPERTS[0])
            pe_.wait_ge(in_w1, 16 * 3)
            attention(LAYERS[2])
            attention(LAYERS[3])
            turn_stream("l1m")
            router("l1m", RW[:, 31:39])
            experts(EXPERTS[1])

            turn_stream("l2x")
            bk, full = front_begin("l2x", 4)
            for b in range(B):
                last = pe_.matmul(bk[:, b:b + 1], CTX[:, b, :], part_one, start=True, stop=True)
            last.then_inc(full, 1)
            stream_turned("l2x")
            r, k = front_use("l2x", 4)
            pe_.wait_ge(f_drained[r], k + 1)
            for g in range(4):
                bk, full = front_begin("l2x", 5 + g)
                for m in range(4):
                    b = 4 * g + m
                    dst = bk[:, P * m:P * m + P]
                    pe_.matmul(dst, YT[:, P * b:P * b + P], WL2[:, 0:P], start=True, stop=False)
                    pe_.matmul(dst, csum[:, b:b + 1].to_broadcast([P, P]), WL2[:, P:2 * P], start=False, stop=False)
                    last = pe_.matmul(dst, ones_row[:, :], bo["l2x"], start=False, stop=True)
                last.then_inc(full, 1)

            turn_stream("l2m")
            router("l2m", RW[:, 39:71])
            pe_.wait_ge(step("l2m.run"), 1)
            bk, full = front_begin("l2m", 5)
            pe_.matmul(bk[:, :], before, sel[:, :, :].rearrange("p b e -> p (b e)"), start=True, stop=False)
            pe_.matmul(bk[:, :], ones_sq, run[0][:, :, :].rearrange("p b e -> p (b e)"), start=False, stop=True).then_inc(full, 1)
            experts(EXPERTS[2])
            attention(LAYERS[4])

            turn_stream("l3m")
            for c in range(4):
                pe_.wait_ge(step("l3m.yq"), c + 1)
                for e in range(6):
                    w, m = e // 3, e % 3
                    bk, full = front_begin("l3m", 4 + 6 * c + e)
                    wt = W3T[:, P * (3 * (1 - w) + m):P * (3 * (1 - w) + m) + P]
                    pe_.matmul(bk[:, :], wt, YT[:, BANK * c:BANK * c + BANK], start=True, stop=True).then_inc(full, 1)
            pe_.wait_ge(step("l3m.o"), 6)
            for g in range(4):
                bk, full = front_begin("l3m", 28 + g)
                for q in range(4):
                    b = 4 * g + q
                    for m in range(3):
                        last = pe_.matmul(bk[:, P * q:P * q + P], G3[:, m, P * b:P * b + P], W3T[:, P * (6 + m):P * (6 + m) + P],
                                          start=(m == 0), stop=(m == 2))
                last.then_inc(full, 1)

        @block.vector
        def _(dve):
            links = [0]

            def link(ins):
                links[0] += 1
                ins.then_inc(dve_chain, 1)
                dve.wait_ge(dve_chain, links[0])

            def moments(src):
                for b in range(B):
                    last = dve.bn_stats(st[:, b, :], src[:, b, :])
                link(last)
                dve.tensor_tensor(t0, st[:, :, 1], st[:, :, 4], ALU.add)
                dve.tensor_tensor(t1, st[:, :, 1], st[:, :, 4], ALU.subtract)
                link(dve.tensor_tensor(ms, st[:, :, 2], st[:, :, 5], ALU.add))
                dve.tensor_scalar(mean, t0, 0.5, None, ALU.mult)
                link(dve.tensor_tensor(srow2, t1, t1, ALU.mult))
                link(dve.scalar_tensor_tensor(var, srow2, 32.0, ms, ALU.mult, ALU.add))

            def powered(name):
                dve.wait_ge(step(name + "_pow"), 1)

            def layer_norm_stats(name, src):
                moments(src)
                dve.tensor_scalar(ve, var, 1.0 / P, EPS, ALU.mult, ALU.add).then_inc(step(name), 1)
                powered(name)

            def again_stats(name):
                link(dve.tensor_tensor(t0, r1, r1, ALU.mult))
                link(dve.tensor_tensor(t0, t0, var, ALU.mult))
                link(dve.tensor_scalar(t0, t0, 1.0 / P, EPS, ALU.mult, ALU.add))
                dve.sem_inc(step(name), 1)
                powered(name)
                link(dve.tensor_tensor(r12, r1, t1, ALU.mult))

            def rms_stats(name, src):
                moments(src)
                link(dve.tensor_tensor(t0, mean, mean, ALU.mult))
                link(dve.scalar_tensor_tensor(t0, var, 1.0 / P, t0, ALU.mult, ALU.add))
                dve.tensor_scalar(ve, t0, EPS, None, ALU.add).then_inc(step(name), 1)
                powered(name)

            def normalise(n, src, centred):
                for g in range(4):
                    for b in range(4 * g, 4 * g + 4):
                        if centred:
                            last = dve.tensor_scalar(Y[:, b, :], src[:, b, :], mean[:, b:b + 1], r1[:, b:b + 1], ALU.subtract, ALU.mult)
                        else:
                            last = dve.tensor_scalar(Y[:, b, :], src[:, b, :], r1[:, b:b + 1], None, ALU.mult)
                    last.then_inc(step(n + ".y"), 1)

            def batches_done(L):
                for c in range(2):
                    r, k = place(back_at[L["name"]], L["back"], PAIRS - 1, c, L["back"] - 1)
                    dve.wait_ge(b_drained[r], k + 1)
                for c in range(L["back"] * 2):
                    r, k = place(back_at[L["name"]], L["back"], PAIRS - 1, 0, c)
                    dve.wait_ge(b_drained[r], k + 1)

            def sets_done(M):
                for d in range(2):
                    total = sum_at[M["name"]] + M["steps"] * CHUNKS * len(M["downs"]) - 1 - d
                    dve.wait_ge(d_drained[total % 2], total // 2 + 2)

            def attention(L):
                n, units = L["name"], L["units"]

                def part(i, s, att, front, j, t):
                    b, nxt = 2 * i + s, 2 * j + t
                    for what, u in ORDER[n]:
                        if what == "Y" and front:
                            last = dve.tensor_scalar(y_tok[t][:, :], tile(X, nxt), col(mean, nxt),
                                                     col(r12 if n in ("l0f", "l1x", "l1f") else r1, nxt), ALU.subtract, ALU.mult)
                            if n == "l1x":
                                last = dve.tensor_scalar(y_aux[t][:, :], tile(CTX, nxt), col(cstat[:, 0, :], nxt),
                                                         col(cstat[:, 1, :], nxt), ALU.subtract, ALU.mult)
                            if n == "l1f":
                                if att:
                                    rb, kb = place(back_at[n], L["back"], i, s, -1)
                                    dve.wait_ge(b_drained[rb], kb + 1)
                                last = dve.tensor_scalar(y_aux[t][:, :], tile(X, nxt), col(mean, nxt), col(r1, nxt),
                                                         ALU.subtract, ALU.mult)
                            last.then_inc(y_ready[t], 1)
                        if what == "F" and front:
                            front_job(j, t, u, nxt)
                        if not att:
                            continue
                        if what in ("S", "V"):
                            r, k = place(unit_at[n], units, i, s, u)
                        if what == "S":
                            src = split(s_bank[r][:, :], HEADS)
                            heads = HEADS
                            dve.wait_ge(s_full[r], k + 1)
                            if n == "l3x":
                                k3 = place(0, 1, i, s, 0)[1]
                                heads = 1
                                dve.tensor_copy(joined[r][:, :], s_bank[r][:, P:2 * P]).then_inc(grouped_ready[r], 1)
                                dve.wait_ge(grouped_ready[r], k3 + 1)
                                dve.tensor_tensor(joined[r][:, :], s_bank[r][:, 0:P], joined[r][:, :], ALU.max).then_inc(joined_ready[r], 1)
                                dve.wait_ge(joined_ready[r], k3 + 1)
                                src = split(joined[r][:, :], 1)
                            dve.tensor_reduce(row_max[r][:, 0:heads], src, AX_X, ALU.max).then_inc(max_ready[r], 1)
                            dve.wait_ge(max_ready[r], k + 1)
                            dve.wait_ge(probs_ready[r], k)
                            dve.tensor_tensor(split(shifted[r][:, 0:P * heads], heads), src, wide(row_max[r][:, 0:heads], heads, P),
                                              ALU.subtract).then_inc(shifted_ready[r], 1)
                        if what == "V":
                            if L["dim"] == 8 and u < units - 1:
                                continue
                            dve.wait_ge(pv_done[r], k + 1)
                            rb, kb = place(back_at[n], L["back"], i, s, u if L["dim"] == 64 else 0)
                            kr = recips_at[n] + (units * i + (units * s + u) // 2 if L["dim"] == 64 else i)
                            rr = r if L["dim"] == 64 else s
                            bk = v_bank[rb]
                            if L["dim"] == 64:
                                o = split(bk[:, 0:260], HEADS)
                                dve.reciprocal(recips[rr][:, 0:HEADS], o[:, :, 64]).then_inc(recip_ready[rr], 1)
                                dve.wait_ge(recip_ready[rr], kr + 1)
                                h0 = 8 * (u // 2) + u % 2
                                dst = o_tok[s][:, :].rearrange("p (h d) -> p h d", d=64)[:, h0:h0 + 7:2, :]
                                dve.tensor_tensor(dst, o[:, :, 0:64], wide(recips[rr][:, 0:HEADS], HEADS, 64), ALU.mult).then_inc(b_drained[rb], 1)
                            elif L["dim"] == 8:
                                o = split(bk[:, 0:144], 16)
                                dve.reciprocal(recips[rr][:, :], o[:, :, 8]).then_inc(recip_ready[rr], 1)
                                dve.wait_ge(recip_ready[rr], kr + 1)
                                dst = split(o_tok[s][:, 0:P], 16)
                                if n == "l1x":
                                    dve.scalar_tensor_tensor(dst, o[:, :, 0:8], col(NANF, b), wide(recips[rr][:, :], 16, 8),
                                                             ALU.mult, ALU.mult).then_inc(b_drained[rb], 1)
                                else:
                                    dve.tensor_tensor(dst, o[:, :, 0:8], wide(recips[rr][:, :], 16, 8), ALU.mult).then_inc(b_drained[rb], 1)
                            else:
                                dve.reciprocal(recips[rr][:, 0:1], bk[:, P:P + 1]).then_inc(recip_ready[rr], 1)
                                dve.wait_ge(recip_ready[rr], kr + 1)
                                dve.scalar_tensor_tensor(tile(X, b), bk[:, 0:P], recips[rr][:, 0:1], tile(X, b), ALU.mult, ALU.add)\
                                    .then_inc(b_drained[rb], 1)
                        if what == "OP":
                            rb, kb = place(back_at[n], L["back"], i, s, L["back"] - 1)
                            dve.wait_ge(projected, proj_at[n] + b + 1)
                            if n in ("l0x", "l1x"):
                                dve.tensor_tensor(tile(X, b), v_bank[rb][:, 0:P], tile(X, b), ALU.add).then_inc(b_drained[rb], 1)
                            else:
                                dve.tensor_tensor(tile(AO, b), v_bank[rb][:, 0:P], y_aux[s][:, :], ALU.add).then_inc(b_drained[rb], 1)

                def front_job(j, t, u, nxt):
                    r, k = place(front_at[n], L["front"], j, t, u)
                    bk = f_bank[r]
                    four = split(bk[:, :], 4)
                    if n == "l0x" and u == 3:
                        dve.wait_ge(f_full[r], k + 1)
                        dve.tensor_copy(V64[t][:, 0:8, 0:64], split(bk[:, :], 8)).then_inc(f_drained[r], 1)
                    if n == "l0f" and 1 <= u <= 8 or n == "l1f" and u in (1, 2):
                        piece = (u - 1) // 2
                        at, per = (0, 4) if n == "l0f" else (4 * B, 2)
                        q, kq = place(at, per, j, t, piece)
                        dve.wait_ge(f_full[r], k + 1)
                        dve.wait_ge(rope_done[q], kq)
                        odd = (u - 1) % 2
                        table = (sin0 if odd else cos0) if n == "l0f" else (sin1 if odd else cos1)
                        dve.tensor_tensor(split((rope_b if odd else rope_a)[q][:, :], 4), four, over(table, 4), ALU.mult).then_inc(f_drained[r], 1)
                    if n == "l0f" and u >= 9:
                        h0 = 8 * (u - 9)
                        dve.wait_ge(f_full[r], k + 1)
                        dve.tensor_tensor(V64[t][:, h0:h0 + 8, 0:64], split(bk[:, :], 8), split(VB[:, BANK * (u - 9):BANK * (u - 9) + BANK], 8),
                                          ALU.add).then_inc(f_drained[r], 1)
                    if n == "l1x" and u == 2:
                        dve.wait_ge(f_full[r], k + 1)
                        dve.scalar_tensor_tensor(split(kT[t][:, 0:BANK], 4), tile(MASK, nxt).unsqueeze(1).to_broadcast([P, 4, P]), ones_at,
                                                 four, ALU.mult, ALU.add).then_inc(f_drained[r], 1)
                    if n == "l1f" and u == 3:
                        q, kq = place(4 * B, 2, j, t, 1)
                        dve.wait_ge(f_full[r], k + 1)
                        dve.wait_ge(rope_done[q], kq)
                        dve.tensor_tensor(rope_a[q][:, 0:P], bk[:, 0:P], cos1, ALU.mult)
                        dve.tensor_tensor(rope_b[q][:, 0:P], bk[:, P:2 * P], sin1, ALU.mult)
                        dve.tensor_copy(V8[t][:, 0:4, 0:8], split(bk[:, 2 * P:2 * P + 32], 4)).then_inc(f_drained[r], 1)
                    if n == "l3x":
                        dve.wait_ge(f_full[r], k + 1)
                        dve.tensor_tensor(qT[t][:, 0:P], bk[:, 0:P], PET[:, 0:P], ALU.add)
                        dve.tensor_tensor(qT[t][:, P:2 * P], bk[:, 0:P], PET[:, P:2 * P], ALU.add).then_inc(f_drained[r], 1)
                batches(dve, part)

            def top(n, k, E):
                for b in range(B):
                    last = dve.max(top8[:, b, :], ex[:, b, 0:E])
                link(last)
                for b in range(B):
                    last = dve.max_index(idx8[:, b, :], top8[:, b, :], ex[:, b, 0:E])
                link(last)
                link(dve.tensor_copy(idxf[:, :, :], idx8[:, :, :]))
                iota = iota_row[:, 0:E].unsqueeze(1).unsqueeze(1).to_broadcast([P, B, k, E])
                link(dve.tensor_tensor(hits[:, :, 0:k, 0:E], iota, idxf[:, :, 0:k].unsqueeze(3).to_broadcast([P, B, k, E]), ALU.is_equal))
                link(dve.tensor_reduce(sel[:, :, 0:E], hits[:, :, 0:k, 0:E].rearrange("p b k e -> p b e k"), AX_X, ALU.add))

            def row_scale(dst, src, by, E):
                return dve.tensor_tensor(dst, src, wide(by, B, E), ALU.mult)

            def softmax_gates(n, E, k, bias, exact):
                r, kk = front_use(n, 4)
                dve.wait_ge(f_full[r], kk + 1)
                logits = split(f_bank[r][:, :], B)[:, :, 0:E]
                if bias is not None:
                    link(dve.tensor_tensor(lg[:, :, 0:E], logits, over(bias, B), ALU.add))
                else:
                    link(dve.tensor_copy(lg[:, :, 0:E], logits))
                dve.sem_inc(f_drained[r], 1)
                link(dve.tensor_reduce(srow0, lg[:, :, 0:E], AX_X, ALU.max))
                dve.tensor_tensor(lg[:, :, 0:E], lg[:, :, 0:E], wide(srow0, B, E), ALU.subtract).then_inc(step(n + ".logits"), 1)
                dve.wait_ge(step(n + ".exp"), 1)
                link(dve.tensor_reduce(srow0, ex[:, :, 0:E], AX_X, ALU.add))
                link(dve.reciprocal(srow1, srow0))
                link(row_scale(ex[:, :, 0:E], ex[:, :, 0:E], srow1, E))
                top(n, k, max(E, 8) + (E == 31))
                if exact:
                    link(dve.tensor_tensor(lg[:, :, 0:E], ex[:, :, 0:E], sel[:, :, 0:E], ALU.mult))
                    link(dve.tensor_reduce(srow0, lg[:, :, 0:E], AX_X, ALU.add))
                    link(dve.reciprocal(srow1, srow0))
                    link(row_scale(GATES[:, :, 0:E], lg[:, :, 0:E], srow1, E))
                else:
                    link(dve.tensor_tensor(GATES[:, :, 0:E], ex[:, :, 0:E], sel[:, :, 0:E], ALU.mult))
                dve.sem_inc(step(n + ".gates"), 1)

            def experts(M):
                n, H, downs = M["name"], M["halves"], M["downs"]
                nD = len(downs)

                def hidden(i, s, c):
                    if not M["gated"]:
                        return
                    for h in range(H):
                        r, k = place(hid_at[n], CHUNKS * H, i, s, c * H + h)
                        dve.wait_ge(g_drained[r], k - ungated // 2 + 1)
                        dve.wait_ge(u_full[r], k - ungated // 2 + 1)
                        dve.tensor_tensor(hT[(c * H + h) % 4][:, :], t_bank[r][:, :], act_sb[r][:, :], ALU.mult).then_inc(h_ready[r], 1)

                def chunk(i, s, c, last):
                    if not last:
                        hidden(*after(i, s, c))
                    for d in range(nD):
                        r, k = place(sum_at[n], CHUNKS * nD, i, s, c * nD + d)
                        dve.wait_ge(d_full[r], k + 1)
                        if d:
                            r0, k0 = place(sum_at[n], CHUNKS * nD, i, s, c * nD + d - 1)
                            dve.wait_ge(d_drained[r0], k0 + 1)
                        gate = nD * (2 * i + s) + d
                        for q in range(4):
                            tok = 4 * c + q
                            ins = dve.scalar_tensor_tensor(X[:, tok, :], v_bank[r][:, P * q:P * q + P], GATES[:, tok, bass.ds(gate, 1)],
                                                           X[:, tok, :], ALU.mult, ALU.add)
                        ins.then_inc(d_drained[r], 1)
                    if n == "l2m" and c == 0 and not last_set(i, s):
                        cast(i + s, 1 - s)

                def last_set(i, s):
                    return isinstance(i, int) and 2 * i + s == M["steps"] - 1

                def cast(i, s):
                    dve.wait_ge(w_loaded[s], 16 * (set_at[n] // 2 + i + 1))
                    dve.tensor_copy(wset[s][:, 0:M["wcols"]], wraw[s][:, 0:M["wcols"]]).then_inc(w_cast[s], 1)

                if n == "l2m":
                    cast(0, 0)
                hidden(0, 0, 0)
                sets(dve, M, chunk)

            dve.wait_ge(in_ctx, 16)
            layer_norm_stats("ctx.stats", CTX)
            dve.tensor_copy(cstat[:, 0, :], mean)
            link(dve.tensor_copy(cstat[:, 1, :], r1))
            dve.wait_ge(in_c, 16 * 4)
            dve.wait_ge(in_l3, 16 * 10)
            link(dve.tensor_scalar(POSG[:, :], POSI[:, :], 4, None, ALU.arith_shift_right))
            dve.tensor_copy(POSF[:, 0, :], POSI[:, :])
            link(dve.tensor_copy(POSF[:, 2, :], POSG[:, :]))
            link(dve.tensor_scalar(POSF[:, 1, :], POSF[:, 2, :], 60.0, None, ALU.add))
            link(dve.tensor_scalar(POSF[:, :, :], POSF[:, :, :], 0.0, P - 1.0, ALU.max, ALU.min))
            dve.tensor_scalar(HOT[:, :, :], POSF[:, :, :], part_no, None, ALU.is_equal).then_inc(step("setup.hot"), 1)
            w3 = W3N[:, :].rearrange("p (n m) -> p n m", m=32)
            link(dve.tensor_reduce(W3M[:, :], w3, AX_X, ALU.max, apply_absolute_value=True))
            link(dve.tensor_scalar(W3S[:, :], W3M[:, :], 1.0 / 7.0, 1e-12, ALU.mult, ALU.max))
            link(dve.reciprocal(W3R[:, :], W3S[:, :]))
            link(dve.tensor_tensor(w3, w3, wide(W3R[:, :], 36, 32), ALU.mult))
            link(dve.tensor_scalar(W3N[:, :], W3N[:, :], MAGIC, None, ALU.add))
            link(dve.tensor_scalar(W3N[:, :], W3N[:, :], MAGIC, 7.0, ALU.subtract, ALU.min))
            link(dve.tensor_scalar(W3N[:, :], W3N[:, :], -8.0, None, ALU.max))
            dve.tensor_tensor(w3, w3, wide(W3S[:, :], 36, 32), ALU.mult).then_inc(step("setup.w3"), 1)
            maskf = MASK[:, :, :].rearrange("p b s -> p (b s)")
            link(dve.tensor_copy(maskf, MASKU[:, :]))
            link(dve.tensor_reduce(NANF[:, :], MASK[:, :, :], AX_X, ALU.max))
            link(dve.reciprocal(srow0, NANF[:, :]))
            link(dve.tensor_tensor(NANF[:, :], NANF[:, :], srow0, ALU.mult))
            link(dve.tensor_scalar(maskf, maskf, -1.0, -NEG, ALU.add, ALU.mult))
            dve.tensor_copy(RW[:, 39:71], RWB[:, :])
            turns = [6.28125, 1.9340515136718750e-3, 1.2556659146e-6]
            link(dve.tensor_scalar(tmpT[:, 2, :], iota_row, vec["theta"], None, ALU.mult))
            for c, quarter in ((0, 0.0), (1, 0.25)):
                link(dve.tensor_scalar(tmpT[:, 3, :], tmpT[:, 2, :], 1.0 / (2.0 * math.pi), quarter, ALU.mult, ALU.add))
                link(dve.tensor_scalar(tmpT[:, 3, :], tmpT[:, 3, :], MAGIC, MAGIC, ALU.add, ALU.subtract))
                link(dve.scalar_tensor_tensor(tmpT[:, c, :], tmpT[:, 3, :], -turns[0], tmpT[:, 2, :], ALU.mult, ALU.add))
                link(dve.scalar_tensor_tensor(tmpT[:, c, :], tmpT[:, 3, :], -turns[1], tmpT[:, c, :], ALU.mult, ALU.add))
                link(dve.scalar_tensor_tensor(tmpT[:, c, :], tmpT[:, 3, :], -turns[2], tmpT[:, c, :], ALU.mult, ALU.add))
            link(dve.tensor_scalar(tmpT[:, 1, :], tmpT[:, 1, :], math.pi / 2, None, ALU.add))
            dve.tensor_scalar(tmpT[:, 0:2, :], tmpT[:, 0:2, :], 3.1415925, -3.1415925, ALU.min, ALU.max).then_inc(step("setup.angles"), 1)
            dve.wait_ge(step("setup.sin"), 1)
            link(dve.tensor_scalar(sin0, tmpT[:, 2, :], sin_sign, None, ALU.mult))
            link(dve.tensor_copy(cos0, tmpT[:, 3, :]))
            for dst, ba, bb in ((tbq, qb_a, qb_b), (tbk, kb_a, kb_b)):
                for m in range(8):
                    last = dve.tensor_scalar(dst[:, P * m:P * m + P], cos0, ba[:, m:m + 1], None, ALU.mult)
                link(last)
                for m in range(8):
                    last = dve.scalar_tensor_tensor(dst[:, P * m:P * m + P], sin0, bb[:, m:m + 1], dst[:, P * m:P * m + P], ALU.mult, ALU.add)
                link(last)
            dve.sem_inc(step("setup.tables"), 1)

            dve.wait_ge(in_x, 16)
            layer_norm_stats("l0x.stats", X)
            attention(LAYERS[0])
            batches_done(LAYERS[0])
            layer_norm_stats("l0f.stats", X)
            again_stats("l0f.stats2")
            attention(LAYERS[1])
            batches_done(LAYERS[1])

            rms_stats("l0m.stats", AO)
            normalise("l0m", AO, False)
            for g in range(4):
                r, k = front_use("l0m", g)
                dve.wait_ge(f_full[r], k + 1)
                dve.tensor_tensor(Y[:, 4 * g:4 * g + 4, :], Y[:, 4 * g:4 * g + 4, :], over(gamma2_row, 4), ALU.mult).then_inc(step("l0m.an"), 1)
            softmax_gates("l0m", 31, 3, RB[:, :], False)
            dve.wait_ge(step("l0m.x_ready"), 1)
            for g in range(4):
                r, k = front_use("l0m", 9 + g)
                dve.wait_ge(f_full[r], k + 1)
                last = dve.tensor_tensor(X[:, 4 * g:4 * g + 4, :], split(f_bank[r][:, :], 4), X[:, 4 * g:4 * g + 4, :], ALU.add)
                last.then_inc(f_drained[r], 1)
                dve.wait_ge(f_drained[r], k + 1)
            experts(EXPERTS[0])
            sets_done(EXPERTS[0])

            layer_norm_stats("l1x.stats", X)
            again_stats("l1x.stats2")
            attention(LAYERS[2])
            batches_done(LAYERS[2])
            layer_norm_stats("l1f.stats", X)
            again_stats("l1f.stats2")
            attention(LAYERS[3])
            batches_done(LAYERS[3])
            rms_stats("l1m.stats", AO)
            normalise("l1m", AO, False)
            softmax_gates("l1m", 8, 2, None, True)
            dve.wait_ge(step("l1m.x_ready"), 1)
            experts(EXPERTS[1])
            sets_done(EXPERTS[1])

            layer_norm_stats("l2x.stats", X)
            normalise("l2x", X, True)
            for g in range(4):
                r, k = front_use("l2x", 5 + g)
                dve.wait_ge(f_full[r], k + 1)
                dve.tensor_tensor(X[:, 4 * g:4 * g + 4, :], split(f_bank[r][:, :], 4), X[:, 4 * g:4 * g + 4, :], ALU.add)\
                    .then_inc(f_drained[r], 1)
                dve.wait_ge(f_drained[r], k + 1)
            layer_norm_stats("l2m.stats", X)
            normalise("l2m", X, True)
            r, k = front_use("l2m", 4)
            dve.wait_ge(f_drained[r], k + 1)
            link(dve.tensor_copy(lg[:, :, :], ex[:, :, :]))
            link(dve.tensor_tensor(ex[:, :, :], ex[:, :, :], over(LB[:, :], B), ALU.add))
            top("l2m", 4, 32)
            link(dve.memset(run[0][:, 0:1, :], 0.0))
            link(dve.tensor_copy(run[0][:, 1:B, :], sel[:, 0:B - 1, :]))
            src = 0
            for hop in (1, 2, 4, 8):
                dve.tensor_copy(run[1 - src][:, 0:hop, :], run[src][:, 0:hop, :])
                link(dve.tensor_tensor(run[1 - src][:, hop:B, :], run[src][:, hop:B, :], run[src][:, 0:B - hop, :], ALU.add))
                src = 1 - src
            dve.sem_inc(step("l2m.run"), 1)
            link(dve.tensor_tensor(lg[:, :, :], lg[:, :, :], sel[:, :, :], ALU.mult))
            link(dve.tensor_reduce(srow0, lg[:, :, :], AX_X, ALU.add))
            link(dve.tensor_scalar(srow0, srow0, 1e-12, None, ALU.max))
            link(dve.reciprocal(srow1, srow0))
            link(row_scale(lg[:, :, :], lg[:, :, :], srow1, 32))
            r, k = front_use("l2m", 5)
            dve.wait_ge(f_full[r], k + 1)
            link(dve.tensor_scalar(ex[:, :, :], split(f_bank[r][:, :], B), float(CAPACITY), None, ALU.is_lt))
            dve.sem_inc(f_drained[r], 1)
            link(dve.tensor_tensor(GATES[:, :, 0:32], lg[:, :, :], ex[:, :, :], ALU.mult))
            experts(EXPERTS[2])
            sets_done(EXPERTS[2])

            layer_norm_stats("l3x.stats", X)
            dve.sem_inc(step("l3x.begin"), 1)
            attention(LAYERS[4])
            batches_done(LAYERS[4])

            layer_norm_stats("l3m.stats", X)
            normalise("l3m", X, True)
            dve.wait_ge(step("l3m.y"), 4)

            def scale(n, waits):
                dve.wait_ge(step("l3m.all_max"), waits)
                link(dve.tensor_scalar(quant[:, n, 2:3], quant[:, n, 1:2], 1.0 / QMAX, 1e-12, ALU.mult, ALU.max))
                dve.reciprocal(quant[:, n, 3:4], quant[:, n, 2:3]).then_inc(step("l3m.scale"), 1)

            def largest(dst, src):
                return dve.tensor_reduce(dst, src, AX_X, ALU.max, apply_absolute_value=True)

            largest(quant[:, 0, 0:1], Y[:, :, :].rearrange("p b d -> p (b d)")).then_inc(step("l3m.part_max"), 1)
            scale(0, 1)
            for g in range(4):
                r, k = front_use("l3m", g)
                dve.wait_ge(f_drained[r], k + 1)
                part = YT[:, BANK * g:BANK * g + BANK]
                dve.tensor_scalar(part, part, MAGIC, quant[:, 0, 2:3], ALU.subtract, ALU.mult).then_inc(step("l3m.yq"), 1)
            for e in range(24):
                r, k = front_use("l3m", 4 + e)
                c, w, m = e // 6, e % 6 // 3, e % 3
                dve.wait_ge(f_drained[r], k + 1)
                last = largest(part_max[:, 12 * w + 3 * c + m:12 * w + 3 * c + m + 1], (U3, G3)[w][:, m, BANK * c:BANK * c + BANK])
            link(last)
            link(largest(quant[:, 1, 0:1], part_max[:, 0:12]))
            largest(quant[:, 2, 0:1], part_max[:, 12:24]).then_inc(step("l3m.part_max"), 1)
            scale(1, 2)
            scale(2, 3)
            for h in range(6):
                part = big[:, 1024 * h:1024 * h + 1024]
                dve.wait_ge(step("l3m.g_round"), h + 1)
                dve.tensor_scalar(part, part, MAGIC, quant[:, 2, 2:3], ALU.subtract, ALU.mult).then_inc(step("l3m.g"), 1)
            for h in range(6):
                part, sg = big[:, 1024 * h:1024 * h + 1024], sig[h % 2][:, :]
                dve.wait_ge(step("l3m.sig"), h + 1)
                link(dve.tensor_scalar(sg, sg, 65536.0, MAGIC, ALU.mult, ALU.add))
                link(dve.tensor_scalar(sg, sg, MAGIC, 65535.0, ALU.subtract, ALU.min))
                dve.scalar_tensor_tensor(part, sg, 1.0 / 65536.0, part, ALU.mult, ALU.mult).then_inc(step("l3m.gs"), 1)
                dve.wait_ge(step("l3m.gs"), h + 1)
                last = largest(part_max[:, h:h + 1], part)
            link(last)
            largest(quant[:, 3, 0:1], part_max[:, 0:6]).then_inc(step("l3m.part_max"), 1)
            scale(3, 4)
            for h in range(6):
                part = big[:, 1024 * h:1024 * h + 1024]
                dve.wait_ge(step("l3m.round3"), h + 1)
                dve.wait_ge(step("l3m.u"), h + 1)
                link(dve.tensor_scalar(part, part, MAGIC, quant[:, 3, 2:3], ALU.subtract, ALU.mult))
                link(dve.tensor_tensor(part, part, U3[:, :, :].rearrange("p m t -> p (m t)")[:, 1024 * h:1024 * h + 1024], ALU.mult))
                last = largest(part_max[:, h:h + 1], part)
            link(last)
            largest(quant[:, 4, 0:1], part_max[:, 0:6]).then_inc(step("l3m.part_max"), 1)
            scale(4, 5)
            for h in range(6):
                part = big[:, 1024 * h:1024 * h + 1024]
                dve.wait_ge(step("l3m.round4"), h + 1)
                dve.tensor_scalar(part, part, MAGIC, quant[:, 4, 2:3], ALU.subtract, ALU.mult).then_inc(step("l3m.o"), 1)
            for g in range(4):
                r, k = front_use("l3m", 28 + g)
                dve.wait_ge(f_full[r], k + 1)
                dve.tensor_tensor(X[:, 4 * g:4 * g + 4, :], split(f_bank[r][:, :], 4), X[:, 4 * g:4 * g + 4, :], ALU.add)\
                    .then_inc(f_drained[r], 1)


def _layout(v):
    import numpy as np

    f = np.float32
    bf = v["L2_ffn_W1"].dtype
    D = P
    A = {}

    def arr(name):
        return np.asarray(v[name])

    A["x"], A["ctx"] = arr("x"), arr("ctx_1024")
    A["ctxT"] = arr("ctx_1024").transpose(0, 2, 1)
    A["pos"] = arr("pos_1xS2").astype(np.int32).reshape(1, P)
    A["mask"] = arr("mask_BxS2_bf1").view(np.uint8).reshape(1, B * P)

    def tiles(w):
        n = w.shape[0] // P
        return w.reshape(n, P, -1).transpose(1, 0, 2).reshape(P, -1)

    A["w0x"] = np.concatenate([arr("L0_xattn_Wq"), arr("L0_xattn_Wk"), arr("L0_xattn_Wv"), tiles(arr("L0_xattn_Wo"))], 1)

    def evens_odds(w, swap):
        w = w.reshape(w.shape[0], 16, 32, 2).transpose(0, 1, 3, 2)
        return (w[:, :, ::-1] if swap else w).reshape(w.shape[0], 1024)

    parts = [evens_odds(arr(n), s) for n in ("L0_ffn_q_w", "L0_ffn_k_w") for s in (0, 1)]
    A["w0f"] = np.concatenate(parts + [arr("L0_ffn_v_w"), tiles(arr("L0_ffn_o_w"))], 1)
    biases = [evens_odds(arr(n).reshape(1, -1), s).reshape(8, P).T for n in ("L0_ffn_q_b", "L0_ffn_k_b") for s in (0, 1)]

    def spread(w, head_of, count, order):
        out = np.zeros((D, count, 4, 32), w.dtype)
        for m in range(count):
            for g in range(4):
                h = head_of(m, g)
                out[:, m, g, 0:8] = w[:, 8 * h:8 * h + 8][:, order]
        return out.reshape(D, count * P)

    same, swapped = list(range(8)), [4, 5, 6, 7, 0, 1, 2, 3]
    x_head, f_head = lambda m, g: 4 * m + g, lambda m, g: 4 * g + m
    A["w1x"] = np.concatenate([spread(arr("L1_xattn_Wq").T, x_head, 4, same), spread(arr("L1_xattn_Wk").T, x_head, 4, same),
                               arr("L1_xattn_Wv").T, arr("L1_xattn_Wo").T], 1)
    qkv = arr("L1_ffn_wqkv").T
    q, k, vv = qkv[:, 0:128], qkv[:, 128:160], qkv[:, 160:192]
    A["w1f"] = np.concatenate([spread(q, f_head, 4, same), spread(q, f_head, 4, swapped), spread(k, lambda m, g: g, 1, same),
                               spread(k, lambda m, g: g, 1, swapped), vv, arr("L1_ffn_wo").T], 1)
    A["wl2"] = np.concatenate([arr("L2_xattn_W")[:, 0:D].T, arr("L2_xattn_W")[:, D:].T], 1)
    A["w3"] = np.concatenate([tiles(arr("L3_ffn_w_gate")), tiles(arr("L3_ffn_w_up")), arr("L3_ffn_w_down")], 1)
    cols = [arr("L1_xattn_g1"), arr("L1_xattn_b1"), arr("L1_xattn_g2"), arr("L1_xattn_b2"), arr("L1_ffn_ln1_w"),
            arr("L1_ffn_ln2_w"), np.tile(arr("L0_ffn_theta"), 4), arr("L0_ffn_gamma2")]
    A["vec"] = np.concatenate([c.reshape(P, 1) for c in cols] + biases, 1)
    A["rows"] = np.concatenate([arr("L0_ffn_gamma1"), arr("L0_ffn_gamma2")]).reshape(1, -1)
    A["l0f_vb"] = arr("L0_ffn_v_b").reshape(1, -1)
    A["l0m_rb"] = arr("L0_ffn_router_b").reshape(1, -1)
    A["l2m_bias"] = arr("L2_ffn_bias").reshape(1, -1)
    A["brow"] = np.concatenate([arr("L0_xattn_bo"), arr("L0_ffn_o_b"), arr("L1_xattn_bo"), arr("L2_xattn_b")]).reshape(1, -1)
    A["b2"] = np.concatenate([arr("L0_ffn_re_b2"), arr("L0_ffn_sh_b2").reshape(1, D)], 0)
    A["rw"] = np.concatenate([arr("L0_ffn_router_w"), arr("L1_ffn_gate_w").T], 1)
    A["rwb"] = arr("L2_ffn_gate_w").T
    w1 = np.concatenate([arr("L0_ffn_re_w1"), arr("L0_ffn_sh_w1")[None]], 0)
    w2 = np.concatenate([arr("L0_ffn_re_w2"), arr("L0_ffn_sh_w2")[None]], 0)
    b1 = np.concatenate([arr("L0_ffn_re_b1"), arr("L0_ffn_sh_b1")[None]], 0)
    A["l0m"] = np.concatenate([w1, w2, b1[:, :, None]], 2)
    w2 = arr("L1_ffn_w2").transpose(0, 2, 1).reshape(8, 2, P, D).transpose(0, 2, 1, 3).reshape(8, P, 2 * D)
    A["l1m"] = np.concatenate([arr("L1_ffn_w13").transpose(0, 2, 1), w2], 2)
    sets = np.zeros((17, P, 3 * P), bf)
    sets[:16, :, 0:P] = arr("L2_ffn_W1").reshape(16, 2, D, 64).transpose(0, 2, 1, 3).reshape(16, D, P)
    sets[:16, :, P:2 * P] = arr("L2_ffn_W3").reshape(16, 2, D, 64).transpose(0, 2, 1, 3).reshape(16, D, P)
    sets[:16, :, 2 * P:] = arr("L2_ffn_W2").reshape(16, P, D)
    sets[16, :, 0:64] = arr("L2_ffn_sw1").T
    sets[16, :, P:P + 64] = arr("L2_ffn_sw3").T
    sets[16, 0:64, 2 * P:] = arr("L2_ffn_sw2").T
    A["l2m"] = sets

    n = np.arange(P)
    pos = np.arange(P, dtype=f)
    div = np.exp(np.arange(0, D, 2, dtype=f) * f(-(math.log(10000.0) / D))).astype(f)
    ang = pos[:, None] * div
    table = np.stack([np.sin(ang), np.cos(ang)], -1).reshape(P, D).astype(f)
    inv = (f(1.0) / f(10000.0) ** (np.arange(0, 8, 2, dtype=f) / f(8))).astype(f)
    freq = (pos[:, None] * inv[None, :]).astype(f)
    emb = np.concatenate([freq, freq], 1)
    cos1, sin1 = np.zeros((P, P), f), np.zeros((P, P), f)
    for g in range(4):
        for d in range(8):
            cos1[32 * g + d] = np.cos(emb[:, d])
            sin1[32 * g + d] = np.sin(emb[:, d]) * (-1 if d < 4 else 1)
    cols = np.stack([n.astype(f), (n % 32 == 8).astype(f), np.where(n // 32 % 2 == 0, -1, 1).astype(f), np.full(P, MAGIC, f)], 1)
    A["cf"] = np.concatenate([np.eye(P, dtype=f), (n[:, None] < n[None, :]).astype(f), np.tile(pos, (P, 1)), table, cos1, sin1,
                              cols, np.ones((P, P), f)], 1)
    causal = n[None, :] <= n[:, None]
    grouped = n[None, :] <= n[:, None] - 64
    hide = lambda keep: np.where(keep, 0.0, NEG).astype(bf)
    A["cb"] = np.concatenate([np.eye(P, dtype=bf)] + [hide(causal)] * HEADS + [hide(causal & ~grouped), hide(grouped)], 1)
    return A


def kernel(**inputs):
    import numpy as np
    import concourse.bacc as bacc
    from concourse.bass_utils import run_bass_kernel_spmd

    nc = bacc.Bacc("TRN2", target_bir_lowering=False, num_devices=1)
    arrays, aps = {}, {}
    for name, value in _layout(inputs).items():
        value = np.ascontiguousarray(value)
        arrays[f"in_{name}"] = value
        aps[name] = nc.dram_tensor(f"in_{name}", value.shape, mybir.dt.from_np(value.dtype), kind="ExternalInput").ap()
    out = nc.dram_tensor("out_x", (B, P, P), F32, kind="ExternalOutput").ap()
    build(nc, aps, out)
    r = run_bass_kernel_spmd(nc, [arrays], core_ids=[0])
    return r.results[0]["out_x"]
```

```python
from contextlib import ExitStack
import math

import concourse.bass as bass
from concourse import mybir
from concourse.alu_op_type import AluOpType as ALU

ACT = mybir.ActivationFunctionType
AX_X = mybir.AxisListType.X
F32 = mybir.dt.float32
BF16 = mybir.dt.bfloat16
I32 = mybir.dt.int32
U32 = mybir.dt.uint32
U8 = mybir.dt.uint8

P = 128
B = 16
BANK = 512
PAIRS = B // 2
HEADS = 4
EPS = 1e-5
NEG = -1e30
MAGIC = 1.5 * 2.0 ** 23
QMAX = 32767.0

LAYERS = [
    dict(name="l0x", units=2, heads=8, dim=64, scale=64 ** -0.5, jobs=[[0, 1], [2, 3]],
         back=["V0", "V1", "OT0", "OP0"]),
    dict(name="l0f", units=4, heads=16, dim=64, scale=64 ** -0.5, jobs=[[0, 1, 2], [3, 4, 5], [6, 7, 8], [9, 10]],
         back=["V0", "V1", "OT0", "V2", "V3", "OT1", "OP0"]),
    dict(name="l1x", units=4, heads=16, dim=8, scale=8 ** -0.5, jobs=[[0], [1], [2], [3]],
         back=["V0", "OB0", "OT0", "OP0"]),
    dict(name="l1f", units=4, heads=16, dim=8, scale=8 ** -0.5, jobs=[[0], [1], [2, 3], []],
         back=["V0", "OB0", "OT0", "OP0"]),
    dict(name="l3x", units=1, heads=1, dim=128, scale=1.0, jobs=[[0]], back=["V0"]),
]
for L in LAYERS:
    L["front"] = sum(len(slot) for slot in L["jobs"])
    L["turns"] = sum(use[:2] == "OT" for use in L["back"])


def schedule(L):
    units = L["units"]
    if units == 1:
        return [("Y", 0, "next"), ("S", 0, "own"), ("T", 0, "last"), ("E", 0, "own"), ("F", 0, "next"), ("V", 0, "last")]

    def unit(what, t):
        return (what, t, "own") if t >= 0 else (what, t + units, "last")

    parts = [("Y", 0, "next")]
    if L["dim"] == 8:
        before_jobs = [[], [("V", 3, "last")], [], [("OP", 0, "last"), ("V", 0, "own")]]
        at_end = [[("V", 2, "last")], [("OB", 0, "last")], [("OT", 0, "last")], [("V", 1, "own")]]
        for t in range(units):
            jobs = [("F", job, "next") for job in L["jobs"][t]]
            parts += [("S", t, "own")] + before_jobs[t] + jobs + [("E", t, "own"), unit("T", t - 1)] + at_end[t]
        return parts
    for t in range(units):
        jobs = [("F", job, "next") for job in L["jobs"][t]]
        parts.append(("S", t, "own"))
        if t == 2:
            parts.append(("OP", 0, "last"))
        parts += [unit("V", t - 2)] + jobs[:1] + [("E", t, "own"), unit("T", t - 1)]
        if units == 2:
            parts += [("OT", 0, "last")] * (t == 1) + jobs[1:] + [("OP", 0, "last")] * (t == 1)
        else:
            parts += jobs[1:]
            if t == 1:
                parts.append(("OT", L["turns"] - 1, "last"))
            if t == 3 and L["turns"] == 2:
                parts.append(("OT", 0, "own"))
    return parts


EXPERTS = [
    dict(name="l0m", steps=32, halves=1, gated=False, downs=[(0, P)], up=P, wcols=2 * P + 1),
    dict(name="l1m", steps=8, halves=2, gated=True, downs=[(0, P)], up=4 * P, wcols=6 * P),
    dict(name="l2m", steps=17, halves=1, gated=True, downs=[(0, 64), (64, P)], up=2 * P, wcols=3 * P),
]
CHUNKS = B * P // BANK
GCOLS = 34
CAPACITY = 2 * 512 * 4 // 32


def build(nc, a, out):
    ctx = ExitStack()
    with ctx:
        def sb(name, shape, dt=F32):
            return ctx.enter_context(nc.sbuf_tensor(name, shape, dt))

        def sem(name):
            return ctx.enter_context(nc.semaphore(name))

        def pair(name):
            return [sem(f"{name}{s}") for s in range(2)]

        def bank(name):
            return ctx.enter_context(nc.psum_tensor(name, [P, BANK], F32))

        s_bank = [bank(f"s_bank{s}") for s in range(2)]
        t_bank = [bank(f"t_bank{s}") for s in range(2)]
        v_bank = [bank(f"v_bank{s}") for s in range(2)]
        f_bank = [bank(f"f_bank{s}") for s in range(2)]

        X = sb("X", [P, B, P])
        AO = sb("AO", [P, B, P])
        Y = sb("Y", [P, B, P])
        YT = sb("YT", [P, B * P])
        CTX = sb("CTX", [P, B, P])
        big = sb("big", [P, 6 * 8 * P])
        work = sb("work", [P, 6 * 8 * P])
        qT = [work[:, 1024 * s:1024 * s + 1024] for s in range(2)]
        kT = [work[:, 1024 * s + 2048:1024 * s + 3072] for s in range(2)]
        o_tok = [work[:, 1024 * s + 4096:1024 * s + 5120] for s in range(2)]
        GT = work[0:32, 0:B * P]
        U3 = work[:, :].rearrange("p (m t) -> p m t", m=3)
        W0X = sb("W0X", [P, 4, 4 * P])
        W1X = sb("W1X", [P, 10 * P])
        W1F = sb("W1F", [P, 8 * P + 2 * P + 32 + P])
        WL2 = sb("WL2", [P, 2 * P])
        W3N = work[:, 1024:1024 + 9 * P]
        POSF = work[:, 0:3 * P].rearrange("p (m s) -> p m s", m=3)
        HOT = work[:, 3 * P:6 * P].rearrange("p (m s) -> p m s", m=3)
        W3T = sb("W3T", [P, 9 * P])
        W3M = sb("W3M", [P, 36])
        W3S = sb("W3S", [P, 36])
        W3R = sb("W3R", [P, 36])
        VEC = sb("VEC", [P, a["vec"].shape[1]])
        ROWS = sb("ROWS", [P, 3 * P])
        RB = sb("RB", [P, 31])
        LB = sb("LB", [P, 32])
        RW = sb("RW", [P, 31 + 8 + 32])
        RWB = sb("RWB", [P, 32], BF16)
        BROW = sb("BROW", [1, 4 * P])
        VB = sb("VB", [P, 8 * P])
        MASK = sb("MASK", [P, B, P], BF16)
        MASKU = sb("MASKU", [P, B * P], U8)
        NANF = sb("NANF", [P, B])
        POSI = sb("POSI", [P, P], I32)
        POSG = sb("POSG", [P, P], I32)
        PET = sb("PET", [P, 3 * P])
        CF = sb("CF", [P, a["cf"].shape[1]])
        CB = sb("CB", [P, a["cb"].shape[1]], BF16)
        ones_row = sb("ones_row", [1, P])
        half_neg = sb("half_neg", [P, B])
        B2 = sb("B2", [32, P])
        GATES = sb("GATES", [P, B, GCOLS])

        y_tok = [sb(f"y_tok{s}", [P, P]) for s in range(2)]
        y_aux = [sb(f"y_aux{s}", [P, P]) for s in range(2)]
        yT = [sb(f"yT{s}", [P, P]) for s in range(2)]
        cT = [sb(f"cT{s}", [P, P]) for s in range(2)]
        V64 = [sb(f"V64_{s}", [P, 16, 65]) for s in range(2)]
        V8 = [W0X[:, 1 + s, :].rearrange("p (h c) -> p h c", c=32) for s in range(2)]
        spread_o = W0X[:, 0, :]
        V128 = [sb(f"V128_{s}", [P, P + 1]) for s in range(2)]
        rope_a = [sb(f"rope_a{s}", [P, BANK]) for s in range(2)]
        rope_b = [sb(f"rope_b{s}", [P, BANK]) for s in range(2)]
        shifted = [sb(f"shifted{s}", [P, BANK]) for s in range(2)]
        h_all = sb("h_all", [P, 4 * BANK])
        hT = [h_all[:, BANK * s:BANK * s + BANK] for s in range(4)]
        probs, probsT = hT[0:2], hT[2:4]
        row_max = [sb(f"row_max{s}", [P, HEADS]) for s in range(2)]
        recips = [sb(f"recips{s}", [P, 16]) for s in range(2)]
        oT = sb("oT", [P, 8 * P])
        wset = [sb(f"wset{s}", [P, 6 * P]) for s in range(2)]
        wraw = [sb(f"wraw{s}", [P, 3 * P], BF16) for s in range(2)]
        act_sb = shifted
        st = sb("st", [P, B, 6])
        small = sb("small", [P, 12, B])
        cstat = sb("cstat", [P, 2, B])
        lg = sb("lg", [P, B, 32])
        ex = sb("ex", [P, B, 32])
        top8 = sb("top8", [P, B, 8])
        idx8 = sb("idx8", [P, B, 8], U32)
        idxf = sb("idxf", [P, B, 8])
        hits = h_all[:, :].rearrange("p (b k e) -> p b k e", b=B, k=4)
        sel = sb("sel", [P, B, 32])
        run = [rope_a[s][:, :].rearrange("p (b e) -> p b e", b=B) for s in range(2)]
        quant = sb("quant", [P, 5, 4])
        part_max = sb("part_max", [P, 24])
        sig = [CTX[:, 8 * s:8 * s + 8, :].rearrange("p b d -> p (b d)") for s in range(2)]
        csum = sb("csum", [P, B])
        tmpT = sb("tmpT", [P, 4, P])
        joined = [sb(f"joined{s}", [P, P]) for s in range(2)]

        mean, r1, r12, var, ve, t0, t1, ms = (small[:, n, :] for n in range(8))
        srow0, srow1, srow2, srow3 = (small[:, n, :] for n in range(8, 12))
        ident = CF[:, 0:P]
        before = CF[:, P:2 * P]
        iota_row = CF[:, 2 * P:3 * P]
        pe = CF[:, 3 * P:4 * P]
        cos1 = CF[:, 4 * P:5 * P]
        sin1 = CF[:, 5 * P:6 * P]
        part_no = CF[:, 6 * P:6 * P + 1]
        ones_at = CF[:, 6 * P + 1:6 * P + 2]
        sin_sign = CF[:, 6 * P + 2:6 * P + 3]
        magic = CF[:, 6 * P + 3:6 * P + 4]
        ones_sq = CF[:, 6 * P + 4:7 * P + 4]
        part_one = CF[:, 6 * P + 4:6 * P + 5]
        ident_bf = CB[:, 0:P]
        causal_bf = CB[:, P:P + BANK]
        own_bf = CB[:, P + BANK:P + BANK + 2 * P]
        names = ["l1x_g1", "l1x_b1", "l1x_g2", "l1x_b2", "l1f_ln1", "l1f_ln2", "theta", "gamma2"]
        vec = {n: VEC[:, j:j + 1] for j, n in enumerate(names)}
        qb_a = VEC[:, 8:16]
        qb_b = VEC[:, 16:24]
        kb_a = VEC[:, 24:32]
        kb_b = VEC[:, 32:40]
        gamma1_row = ROWS[:, 0:P]
        gamma2_row = ROWS[:, P:2 * P]
        bo = {"l0x": BROW[:, 0:P], "l0f": BROW[:, P:2 * P], "l1x": BROW[:, 2 * P:3 * P], "l2x": BROW[:, 3 * P:4 * P]}
        w0f = {n: big[:, 1024 * j:1024 * j + 1024] for j, n in enumerate(["qa", "qb", "ka", "kb", "v", "o"])}
        w1f = {"qa": W1F[:, 0:512], "qb": W1F[:, 512:1024], "ka": W1F[:, 1024:1152], "kb": W1F[:, 1152:1280],
               "v": W1F[:, 1280:1312], "o": W1F[:, 1312:1440]}
        w1x = {"q": W1X[:, 0:512], "k": W1X[:, 512:1024], "v": W1X[:, 1024:1152], "o": W1X[:, 1152:1280]}
        TAB = sb("TAB", [P, 2 * P + 16 * P])
        cos0, sin0 = TAB[:, 0:P], TAB[:, P:2 * P]
        tbq, tbk = TAB[:, 2 * P:10 * P], TAB[:, 10 * P:18 * P]
        G3 = big[:, :].rearrange("p (m t) -> p m t", m=3)

        in_x, in_ctx, in_c, in_w0x, in_w0f, in_w1, in_l3 = (sem(n) for n in (
            "in_x", "in_ctx", "in_c", "in_w0x", "in_w0f", "in_w1", "in_l3"))
        y_ready, aux_ready, cT_ready, v_dma = pair("y_ready"), pair("aux_ready"), pair("cT_ready"), pair("v_dma")
        f_full, f_drained = pair("f_full"), pair("f_drained")
        b_drained, turned, projected, regrouped = pair("b_drained"), sem("turned"), sem("projected"), sem("regrouped")
        s_full, shifted_ready, max_ready = pair("s_full"), pair("shifted_ready"), pair("max_ready")
        probs_ready, t_full, probsT_ready = pair("probs_ready"), pair("t_full"), pair("probsT_ready")
        pv_done, recip_ready = pair("pv_done"), pair("recip_ready")
        rope_sum, rope_done, k3_ready = pair("rope_sum"), pair("rope_done"), pair("k3_ready")
        grouped_ready, joined_ready = pair("grouped_ready"), pair("joined_ready")
        dve_chain, pool_chain = sem("dve_chain"), sem("pool_chain")
        w_loaded, w_cast = pair("w_loaded"), pair("w_cast")
        g_full, g_drained, u_full, h_ready = pair("g_full"), pair("g_drained"), pair("u_full"), pair("h_ready")
        d_full, d_drained = pair("d_full"), pair("d_drained")
        stored = sem("stored")
        step_sem = {}

        def step(name):
            if name not in step_sem:
                step_sem[name] = sem(name.replace(".", "_"))
            return step_sem[name]

        front_at, n = {}, 0
        for name, uses in [("setup", 4), ("l0x", 4 * B), ("l0f", 11 * B), ("l0m", 13), ("l1x", 4 * B), ("l1f", 4 * B),
                           ("l1m", 5), ("l2x", 9), ("l2m", 6), ("l3x", B), ("l3m", 32)]:
            front_at[name] = n
            n += uses
        unit_at, back_at, turn_at, proj_at = {}, {}, {}, {}
        nu = nb = nt = np_ = 0
        for j, L in enumerate(LAYERS):
            name = L["name"]
            L["no"] = j
            unit_at[name], back_at[name], turn_at[name], proj_at[name] = nu, nb, nt, np_
            nu, nb, nt = nu + L["units"] * B, nb + len(L["back"]) * B, nt + L["turns"] * B
            np_ += B * (L["turns"] > 0)
        hid_at, sum_at, set_at = {}, {}, {}
        nh = nd = ns = 0
        for M in EXPERTS:
            hid_at[M["name"]], sum_at[M["name"]], set_at[M["name"]] = nh, nd, ns
            nh += M["steps"] * CHUNKS * M["halves"]
            nd += M["steps"] * CHUNKS * len(M["downs"])
            ns += M["steps"]
        ungated = hid_at["l1m"]
        ORDER = {L["name"]: schedule(L) for L in LAYERS}

        def place(at, per, i, s, c):
            c = at + per * s + c
            return c % 2, per * i + c // 2 + 1

        def front_use(name, c):
            c += front_at[name]
            return c % 2, c // 2 + 1

        def heads_of(L, u):
            if L["dim"] == 64:
                return [(8 * (u // 2) + u % 2 + 2 * m, 64 * (u % 2), 4 * (u // 2) + m, 4 * (u // 2) + m, 64,
                         8 * (u // 2) + u % 2 + 2 * m) for m in range(HEADS)]
            if L["name"] == "l1x":
                return [(4 * u + m, 32 * u, m, m, 32, 4 * u + m) for m in range(HEADS)]
            return [(4 * u + m, 32 * u, m, 0, 32, u) for m in range(HEADS)]

        regrouped_at = {"l1x": 0, "l1f": B}
        recips_at, nr = {}, 0
        for L in LAYERS:
            recips_at[L["name"]] = nr
            nr += L["units"] * PAIRS if L["dim"] == 64 else PAIRS

        def batches(eng, n, do):
            def step_of(i, own):
                for what, u, whose in ORDER[n]:
                    s = own + {"last": -1, "own": 0, "next": 1}[whose]
                    if isinstance(i, int):
                        if not 0 <= 2 * i + s < B:
                            continue
                        do(what, u, i + s // 2, s % 2)
                    else:
                        do(what, u, i, s)

            step_of(0, -1)
            step_of(0, 0)
            with eng.Fori(0, PAIRS - 1) as i:
                step_of(i, 1)
                step_of(i, 2)
            step_of(PAIRS - 1, 1)
            step_of(PAIRS - 1, 2)

        def back_use(L, use, i, s):
            return place(back_at[L["name"]], len(L["back"]), i, s, L["back"].index(use))

        def pv_use(L, u):
            return f"V{u}" if L["dim"] == 64 else "V0"

        def sets(eng, M, chunk):
            pairs, odd = M["steps"] // 2, M["steps"] % 2
            with eng.Fori(0, pairs - 1 + odd) as i:
                for s in range(2):
                    for c in range(CHUNKS):
                        chunk(i, s, c, False)
            for s in range(1 if odd else 2):
                for c in range(CHUNKS):
                    chunk(pairs - 1 + odd, s, c, s == (0 if odd else 1) and c == CHUNKS - 1)

        def after(i, s, c):
            return (i, s, c + 1) if c + 1 < CHUNKS else (i, 1, 0) if s == 0 else (i + 1, 0, 0)

        def last_sum(M, i, s):
            per = CHUNKS * len(M["downs"])
            return place(sum_at[M["name"]], per, i, s, per - 1)

        def col(ap, b):
            return ap[:, bass.ds(b, 1)]

        def tile(t, b):
            return t[:, bass.ds(b, 1), :].rearrange("p o d -> p (o d)")

        def wide(ap, n, m):
            return ap.unsqueeze(2).to_broadcast([P, n, m])

        def over(ap, n):
            return ap.unsqueeze(1).to_broadcast([P, n, ap.shape[1]])

        def split(ap, n):
            return ap.rearrange("p (n m) -> p n m", n=n)

        def rows_to_all(ap):
            return ap.partition_broadcast(P).rearrange("p o n -> p (o n)")

        block = ctx.enter_context(nc.Block())

        @block.sync
        def _(sp):
            def load(dst, src, s):
                sp.dma_start(dst, src).then_inc(s, 16)

            load(X[:, :, :], a["x"].rearrange("b s d -> s b d"), in_x)
            load(CF[:, :], a["cf"], in_c)
            load(CB[:, :], a["cb"], in_c)
            load(VEC[:, :], a["vec"], in_c)
            load(BROW[:, :], a["brow"], in_c)
            load(W0X[:, :, :], split(a["w0x"], 4), in_w0x)
            load(CTX[:, :, :], a["ctx"].rearrange("b s d -> s b d"), in_ctx)
            load(POSI[:, :], rows_to_all(a["pos"]), in_l3)
            load(MASKU[:, :], rows_to_all(a["mask"]), in_l3)
            load(W3N[:, :], a["w3"], in_l3)
            load(ROWS[:, 0:2 * P], rows_to_all(a["rows"]), in_l3)
            load(VB[:, :], rows_to_all(a["l0f_vb"]), in_l3)
            load(RB[:, :], rows_to_all(a["l0m_rb"]), in_l3)
            load(LB[:, :], rows_to_all(a["l2m_bias"]), in_l3)
            load(B2[:, :], a["b2"], in_l3)
            load(RW[:, 0:39], a["rw"], in_l3)
            load(RWB[:, :], a["rwb"], in_l3)

            def context0(i, s):
                sp.dma_start(cT[s][:, :], a["ctxT"][bass.ds(2 * i + s, 1), :, :].rearrange("o p n -> (o p) n")).then_inc(cT_ready[s], 16)

            for s in range(2):
                context0(0, s)
            load(big[:, :], a["w0f"], in_w0f)
            load(W1X[:, :], a["w1x"], in_w1)
            load(W1F[:, :], a["w1f"], in_w1)
            load(WL2[:, :], a["wl2"], in_w1)
            with sp.Fori(1, PAIRS) as i:
                for s in range(2):
                    for job in (2, 3):
                        r, k = place(front_at["l0x"], 4, i - 1, s, job)
                        sp.wait_ge(f_full[r], k + 1)
                    context0(i, s)

            def weights(M, dst, wait):
                def one(i, s):
                    wait(i, s)
                    sp.dma_start(dst[s][:, 0:M["wcols"]], a[M["name"]][bass.ds(2 * i + s, 1), :, :].rearrange("o p n -> (o p) n")).then_inc(w_loaded[s], 16)

                for s in range(2):
                    one(0, s)
                with sp.Fori(1, M["steps"] // 2) as i:
                    for s in range(2):
                        one(i, s)
                if M["steps"] % 2:
                    one(M["steps"] // 2, 0)

            def slot_free(M, prev):
                def wait(i, s):
                    if isinstance(i, int) and i == 0:
                        if prev is None:
                            return
                        r, k = last_sum(prev, prev["steps"] // 2 - 1, s)
                    else:
                        r, k = last_sum(M, i - 1, s)
                    sp.wait_ge(d_full[r], k + 1)
                return wait

            weights(EXPERTS[0], wset, slot_free(EXPERTS[0], None))
            weights(EXPERTS[1], wset, slot_free(EXPERTS[1], EXPERTS[0]))

            def raw_free(i, s):
                if isinstance(i, int) and i == 0:
                    sp.wait_ge(w_loaded[s], 16 * (set_at["l2m"] // 2))
                else:
                    sp.wait_ge(w_cast[s], i)

            weights(EXPERTS[2], wraw, raw_free)

            sp.wait_ge(step("l3x.begin"), 1)

            def context3(i, s):
                b = 2 * i + s
                if not (isinstance(i, int) and i == 0):
                    sp.wait_ge(k3_ready[s], 2 * i)
                sp.dma_start(cT[s][:, :], a["ctxT"][bass.ds(b, 1), :, :].rearrange("o p n -> (o p) n")).then_inc(cT_ready[s], 16)
                if not (isinstance(i, int) and i == 0):
                    r, k = place(unit_at["l3x"], 1, i - 1, s, 0)
                    sp.wait_ge(pv_done[r], k + 1)
                sp.dma_start(V128[s][:, 0:P], a["ctx"][bass.ds(b, 1), :, :].rearrange("o p n -> (o p) n")).then_inc(v_dma[s], 16)

            for s in range(2):
                context3(0, s)
            with sp.Fori(1, PAIRS) as i:
                for s in range(2):
                    context3(i, s)

            for g in range(4):
                r, k = front_use("l3m", 28 + g)
                sp.wait_ge(f_drained[r], k + 1)
                sp.dma_start(out[4 * g:4 * g + 4].rearrange("b s d -> s b d"), X[:, 4 * g:4 * g + 4, :]).then_inc(stored, 16)
            sp.wait_ge(stored, 4 * 16)

        @block.gpsimd
        def _(pool):
            links = [0]

            def link(ins):
                links[0] += 1
                ins.then_inc(pool_chain, 1)
                pool.wait_ge(pool_chain, links[0])

            for ring in (f_full, f_drained, b_drained, s_full, shifted_ready, max_ready, probs_ready, t_full, probsT_ready,
                         pv_done, rope_sum, rope_done, grouped_ready, joined_ready, g_full, g_drained, u_full, h_ready,
                         d_full, d_drained):
                for s in range(2):
                    pool.sem_inc(ring[s], 1)
            link(pool.memset(half_neg[:, :], -0.5))
            pool.memset(ones_row[:, :], 1.0)
            for s in range(2):
                pool.memset(V64[s][:, :, 64:65], 1.0)
                pool.memset(V128[s][:, P:P + 1], 1.0)
            pool.memset(ex[:, :, :], -1.0)
            link(pool.memset(GATES[:, :, :], 0.0))
            pool.memset(GATES[:, :, 32:33], 1.0)
            pool.memset(GATES[:, :, 31:32], 1.0).then_inc(step("setup.ones"), 1)

            def power(name, src, dst):
                pool.wait_ge(step(name), 1)
                pool.tensor_tensor(dst, src, half_neg[:, :], ALU.pow).then_inc(step(name + "_pow"), 1)

            def attention(L):
                n = L["name"]

                def do(what, u, i, s):
                    t = s % 2
                    if n == "l0f" and what == "Y":
                        pool.wait_ge(y_ready[t], PAIRS * L["no"] + s // 2 + 1 + i)
                        pool.tensor_tensor(y_aux[t][:, :], y_tok[t][:, :], gamma1_row, ALU.mult).then_inc(aux_ready[t], 1)
                    if n == "l0f" and what == "F" and u in (2, 4, 6, 8):
                        piece = u // 2 - 1
                        half = slice(BANK * (piece % 2), BANK * (piece % 2) + BANK)
                        r, k = place(front_at[n], L["front"], i, s, u)
                        pool.wait_ge(f_drained[r], k + 1)
                        r, k = place(0, 4, i, s, piece)
                        pool.tensor_tensor(rope_a[r][:, :], rope_a[r][:, :], rope_b[r][:, :], ALU.add).then_inc(rope_sum[r], 1)
                        pool.wait_ge(rope_sum[r], k + 1)
                        pool.tensor_tensor((qT if piece < 2 else kT)[t][:, half], rope_a[r][:, :],
                                           (tbq if piece < 2 else tbk)[:, half], ALU.add).then_inc(rope_done[r], 1)
                    if n == "l1f" and what == "F" and u in (2, 3):
                        r, k = place(front_at[n], L["front"], i, s, u)
                        pool.wait_ge(f_drained[r], k + 1)
                        r, k = place(4 * B, 2, i, s, u - 2)
                        cols = BANK if u == 2 else P
                        pool.tensor_tensor((qT if u == 2 else kT)[t][:, 0:cols], rope_a[r][:, 0:cols],
                                           rope_b[r][:, 0:cols], ALU.add).then_inc(rope_done[r], 1)
                    if n == "l3x" and what == "F":
                        pool.wait_ge(cT_ready[t], 16 * (PAIRS + s // 2 + 1) + 16 * i)
                        pool.wait_ge(y_ready[t], PAIRS * L["no"] + s // 2 + 1 + i)
                        pool.tensor_tensor(kT[t][:, 0:P], cT[t][:, :], PET[:, 0:P], ALU.add).then_inc(k3_ready[t], 1)
                        pool.tensor_tensor(kT[t][:, P:2 * P], cT[t][:, :], PET[:, 2 * P:3 * P], ALU.add).then_inc(k3_ready[t], 1)
                batches(pool, n, do)

            def residual(name):
                pool.wait_ge(step(name + ".y"), 4)
                link(pool.tensor_tensor(X[:, :, :], X[:, :, :], AO[:, :, :], ALU.add))
                if name == "l0m":
                    pool.wait_ge(step("l0m.an"), 4)
                    link(pool.tensor_tensor(X[:, :, :], X[:, :, :], Y[:, :, :], ALU.add))
                pool.sem_inc(step(name + ".x_ready"), 1)

            power("ctx.stats", ve, r1)
            power("l0x.stats", ve, r1)
            pool.wait_ge(in_l3, 16 * 10)
            power("l0f.stats", ve, r1)
            power("l0f.stats2", t0, t1)
            for s in range(2):
                pool.memset(V8[s][:, :, 8:9], 1.0)
                pool.memset(V8[s][:, :, 9:32], 0.0)
            pool.wait_ge(step("setup.tables"), 1)
            attention(LAYERS[1])
            power("l0m.stats", ve, r1)
            residual("l0m")
            power("l1x.stats", ve, r1)
            power("l1x.stats2", t0, t1)
            power("l1f.stats", ve, r1)
            power("l1f.stats2", t0, t1)
            attention(LAYERS[3])
            power("l1m.stats", ve, r1)
            residual("l1m")
            power("l2x.stats", ve, r1)
            power("l2m.stats", ve, r1)
            power("l3x.stats", ve, r1)
            attention(LAYERS[4])
            power("l3m.stats", ve, r1)
            largest = 0
            for n, count in enumerate([1, 2, 1, 1]):
                pool.wait_ge(step("l3m.part_max"), n + 1)
                for c in range(count):
                    pool.partition_all_reduce(quant[:, largest, 1:2], quant[:, largest, 0:1], P,
                                              bass.bass_isa.ReduceOp.max).then_inc(step("l3m.all_max"), 1)
                    largest += 1
                if n == 1:
                    for h in range(6):
                        pool.wait_ge(step("l3m.u_round"), h + 1)
                        u = U3[:, :, :].rearrange("p m t -> p (m t)")[:, 1024 * h:1024 * h + 1024]
                        pool.tensor_scalar(u, u, MAGIC, quant[:, 1, 2:3], ALU.subtract, ALU.mult).then_inc(step("l3m.u"), 1)

        @block.scalar
        def _(act):
            def attention(L):
                n, units = L["name"], L["units"]
                cols = BANK if units > 1 else P

                def do(what, u, i, s):
                    t = s % 2
                    if what == "E":
                        r, k = place(unit_at[n], units, i, s, u)
                        act.wait_ge(shifted_ready[r], k + 1)
                        act.wait_ge(t_full[r], k)
                        act.activation(probs[r][:, 0:cols], shifted[r][:, 0:cols], ACT.Exp, scale=L["scale"]).then_inc(probs_ready[r], 1)
                    if what == "T":
                        r, k = place(unit_at[n], units, i, s, u)
                        act.wait_ge(t_full[r], k + 1)
                        act.wait_ge(pv_done[r], k)
                        act.activation(probsT[r][:, 0:cols], t_bank[r][:, 0:cols], ACT.Copy).then_inc(probsT_ready[r], 1)
                    if what == "V" and u == units - 1 and L["dim"] == 8:
                        r, k = place(unit_at[n], units, i, s, u)
                        act.wait_ge(pv_done[r], k + 1)
                        r, k = back_use(L, "V0", i, s)
                        act.activation(spread_o[:, :], v_bank[r][:, :], ACT.Copy).then_inc(b_drained[r], 1)
                    if what == "OT":
                        r, k = back_use(L, f"OT{u}", i, s)
                        act.wait_ge(turned, turn_at[n] + L["turns"] * s + u + 1 + 2 * L["turns"] * i)
                        c = BANK if L["dim"] == 64 else P
                        act.activation(oT[:, BANK * u:BANK * u + c], v_bank[r][:, 0:c], ACT.Copy).then_inc(b_drained[r], 1)
                    if what != "F":
                        return
                    r, k = place(front_at[n], L["front"], i, s, u)
                    bk = f_bank[r]
                    if u == 0 and n != "l3x":
                        act.wait_ge(f_full[r], k + 1)
                        if n == "l1x":
                            act.activation(yT[t][:, :], bk[:, 0:P], ACT.Identity, scale=vec["l1x_g1"], bias=vec["l1x_b1"])
                            act.activation(cT[t][:, :], bk[:, P:2 * P], ACT.Identity, scale=vec["l1x_g2"],
                                           bias=vec["l1x_b2"]).then_inc(f_drained[r], 1)
                        elif n == "l1f":
                            act.activation(yT[t][:, :], bk[:, 0:P], ACT.Copy, scale=vec["l1f_ln1"]).then_inc(f_drained[r], 1)
                        else:
                            act.activation(yT[t][:, :], bk[:, 0:P], ACT.Copy).then_inc(f_drained[r], 1)
                    if n == "l0x" and u in (1, 2):
                        act.wait_ge(f_full[r], k + 1)
                        act.activation((qT if u == 1 else kT)[t][:, 0:BANK], bk[:, :], ACT.Copy).then_inc(f_drained[r], 1)
                    if n == "l1x" and u == 1:
                        act.wait_ge(f_full[r], k + 1)
                        act.activation(qT[t][:, 0:BANK], bk[:, :], ACT.Identity, bias=ones_at).then_inc(f_drained[r], 1)
                    if n == "l1x" and u == 3:
                        act.wait_ge(f_full[r], k + 1)
                        act.activation(V8[t][:, :, 0:8], split(bk[:, 0:P], 16), ACT.Copy).then_inc(f_drained[r], 1)
                batches(act, n, do)

            def turned_stream(n, **how):
                for g in range(4):
                    r, k = front_use(n, g)
                    act.wait_ge(f_full[r], k + 1)
                    act.activation(YT[:, BANK * g:BANK * g + BANK], f_bank[r][:, :], ACT.Copy, **how).then_inc(f_drained[r], 1)

            def experts(M):
                n, H = M["name"], M["halves"]

                def chunk(i, s, c, last):
                    for h in range(H):
                        r, k = place(hid_at[n], CHUNKS * H, i, s, c * H + h)
                        act.wait_ge(g_full[r], k + 1)
                        if M["gated"]:
                            act.wait_ge(h_ready[r], k)
                            act.activation(act_sb[r][:, :], s_bank[r][:, :], ACT.Silu).then_inc(g_drained[r], 1)
                        else:
                            act.activation(hT[(c * H + h) % 4][:, :], s_bank[r][:, :], ACT.Gelu,
                                           bias=wset[s][:, 2 * P:2 * P + 1]).then_inc(h_ready[r], 1)
                sets(act, M, chunk)

            act.wait_ge(step("setup.angles"), 1)
            act.activation(tmpT[:, 2:4, :], tmpT[:, 0:2, :], ACT.Sin).then_inc(step("setup.sin"), 1)
            for g, dst in enumerate([PET[:, 0:3 * P], W3T[:, 0:BANK], W3T[:, BANK:2 * BANK], W3T[:, 2 * BANK:9 * P]]):
                r, k = front_use("setup", g)
                act.wait_ge(f_full[r], k + 1)
                act.activation(dst, f_bank[r][:, 0:dst.shape[1]], ACT.Copy).then_inc(f_drained[r], 1)
            attention(LAYERS[0])
            attention(LAYERS[1])
            turned_stream("l0m", scale=vec["gamma2"])
            act.wait_ge(step("l0m.logits"), 1)
            act.activation(ex[:, :, 0:31], lg[:, :, 0:31], ACT.Exp).then_inc(step("l0m.exp"), 1)
            for g in range(4):
                r, k = front_use("l0m", 5 + g)
                act.wait_ge(f_full[r], k + 1)
                act.activation(GT[:, BANK * g:BANK * g + BANK], f_bank[r][0:32, :], ACT.Copy).then_inc(f_drained[r], 1)
            experts(EXPERTS[0])
            attention(LAYERS[2])
            attention(LAYERS[3])
            turned_stream("l1m", scale=vec["l1f_ln2"])
            act.wait_ge(step("l1m.logits"), 1)
            act.activation(ex[:, :, 0:8], lg[:, :, 0:8], ACT.Exp).then_inc(step("l1m.exp"), 1)
            experts(EXPERTS[1])
            turned_stream("l2x")
            r, k = front_use("l2x", 4)
            act.wait_ge(f_full[r], k + 1)
            act.activation(csum[:, :], f_bank[r][:, 0:B], ACT.Copy, scale=1.0 / P).then_inc(f_drained[r], 1)
            turned_stream("l2m")
            r, k = front_use("l2m", 4)
            act.wait_ge(f_full[r], k + 1)
            act.activation(ex[:, :, :], split(f_bank[r][:, :], B), ACT.Sigmoid).then_inc(f_drained[r], 1)
            experts(EXPERTS[2])
            attention(LAYERS[4])

            act.wait_ge(step("l3m.scale"), 1)
            for g in range(4):
                r, k = front_use("l3m", g)
                act.wait_ge(f_full[r], k + 1)
                act.activation(YT[:, BANK * g:BANK * g + BANK], f_bank[r][:, :], ACT.Identity, scale=quant[:, 0, 3:4],
                               bias=magic).then_inc(f_drained[r], 1)
            for e in range(24):
                r, k = front_use("l3m", 4 + e)
                c, w, m = e // 6, e % 6 // 3, e % 3
                act.wait_ge(f_full[r], k + 1)
                act.activation((U3, G3)[w][:, m, BANK * c:BANK * c + BANK], f_bank[r][:, :], ACT.Copy).then_inc(f_drained[r], 1)
            Uf = U3[:, :, :].rearrange("p m t -> p (m t)")
            act.wait_ge(step("l3m.scale"), 3)
            for h in range(6):
                part = big[:, 1024 * h:1024 * h + 1024]
                act.activation(part, part, ACT.Identity, scale=quant[:, 2, 3:4], bias=magic).then_inc(step("l3m.g_round"), 1)
            for h in range(6):
                part = Uf[:, 1024 * h:1024 * h + 1024]
                act.activation(part, part, ACT.Identity, scale=quant[:, 1, 3:4], bias=magic).then_inc(step("l3m.u_round"), 1)
            for h in range(6):
                act.wait_ge(step("l3m.g"), h + 1)
                if h >= 2:
                    act.wait_ge(step("l3m.gs"), h - 1)
                act.activation(sig[h % 2][:, :], big[:, 1024 * h:1024 * h + 1024], ACT.Sigmoid).then_inc(step("l3m.sig"), 1)
            for stage in (3, 4):
                act.wait_ge(step("l3m.scale"), stage + 1)
                for h in range(6):
                    part = big[:, 1024 * h:1024 * h + 1024]
                    act.activation(part, part, ACT.Identity, scale=quant[:, stage, 3:4], bias=magic).then_inc(step(f"l3m.round{stage}"), 1)

        @block.tensor
        def _(pe_):
            def front_begin(n, c):
                r, k = front_use(n, c)
                pe_.wait_ge(f_drained[r], k)
                return f_bank[r], f_full[r]

            def attention(L):
                n, units, F, U = L["name"], L["units"], L["front"], L["units"]
                causal = n in ("l0f", "l1f")

                def drained(i, s, job):
                    r, k = place(front_at[n], F, i, s, job)
                    pe_.wait_ge(f_drained[r], k + 1)

                def roped(i, s, piece):
                    at, per = (0, 4) if n == "l0f" else (4 * B, 2)
                    r, k = place(at, per, i, s, piece)
                    pe_.wait_ge(rope_done[r], k + 1)

                def front_job(i, s, u):
                    t = s % 2
                    r, k = place(front_at[n], F, i, s, u)
                    pe_.wait_ge(f_drained[r], k)
                    bk = f_bank[r]

                    def product(cols, w, m, count, x):
                        for q in range(count):
                            last = pe_.matmul(bk[:, cols + P * q:cols + P * q + P], w[:, P * (m + q):P * (m + q) + P], x[:, :],
                                              start=True, stop=True)
                        return last

                    if u == 0:
                        if n == "l0f":
                            pe_.wait_ge(aux_ready[t], s // 2 + 1 + i)
                            last = pe_.transpose(bk[:, 0:P], y_aux[t][:, :], ident)
                        else:
                            pe_.wait_ge(y_ready[t], PAIRS * L["no"] + s // 2 + 1 + i)
                            last = pe_.transpose(bk[:, 0:P], y_tok[t][:, :], ident)
                            if n == "l1x":
                                last = pe_.transpose(bk[:, P:2 * P], y_aux[t][:, :], ident)
                    elif n == "l0x":
                        if u == 1:
                            drained(i, s, 0)
                            last = product(0, W0X[:, 0, :], 0, 4, yT[t])
                        if u == 2:
                            pe_.wait_ge(cT_ready[t], 16 * (s // 2 + 1) + 16 * i)
                            last = product(0, W0X[:, 1, :], 0, 4, cT[t])
                        if u == 3:
                            last = pe_.matmul(bk[:, :], cT[t][:, :], W0X[:, 2, :], start=True, stop=True)
                    elif n == "l0f":
                        if u == 1:
                            drained(i, s, 0)
                        if u < 9:
                            piece = (u - 1) // 2
                            w = w0f[["qa", "qb", "ka", "kb"][2 * (piece // 2) + (u - 1) % 2]]
                            last = product(0, w, 4 * (piece % 2), 4, yT[t])
                        else:
                            last = pe_.matmul(bk[:, :], yT[t][:, :], w0f["v"][:, BANK * (u - 9):BANK * (u - 9) + BANK], start=True, stop=True)
                    elif n == "l1x":
                        if u == 1:
                            drained(i, s, 0)
                            last = product(0, w1x["q"], 0, 4, yT[t])
                        if u == 2:
                            last = product(0, w1x["k"], 0, 4, cT[t])
                        if u == 3:
                            last = pe_.matmul(bk[:, 0:P], cT[t][:, :], w1x["v"], start=True, stop=True)
                    elif n == "l1f":
                        if u == 1:
                            drained(i, s, 0)
                        if u < 3:
                            last = product(0, w1f[("qa", "qb")[u - 1]], 0, 4, yT[t])
                        else:
                            product(0, w1f["ka"], 0, 1, yT[t])
                            product(P, w1f["kb"], 0, 1, yT[t])
                            last = pe_.matmul(bk[:, 2 * P:2 * P + 32], yT[t][:, :], w1f["v"], start=True, stop=True)
                    last.then_inc(f_full[r], 1)

                def uses_drained(i, s, uses):
                    last_of = {}
                    for c in sorted(uses):
                        r, k = place(back_at[n], len(L["back"]), i, s, c)
                        last_of[r] = k
                    for r, k in last_of.items():
                        pe_.wait_ge(b_drained[r], k + 1)

                def operands_ready(i, s, u):
                    if n in ("l0x", "l1x") and u == 0:
                        drained(i, s, 1)
                        drained(i, s, 2)
                    if n == "l0f" and u % 2 == 0:
                        roped(i, s, 2 + u // 2)
                    if n == "l1f" and u == 0:
                        roped(i, s, 0)
                        roped(i, s, 1)
                    if n == "l3x":
                        drained(i, s, 0)
                        pe_.wait_ge(k3_ready[s % 2], 2 * (s // 2) + 2 + 2 * i)

                def do(what, u, i, s):
                    slot = s % 2
                    if what == "F":
                        front_job(i, s, u)
                    if what in ("S", "T", "V"):
                        r, k = place(unit_at[n], units, i, s, u)
                    if what == "S":
                        pe_.wait_ge(shifted_ready[r], k)
                        operands_ready(i, s, u)
                        bk = s_bank[r]
                        if causal:
                            pe_.matmul(bk[:, :], ident_bf, causal_bf, start=True, stop=False, skip_group_check=True)
                        if n == "l3x":
                            pe_.matmul(bk[:, 0:2 * P], ident_bf, own_bf, start=True, stop=False, skip_group_check=True)
                            for m in range(2):
                                last = pe_.matmul(bk[:, P * m:P * m + P], qT[slot][:, P * m:P * m + P], kT[slot][:, P * m:P * m + P],
                                                  start=False, stop=True, skip_group_check=True)
                        else:
                            for m, (_, row, tq, tk, rows, _) in enumerate(heads_of(L, u)):
                                last = pe_.matmul(bk[:, P * m:P * m + P], qT[slot][row:row + rows, P * tq:P * tq + P],
                                                  kT[slot][row:row + rows, P * tk:P * tk + P],
                                                  start=not causal, stop=True, skip_group_check=causal)
                        last.then_inc(s_full[r], 1)
                    if what == "T":
                        pe_.wait_ge(probs_ready[r], k + 1)
                        pe_.wait_ge(probsT_ready[r], k)
                        for m in range(HEADS if units > 1 else 1):
                            last = pe_.transpose(t_bank[r][:, P * m:P * m + P], probs[r][:, P * m:P * m + P], ident)
                        last.then_inc(t_full[r], 1)
                    if what == "V":
                        pe_.wait_ge(probsT_ready[r], k + 1)
                        rb, kb = back_use(L, pv_use(L, u), i, s)
                        if L["dim"] == 64 or u == 0:
                            pe_.wait_ge(b_drained[rb], kb)
                        if n == "l0x" and u == 0:
                            drained(i, s, 3)
                        if n == "l0f" and u % 2 == 0:
                            drained(i, s, 9 + u // 2)
                        if n in ("l1x", "l1f") and u == 0:
                            drained(i, s, 3)
                        bk = v_bank[rb]
                        if n == "l3x":
                            pe_.wait_ge(v_dma[slot], 16 * (s // 2 + 1) + 16 * i)
                            last = pe_.matmul(bk[:, 0:P + 1], probsT[r][:, 0:P], V128[slot][:, :], start=True, stop=True)
                        else:
                            for m, (h, _, _, _, _, hv) in enumerate(heads_of(L, u)):
                                turned_probs = probsT[r][:, P * m:P * m + P]
                                if L["dim"] == 64:
                                    last = pe_.matmul(bk[:, 65 * m:65 * m + 65], turned_probs, V64[slot][:, hv, :], start=True, stop=True)
                                else:
                                    last = pe_.matmul(bk[32 * m:32 * m + 32, P * u:P * u + P], V8[slot][:, hv, :], turned_probs,
                                                      start=True, stop=True)
                        last.then_inc(pv_done[r], 1)
                    if what == "OB":
                        uses_drained(i, s, [0, -1])
                        rb, kb = back_use(L, "OB0", i, s)
                        for v in range(units):
                            last = pe_.transpose(v_bank[rb][:, P * v:P * v + P], spread_o[:, P * v:P * v + P], ident)
                        last.then_inc(regrouped, 1)
                    if what == "OT":
                        c = L["back"].index(f"OT{u}")
                        mine = [L["back"].index(v) for v in ((f"V{2 * u}", f"V{2 * u + 1}") if L["dim"] == 64 else ("OB0",))]
                        uses_drained(i, s, mine + [c - 2])
                        rb, kb = back_use(L, f"OT{u}", i, s)
                        for m in range(4 if L["dim"] == 64 else 1):
                            c = BANK * u + P * m
                            last = pe_.transpose(v_bank[rb][:, P * m:P * m + P], o_tok[slot][:, c:c + P], ident)
                        last.then_inc(turned, 1)
                    if what == "OP":
                        c = L["back"].index("OP0")
                        uses_drained(i, s, [L["back"].index(f"OT{v}") for v in range(L["turns"])] + [c - 2])
                        rb, kb = back_use(L, "OP0", i, s)
                        count = {"l0x": 4, "l0f": 8, "l1x": 1, "l1f": 1}[n]
                        w = {"l0x": W0X[:, 3, :], "l0f": w0f["o"], "l1x": w1x["o"], "l1f": w1f["o"]}[n]
                        for m in range(count):
                            last = pe_.matmul(v_bank[rb][:, 0:P], oT[:, P * m:P * m + P], w[:, P * m:P * m + P],
                                              start=(m == 0), stop=(m == count - 1 and n == "l1f"))
                        if n != "l1f":
                            last = pe_.matmul(v_bank[rb][:, 0:P], ones_row[:, :], bo[n], start=False, stop=True)
                        last.then_inc(projected, 1)
                batches(pe_, n, do)

            def turn_stream(n, src=None):
                for g in range(4):
                    bk, full = front_begin(n, g)
                    pe_.wait_ge(step(n + ".y"), g + 1)
                    for m in range(4):
                        last = pe_.transpose(bk[:, P * m:P * m + P], Y[:, 4 * g + m, :], ident)
                    last.then_inc(full, 1)

            def stream_turned(n):
                for c in range(4):
                    r, k = front_use(n, c)
                    pe_.wait_ge(f_drained[r], k + 1)

            def router(n, w):
                stream_turned(n)
                bk, full = front_begin(n, 4)
                for b in range(B):
                    last = pe_.matmul(bk[:, 32 * b:32 * b + w.shape[1]], YT[:, P * b:P * b + P], w, start=True, stop=True)
                last.then_inc(full, 1)

            def experts(M):
                n, H, downs = M["name"], M["halves"], M["downs"]

                def hidden(i, s, c):
                    if c == 0:
                        if n == "l2m":
                            pe_.wait_ge(w_cast[s], i + 1)
                        else:
                            pe_.wait_ge(w_loaded[s], 16 * (set_at[n] // 2 + i + 1))
                    x = YT[:, BANK * c:BANK * c + BANK]
                    for h in range(H):
                        r, k = place(hid_at[n], CHUNKS * H, i, s, c * H + h)
                        if M["gated"]:
                            pe_.wait_ge(g_drained[r], k - ungated // 2)
                        pe_.wait_ge(h_ready[r], k)
                        pe_.matmul(s_bank[r][:, :], wset[s][:, P * h:P * h + P], x, start=True, stop=True).then_inc(g_full[r], 1)
                        if M["gated"]:
                            up = (M["up"] // 2) + P * h
                            pe_.matmul(t_bank[r][:, :], wset[s][:, up:up + P], x, start=True, stop=True).then_inc(u_full[r], 1)

                def sums(i, s, c):
                    for h in range(H):
                        r, k = place(hid_at[n], CHUNKS * H, i, s, c * H + h)
                        pe_.wait_ge(h_ready[r], k + 1)
                    for d, (lo, hi) in enumerate(downs):
                        r, k = place(sum_at[n], CHUNKS * len(downs), i, s, c * len(downs) + d)
                        pe_.wait_ge(d_drained[r], k)
                        for q in range(4):
                            for h in range(H):
                                last = pe_.matmul(v_bank[r][:, P * q:P * q + P], hT[(c * H + h) % 4][lo:hi, P * q:P * q + P],
                                                  wset[s][lo:hi, (M["up"] + P * h):(M["up"] + P * h) + P],
                                                  start=(h == 0), stop=(h == H - 1))
                        last.then_inc(d_full[r], 1)

                def chunk(i, s, c, last):
                    if not last:
                        hidden(*after(i, s, c))
                    sums(i, s, c)

                hidden(0, 0, 0)
                sets(pe_, M, chunk)

            pe_.wait_ge(in_c, 16 * 4)
            pe_.wait_ge(step("setup.hot"), 1)
            bk, full = front_begin("setup", 0)
            pe_.matmul(bk[:, 0:3 * P], pe, HOT[:, :, :].rearrange("p m s -> p (m s)"), start=True, stop=True).then_inc(full, 1)
            pe_.wait_ge(step("setup.w3"), 1)
            for g in range(3):
                bk, full = front_begin("setup", 1 + g)
                for m in range(4 * g, min(4 * g + 4, 9)):
                    last = pe_.transpose(bk[:, P * (m - 4 * g):P * (m - 4 * g) + P], W3N[:, P * m:P * m + P], ident)
                last.then_inc(full, 1)
            pe_.wait_ge(in_w0x, 16)
            pe_.wait_ge(step("setup.ones"), 1)
            attention(LAYERS[0])
            pe_.wait_ge(in_w0f, 16)
            attention(LAYERS[1])
            turn_stream("l0m")
            pe_.wait_ge(in_l3, 16 * 10)
            router("l0m", RW[:, 0:31])
            pe_.wait_ge(step("l0m.gates"), 1)
            for g in range(4):
                bk, full = front_begin("l0m", 5 + g)
                for m in range(4):
                    last = pe_.transpose(bk[0:32, P * m:P * m + P], GATES[:, 4 * g + m, 0:32], ident)
                last.then_inc(full, 1)
            for g in range(4):
                r, k = front_use("l0m", 5 + g)
                pe_.wait_ge(f_drained[r], k + 1)
            for g in range(4):
                bk, full = front_begin("l0m", 9 + g)
                for m in range(4):
                    b = 4 * g + m
                    last = pe_.matmul(bk[:, P * m:P * m + P], GT[:, P * b:P * b + P], B2[:, :], start=True, stop=True)
                last.then_inc(full, 1)
            experts(EXPERTS[0])
            pe_.wait_ge(in_w1, 16 * 3)
            attention(LAYERS[2])
            attention(LAYERS[3])
            turn_stream("l1m")
            router("l1m", RW[:, 31:39])
            experts(EXPERTS[1])

            turn_stream("l2x")
            bk, full = front_begin("l2x", 4)
            for b in range(B):
                last = pe_.matmul(bk[:, b:b + 1], CTX[:, b, :], part_one, start=True, stop=True)
            last.then_inc(full, 1)
            stream_turned("l2x")
            r, k = front_use("l2x", 4)
            pe_.wait_ge(f_drained[r], k + 1)
            for g in range(4):
                bk, full = front_begin("l2x", 5 + g)
                for m in range(4):
                    b = 4 * g + m
                    dst = bk[:, P * m:P * m + P]
                    pe_.matmul(dst, YT[:, P * b:P * b + P], WL2[:, 0:P], start=True, stop=False)
                    pe_.matmul(dst, csum[:, b:b + 1].to_broadcast([P, P]), WL2[:, P:2 * P], start=False, stop=False)
                    last = pe_.matmul(dst, ones_row[:, :], bo["l2x"], start=False, stop=True)
                last.then_inc(full, 1)

            turn_stream("l2m")
            router("l2m", RW[:, 39:71])
            pe_.wait_ge(step("l2m.run"), 1)
            bk, full = front_begin("l2m", 5)
            pe_.matmul(bk[:, :], before, sel[:, :, :].rearrange("p b e -> p (b e)"), start=True, stop=False)
            pe_.matmul(bk[:, :], ones_sq, run[0][:, :, :].rearrange("p b e -> p (b e)"), start=False, stop=True).then_inc(full, 1)
            experts(EXPERTS[2])
            attention(LAYERS[4])

            turn_stream("l3m")
            for c in range(4):
                pe_.wait_ge(step("l3m.yq"), c + 1)
                for e in range(6):
                    w, m = e // 3, e % 3
                    bk, full = front_begin("l3m", 4 + 6 * c + e)
                    wt = W3T[:, P * (3 * (1 - w) + m):P * (3 * (1 - w) + m) + P]
                    pe_.matmul(bk[:, :], wt, YT[:, BANK * c:BANK * c + BANK], start=True, stop=True).then_inc(full, 1)
            pe_.wait_ge(step("l3m.o"), 6)
            for g in range(4):
                bk, full = front_begin("l3m", 28 + g)
                for q in range(4):
                    b = 4 * g + q
                    for m in range(3):
                        last = pe_.matmul(bk[:, P * q:P * q + P], G3[:, m, P * b:P * b + P], W3T[:, P * (6 + m):P * (6 + m) + P],
                                          start=(m == 0), stop=(m == 2))
                last.then_inc(full, 1)

        @block.vector
        def _(dve):
            links = [0]

            def link(ins):
                links[0] += 1
                ins.then_inc(dve_chain, 1)
                dve.wait_ge(dve_chain, links[0])

            def moments(src):
                for b in range(B):
                    last = dve.bn_stats(st[:, b, :], src[:, b, :])
                link(last)
                dve.tensor_tensor(t0, st[:, :, 1], st[:, :, 4], ALU.add)
                dve.tensor_tensor(t1, st[:, :, 1], st[:, :, 4], ALU.subtract)
                link(dve.tensor_tensor(ms, st[:, :, 2], st[:, :, 5], ALU.add))
                dve.tensor_scalar(mean, t0, 0.5, None, ALU.mult)
                link(dve.tensor_tensor(srow2, t1, t1, ALU.mult))
                link(dve.scalar_tensor_tensor(var, srow2, 32.0, ms, ALU.mult, ALU.add))

            def powered(name):
                dve.wait_ge(step(name + "_pow"), 1)

            def layer_norm_stats(name, src):
                moments(src)
                dve.tensor_scalar(ve, var, 1.0 / P, EPS, ALU.mult, ALU.add).then_inc(step(name), 1)
                powered(name)

            def again_stats(name):
                link(dve.tensor_tensor(t0, r1, r1, ALU.mult))
                link(dve.tensor_tensor(t0, t0, var, ALU.mult))
                link(dve.tensor_scalar(t0, t0, 1.0 / P, EPS, ALU.mult, ALU.add))
                dve.sem_inc(step(name), 1)
                powered(name)
                link(dve.tensor_tensor(r12, r1, t1, ALU.mult))

            def rms_stats(name, src):
                moments(src)
                link(dve.tensor_tensor(t0, mean, mean, ALU.mult))
                link(dve.scalar_tensor_tensor(t0, var, 1.0 / P, t0, ALU.mult, ALU.add))
                dve.tensor_scalar(ve, t0, EPS, None, ALU.add).then_inc(step(name), 1)
                powered(name)

            def normalise(n, src, centred):
                for g in range(4):
                    for b in range(4 * g, 4 * g + 4):
                        if centred:
                            last = dve.tensor_scalar(Y[:, b, :], src[:, b, :], mean[:, b:b + 1], r1[:, b:b + 1], ALU.subtract, ALU.mult)
                        else:
                            last = dve.tensor_scalar(Y[:, b, :], src[:, b, :], r1[:, b:b + 1], None, ALU.mult)
                    last.then_inc(step(n + ".y"), 1)

            def batches_done(L):
                for c in (-2, -1):
                    r, k = place(back_at[L["name"]] + len(L["back"]) * B, 0, 0, 0, c)
                    dve.wait_ge(b_drained[r], k + 1)

            def sets_done(M):
                for d in range(2):
                    total = sum_at[M["name"]] + M["steps"] * CHUNKS * len(M["downs"]) - 1 - d
                    dve.wait_ge(d_drained[total % 2], total // 2 + 2)

            def attention(L):
                n, units = L["name"], L["units"]

                def do(what, u, i, s):
                    b, slot = 2 * i + s, s % 2
                    if what == "Y":
                        last = dve.tensor_scalar(y_tok[slot][:, :], tile(X, b), col(mean, b),
                                                 col(r12 if n in ("l0f", "l1x", "l1f") else r1, b), ALU.subtract, ALU.mult)
                        if n == "l1x":
                            last = dve.tensor_scalar(y_aux[slot][:, :], tile(CTX, b), col(cstat[:, 0, :], b),
                                                     col(cstat[:, 1, :], b), ALU.subtract, ALU.mult)
                        if n == "l1f":
                            last = dve.tensor_scalar(tile(AO, b), tile(X, b), col(mean, b), col(r1, b), ALU.subtract, ALU.mult)
                        last.then_inc(y_ready[slot], 1)
                        if n == "l0f":
                            dve.wait_ge(y_ready[slot], PAIRS * L["no"] + s // 2 + 1 + i)
                            dve.tensor_tensor(tile(AO, b), y_tok[slot][:, :], gamma1_row, ALU.mult)
                    if what == "F":
                        front_job(i, s, u, b)
                    if what in ("S", "V"):
                        r, k = place(unit_at[n], units, i, s, u)
                    if what == "S":
                        src = split(s_bank[r][:, :], HEADS)
                        heads = HEADS
                        dve.wait_ge(s_full[r], k + 1)
                        if n == "l3x":
                            k3 = place(0, 1, i, s, 0)[1]
                            heads = 1
                            dve.tensor_copy(joined[r][:, :], s_bank[r][:, P:2 * P]).then_inc(grouped_ready[r], 1)
                            dve.wait_ge(grouped_ready[r], k3 + 1)
                            dve.tensor_tensor(joined[r][:, :], s_bank[r][:, 0:P], joined[r][:, :], ALU.max).then_inc(joined_ready[r], 1)
                            dve.wait_ge(joined_ready[r], k3 + 1)
                            src = split(joined[r][:, :], 1)
                        dve.tensor_reduce(row_max[r][:, 0:heads], src, AX_X, ALU.max).then_inc(max_ready[r], 1)
                        dve.wait_ge(max_ready[r], k + 1)
                        dve.wait_ge(probs_ready[r], k)
                        dve.tensor_tensor(split(shifted[r][:, 0:P * heads], heads), src, wide(row_max[r][:, 0:heads], heads, P),
                                          ALU.subtract).then_inc(shifted_ready[r], 1)
                    if what == "V" and L["dim"] != 8:
                        dve.wait_ge(pv_done[r], k + 1)
                        rb, kb = back_use(L, pv_use(L, u), i, s)
                        kr = recips_at[n] + ((units * s + u) // 2 + 1 + units * i if L["dim"] == 64 else s // 2 + 1 + i)
                        rr = r if L["dim"] == 64 else slot
                        bk = v_bank[rb]
                        if L["dim"] == 64:
                            o = split(bk[:, 0:260], HEADS)
                            dve.reciprocal(recips[rr][:, 0:HEADS], o[:, :, 64]).then_inc(recip_ready[rr], 1)
                            dve.wait_ge(recip_ready[rr], kr)
                            h0 = 8 * (u // 2) + u % 2
                            dst = o_tok[slot][:, :].rearrange("p (h d) -> p h d", d=64)[:, h0:h0 + 7:2, :]
                            dve.tensor_tensor(dst, o[:, :, 0:64], wide(recips[rr][:, 0:HEADS], HEADS, 64), ALU.mult).then_inc(b_drained[rb], 1)
                        else:
                            dve.reciprocal(recips[rr][:, 0:1], bk[:, P:P + 1]).then_inc(recip_ready[rr], 1)
                            dve.wait_ge(recip_ready[rr], kr)
                            dve.scalar_tensor_tensor(tile(X, b), bk[:, 0:P], recips[rr][:, 0:1], tile(X, b), ALU.mult, ALU.add)\
                                .then_inc(b_drained[rb], 1)
                    if what == "OB":
                        rb, kb = back_use(L, "OB0", i, s)
                        dve.wait_ge(regrouped, regrouped_at[n] + s + 1 + 2 * i)
                        o = split(v_bank[rb][:, :], 16)
                        dve.reciprocal(recips[slot][:, :], o[:, :, 8]).then_inc(recip_ready[slot], 1)
                        dve.wait_ge(recip_ready[slot], recips_at[n] + s // 2 + 1 + i)
                        dst = split(o_tok[slot][:, 0:P], 16)
                        by = wide(recips[slot][:, :], 16, 8)
                        if n == "l1x":
                            dve.scalar_tensor_tensor(dst, o[:, :, 0:8], col(NANF, b), by, ALU.mult, ALU.mult).then_inc(b_drained[rb], 1)
                        else:
                            dve.tensor_tensor(dst, o[:, :, 0:8], by, ALU.mult).then_inc(b_drained[rb], 1)
                    if what == "OP":
                        rb, kb = back_use(L, "OP0", i, s)
                        dve.wait_ge(projected, proj_at[n] + s + 1 + 2 * i)
                        if n in ("l0x", "l1x"):
                            dve.tensor_tensor(tile(X, b), v_bank[rb][:, 0:P], tile(X, b), ALU.add).then_inc(b_drained[rb], 1)
                        else:
                            dve.tensor_tensor(tile(AO, b), v_bank[rb][:, 0:P], tile(AO, b), ALU.add).then_inc(b_drained[rb], 1)

                def front_job(i, s, u, b):
                    t = s % 2
                    r, k = place(front_at[n], L["front"], i, s, u)
                    bk = f_bank[r]
                    four = split(bk[:, :], 4)
                    if n == "l0x" and u == 3:
                        dve.wait_ge(f_full[r], k + 1)
                        dve.tensor_copy(V64[t][:, 0:8, 0:64], split(bk[:, :], 8)).then_inc(f_drained[r], 1)
                    if n == "l0f" and 1 <= u <= 8 or n == "l1f" and u in (1, 2):
                        piece = (u - 1) // 2
                        at, per = (0, 4) if n == "l0f" else (4 * B, 2)
                        q, kq = place(at, per, i, s, piece)
                        dve.wait_ge(f_full[r], k + 1)
                        dve.wait_ge(rope_done[q], kq)
                        odd = (u - 1) % 2
                        table = (sin0 if odd else cos0) if n == "l0f" else (sin1 if odd else cos1)
                        dve.tensor_tensor(split((rope_b if odd else rope_a)[q][:, :], 4), four, over(table, 4), ALU.mult).then_inc(f_drained[r], 1)
                    if n == "l0f" and u >= 9:
                        h0 = 8 * (u - 9)
                        dve.wait_ge(f_full[r], k + 1)
                        dve.tensor_tensor(V64[t][:, h0:h0 + 8, 0:64], split(bk[:, :], 8), split(VB[:, BANK * (u - 9):BANK * (u - 9) + BANK], 8),
                                          ALU.add).then_inc(f_drained[r], 1)
                    if n == "l1x" and u == 2:
                        dve.wait_ge(f_full[r], k + 1)
                        dve.scalar_tensor_tensor(split(kT[t][:, 0:BANK], 4), tile(MASK, b).unsqueeze(1).to_broadcast([P, 4, P]), ones_at,
                                                 four, ALU.mult, ALU.add).then_inc(f_drained[r], 1)
                    if n == "l1f" and u == 3:
                        q, kq = place(4 * B, 2, i, s, 1)
                        dve.wait_ge(f_full[r], k + 1)
                        dve.wait_ge(rope_done[q], kq)
                        dve.tensor_tensor(rope_a[q][:, 0:P], bk[:, 0:P], cos1, ALU.mult)
                        dve.tensor_tensor(rope_b[q][:, 0:P], bk[:, P:2 * P], sin1, ALU.mult)
                        dve.tensor_copy(V8[t][:, 0:4, 0:8], split(bk[:, 2 * P:2 * P + 32], 4)).then_inc(f_drained[r], 1)
                    if n == "l3x":
                        dve.wait_ge(f_full[r], k + 1)
                        dve.tensor_tensor(qT[t][:, 0:P], bk[:, 0:P], PET[:, 0:P], ALU.add)
                        dve.tensor_tensor(qT[t][:, P:2 * P], bk[:, 0:P], PET[:, P:2 * P], ALU.add).then_inc(f_drained[r], 1)
                batches(dve, n, do)

            def top(n, k, E):
                for b in range(B):
                    last = dve.max(top8[:, b, :], ex[:, b, 0:E])
                link(last)
                for b in range(B):
                    last = dve.max_index(idx8[:, b, :], top8[:, b, :], ex[:, b, 0:E])
                link(last)
                link(dve.tensor_copy(idxf[:, :, :], idx8[:, :, :]))
                iota = iota_row[:, 0:E].unsqueeze(1).unsqueeze(1).to_broadcast([P, B, k, E])
                link(dve.tensor_tensor(hits[:, :, 0:k, 0:E], iota, idxf[:, :, 0:k].unsqueeze(3).to_broadcast([P, B, k, E]), ALU.is_equal))
                link(dve.tensor_reduce(sel[:, :, 0:E], hits[:, :, 0:k, 0:E].rearrange("p b k e -> p b e k"), AX_X, ALU.add))

            def row_scale(dst, src, by, E):
                return dve.tensor_tensor(dst, src, wide(by, B, E), ALU.mult)

            def softmax_gates(n, E, k, bias, exact):
                r, kk = front_use(n, 4)
                dve.wait_ge(f_full[r], kk + 1)
                logits = split(f_bank[r][:, :], B)[:, :, 0:E]
                if bias is not None:
                    link(dve.tensor_tensor(lg[:, :, 0:E], logits, over(bias, B), ALU.add))
                else:
                    link(dve.tensor_copy(lg[:, :, 0:E], logits))
                dve.sem_inc(f_drained[r], 1)
                link(dve.tensor_reduce(srow0, lg[:, :, 0:E], AX_X, ALU.max))
                dve.tensor_tensor(lg[:, :, 0:E], lg[:, :, 0:E], wide(srow0, B, E), ALU.subtract).then_inc(step(n + ".logits"), 1)
                dve.wait_ge(step(n + ".exp"), 1)
                link(dve.tensor_reduce(srow0, ex[:, :, 0:E], AX_X, ALU.add))
                link(dve.reciprocal(srow1, srow0))
                link(row_scale(ex[:, :, 0:E], ex[:, :, 0:E], srow1, E))
                top(n, k, max(E, 8) + (E == 31))
                if exact:
                    link(dve.tensor_tensor(lg[:, :, 0:E], ex[:, :, 0:E], sel[:, :, 0:E], ALU.mult))
                    link(dve.tensor_reduce(srow0, lg[:, :, 0:E], AX_X, ALU.add))
                    link(dve.reciprocal(srow1, srow0))
                    link(row_scale(GATES[:, :, 0:E], lg[:, :, 0:E], srow1, E))
                else:
                    link(dve.tensor_tensor(GATES[:, :, 0:E], ex[:, :, 0:E], sel[:, :, 0:E], ALU.mult))
                dve.sem_inc(step(n + ".gates"), 1)

            def experts(M):
                n, H, downs = M["name"], M["halves"], M["downs"]
                nD = len(downs)

                def hidden(i, s, c):
                    if not M["gated"]:
                        return
                    for h in range(H):
                        r, k = place(hid_at[n], CHUNKS * H, i, s, c * H + h)
                        dve.wait_ge(g_drained[r], k - ungated // 2 + 1)
                        dve.wait_ge(u_full[r], k - ungated // 2 + 1)
                        dve.tensor_tensor(hT[(c * H + h) % 4][:, :], t_bank[r][:, :], act_sb[r][:, :], ALU.mult).then_inc(h_ready[r], 1)

                def chunk(i, s, c, last):
                    if not last:
                        hidden(*after(i, s, c))
                    for d in range(nD):
                        r, k = place(sum_at[n], CHUNKS * nD, i, s, c * nD + d)
                        dve.wait_ge(d_full[r], k + 1)
                        if d:
                            r0, k0 = place(sum_at[n], CHUNKS * nD, i, s, c * nD + d - 1)
                            dve.wait_ge(d_drained[r0], k0 + 1)
                        gate = nD * (2 * i + s) + d
                        for q in range(4):
                            tok = 4 * c + q
                            ins = dve.scalar_tensor_tensor(X[:, tok, :], v_bank[r][:, P * q:P * q + P], GATES[:, tok, bass.ds(gate, 1)],
                                                           X[:, tok, :], ALU.mult, ALU.add)
                        ins.then_inc(d_drained[r], 1)
                    if n == "l2m" and c == 0 and not last_set(i, s):
                        cast(i + s, 1 - s)

                def last_set(i, s):
                    return isinstance(i, int) and 2 * i + s == M["steps"] - 1

                def cast(i, s):
                    dve.wait_ge(w_loaded[s], 16 * (set_at[n] // 2 + i + 1))
                    dve.tensor_copy(wset[s][:, 0:M["wcols"]], wraw[s][:, 0:M["wcols"]]).then_inc(w_cast[s], 1)

                if n == "l2m":
                    cast(0, 0)
                hidden(0, 0, 0)
                sets(dve, M, chunk)

            dve.wait_ge(in_ctx, 16)
            layer_norm_stats("ctx.stats", CTX)
            dve.tensor_copy(cstat[:, 0, :], mean)
            link(dve.tensor_copy(cstat[:, 1, :], r1))
            dve.wait_ge(in_c, 16 * 4)
            dve.wait_ge(in_l3, 16 * 10)
            link(dve.tensor_scalar(POSG[:, :], POSI[:, :], 4, None, ALU.arith_shift_right))
            dve.tensor_copy(POSF[:, 0, :], POSI[:, :])
            link(dve.tensor_copy(POSF[:, 2, :], POSG[:, :]))
            link(dve.tensor_scalar(POSF[:, 1, :], POSF[:, 2, :], 60.0, None, ALU.add))
            link(dve.tensor_scalar(POSF[:, :, :], POSF[:, :, :], 0.0, P - 1.0, ALU.max, ALU.min))
            dve.tensor_scalar(HOT[:, :, :], POSF[:, :, :], part_no, None, ALU.is_equal).then_inc(step("setup.hot"), 1)
            w3 = W3N[:, :].rearrange("p (n m) -> p n m", m=32)
            link(dve.tensor_reduce(W3M[:, :], w3, AX_X, ALU.max, apply_absolute_value=True))
            link(dve.tensor_scalar(W3S[:, :], W3M[:, :], 1.0 / 7.0, 1e-12, ALU.mult, ALU.max))
            link(dve.reciprocal(W3R[:, :], W3S[:, :]))
            link(dve.tensor_tensor(w3, w3, wide(W3R[:, :], 36, 32), ALU.mult))
            link(dve.tensor_scalar(W3N[:, :], W3N[:, :], MAGIC, None, ALU.add))
            link(dve.tensor_scalar(W3N[:, :], W3N[:, :], MAGIC, 7.0, ALU.subtract, ALU.min))
            link(dve.tensor_scalar(W3N[:, :], W3N[:, :], -8.0, None, ALU.max))
            dve.tensor_tensor(w3, w3, wide(W3S[:, :], 36, 32), ALU.mult).then_inc(step("setup.w3"), 1)
            maskf = MASK[:, :, :].rearrange("p b s -> p (b s)")
            link(dve.tensor_copy(maskf, MASKU[:, :]))
            link(dve.tensor_reduce(NANF[:, :], MASK[:, :, :], AX_X, ALU.max))
            link(dve.reciprocal(srow0, NANF[:, :]))
            link(dve.tensor_tensor(NANF[:, :], NANF[:, :], srow0, ALU.mult))
            link(dve.tensor_scalar(maskf, maskf, -1.0, -NEG, ALU.add, ALU.mult))
            dve.tensor_copy(RW[:, 39:71], RWB[:, :])
            turns = [6.28125, 1.9340515136718750e-3, 1.2556659146e-6]
            link(dve.tensor_scalar(tmpT[:, 2, :], iota_row, vec["theta"], None, ALU.mult))
            for c, quarter in ((0, 0.0), (1, 0.25)):
                link(dve.tensor_scalar(tmpT[:, 3, :], tmpT[:, 2, :], 1.0 / (2.0 * math.pi), quarter, ALU.mult, ALU.add))
                link(dve.tensor_scalar(tmpT[:, 3, :], tmpT[:, 3, :], MAGIC, MAGIC, ALU.add, ALU.subtract))
                link(dve.scalar_tensor_tensor(tmpT[:, c, :], tmpT[:, 3, :], -turns[0], tmpT[:, 2, :], ALU.mult, ALU.add))
                link(dve.scalar_tensor_tensor(tmpT[:, c, :], tmpT[:, 3, :], -turns[1], tmpT[:, c, :], ALU.mult, ALU.add))
                link(dve.scalar_tensor_tensor(tmpT[:, c, :], tmpT[:, 3, :], -turns[2], tmpT[:, c, :], ALU.mult, ALU.add))
            link(dve.tensor_scalar(tmpT[:, 1, :], tmpT[:, 1, :], math.pi / 2, None, ALU.add))
            dve.tensor_scalar(tmpT[:, 0:2, :], tmpT[:, 0:2, :], 3.1415925, -3.1415925, ALU.min, ALU.max).then_inc(step("setup.angles"), 1)
            dve.wait_ge(step("setup.sin"), 1)
            link(dve.tensor_scalar(sin0, tmpT[:, 2, :], sin_sign, None, ALU.mult))
            link(dve.tensor_copy(cos0, tmpT[:, 3, :]))
            for dst, ba, bb in ((tbq, qb_a, qb_b), (tbk, kb_a, kb_b)):
                for m in range(8):
                    last = dve.tensor_scalar(dst[:, P * m:P * m + P], cos0, ba[:, m:m + 1], None, ALU.mult)
                link(last)
                for m in range(8):
                    last = dve.scalar_tensor_tensor(dst[:, P * m:P * m + P], sin0, bb[:, m:m + 1], dst[:, P * m:P * m + P], ALU.mult, ALU.add)
                link(last)
            dve.sem_inc(step("setup.tables"), 1)

            dve.wait_ge(in_x, 16)
            layer_norm_stats("l0x.stats", X)
            attention(LAYERS[0])
            batches_done(LAYERS[0])
            layer_norm_stats("l0f.stats", X)
            again_stats("l0f.stats2")
            attention(LAYERS[1])
            batches_done(LAYERS[1])

            rms_stats("l0m.stats", AO)
            normalise("l0m", AO, False)
            for g in range(4):
                r, k = front_use("l0m", g)
                dve.wait_ge(f_full[r], k + 1)
                dve.tensor_tensor(Y[:, 4 * g:4 * g + 4, :], Y[:, 4 * g:4 * g + 4, :], over(gamma2_row, 4), ALU.mult).then_inc(step("l0m.an"), 1)
            softmax_gates("l0m", 31, 3, RB[:, :], False)
            dve.wait_ge(step("l0m.x_ready"), 1)
            for g in range(4):
                r, k = front_use("l0m", 9 + g)
                dve.wait_ge(f_full[r], k + 1)
                last = dve.tensor_tensor(X[:, 4 * g:4 * g + 4, :], split(f_bank[r][:, :], 4), X[:, 4 * g:4 * g + 4, :], ALU.add)
                last.then_inc(f_drained[r], 1)
                dve.wait_ge(f_drained[r], k + 1)
            experts(EXPERTS[0])
            sets_done(EXPERTS[0])

            layer_norm_stats("l1x.stats", X)
            again_stats("l1x.stats2")
            attention(LAYERS[2])
            batches_done(LAYERS[2])
            layer_norm_stats("l1f.stats", X)
            again_stats("l1f.stats2")
            attention(LAYERS[3])
            batches_done(LAYERS[3])
            rms_stats("l1m.stats", AO)
            normalise("l1m", AO, False)
            softmax_gates("l1m", 8, 2, None, True)
            dve.wait_ge(step("l1m.x_ready"), 1)
            experts(EXPERTS[1])
            sets_done(EXPERTS[1])

            layer_norm_stats("l2x.stats", X)
            normalise("l2x", X, True)
            for g in range(4):
                r, k = front_use("l2x", 5 + g)
                dve.wait_ge(f_full[r], k + 1)
                dve.tensor_tensor(X[:, 4 * g:4 * g + 4, :], split(f_bank[r][:, :], 4), X[:, 4 * g:4 * g + 4, :], ALU.add)\
                    .then_inc(f_drained[r], 1)
                dve.wait_ge(f_drained[r], k + 1)
            layer_norm_stats("l2m.stats", X)
            normalise("l2m", X, True)
            r, k = front_use("l2m", 4)
            dve.wait_ge(f_drained[r], k + 1)
            link(dve.tensor_copy(lg[:, :, :], ex[:, :, :]))
            link(dve.tensor_tensor(ex[:, :, :], ex[:, :, :], over(LB[:, :], B), ALU.add))
            top("l2m", 4, 32)
            link(dve.memset(run[0][:, 0:1, :], 0.0))
            link(dve.tensor_copy(run[0][:, 1:B, :], sel[:, 0:B - 1, :]))
            src = 0
            for hop in (1, 2, 4, 8):
                dve.tensor_copy(run[1 - src][:, 0:hop, :], run[src][:, 0:hop, :])
                link(dve.tensor_tensor(run[1 - src][:, hop:B, :], run[src][:, hop:B, :], run[src][:, 0:B - hop, :], ALU.add))
                src = 1 - src
            dve.sem_inc(step("l2m.run"), 1)
            link(dve.tensor_tensor(lg[:, :, :], lg[:, :, :], sel[:, :, :], ALU.mult))
            link(dve.tensor_reduce(srow0, lg[:, :, :], AX_X, ALU.add))
            link(dve.tensor_scalar(srow0, srow0, 1e-12, None, ALU.max))
            link(dve.reciprocal(srow1, srow0))
            link(row_scale(lg[:, :, :], lg[:, :, :], srow1, 32))
            r, k = front_use("l2m", 5)
            dve.wait_ge(f_full[r], k + 1)
            link(dve.tensor_scalar(ex[:, :, :], split(f_bank[r][:, :], B), float(CAPACITY), None, ALU.is_lt))
            dve.sem_inc(f_drained[r], 1)
            link(dve.tensor_tensor(GATES[:, :, 0:32], lg[:, :, :], ex[:, :, :], ALU.mult))
            experts(EXPERTS[2])
            sets_done(EXPERTS[2])

            layer_norm_stats("l3x.stats", X)
            dve.sem_inc(step("l3x.begin"), 1)
            attention(LAYERS[4])
            batches_done(LAYERS[4])

            layer_norm_stats("l3m.stats", X)
            normalise("l3m", X, True)
            dve.wait_ge(step("l3m.y"), 4)

            def scale(n, waits):
                dve.wait_ge(step("l3m.all_max"), waits)
                link(dve.tensor_scalar(quant[:, n, 2:3], quant[:, n, 1:2], 1.0 / QMAX, 1e-12, ALU.mult, ALU.max))
                dve.reciprocal(quant[:, n, 3:4], quant[:, n, 2:3]).then_inc(step("l3m.scale"), 1)

            def largest(dst, src):
                return dve.tensor_reduce(dst, src, AX_X, ALU.max, apply_absolute_value=True)

            largest(quant[:, 0, 0:1], Y[:, :, :].rearrange("p b d -> p (b d)")).then_inc(step("l3m.part_max"), 1)
            scale(0, 1)
            for g in range(4):
                r, k = front_use("l3m", g)
                dve.wait_ge(f_drained[r], k + 1)
                part = YT[:, BANK * g:BANK * g + BANK]
                dve.tensor_scalar(part, part, MAGIC, quant[:, 0, 2:3], ALU.subtract, ALU.mult).then_inc(step("l3m.yq"), 1)
            for e in range(24):
                r, k = front_use("l3m", 4 + e)
                c, w, m = e // 6, e % 6 // 3, e % 3
                dve.wait_ge(f_drained[r], k + 1)
                last = largest(part_max[:, 12 * w + 3 * c + m:12 * w + 3 * c + m + 1], (U3, G3)[w][:, m, BANK * c:BANK * c + BANK])
            link(last)
            link(largest(quant[:, 1, 0:1], part_max[:, 0:12]))
            largest(quant[:, 2, 0:1], part_max[:, 12:24]).then_inc(step("l3m.part_max"), 1)
            scale(1, 2)
            scale(2, 3)
            for h in range(6):
                part = big[:, 1024 * h:1024 * h + 1024]
                dve.wait_ge(step("l3m.g_round"), h + 1)
                dve.tensor_scalar(part, part, MAGIC, quant[:, 2, 2:3], ALU.subtract, ALU.mult).then_inc(step("l3m.g"), 1)
            for h in range(6):
                part, sg = big[:, 1024 * h:1024 * h + 1024], sig[h % 2][:, :]
                dve.wait_ge(step("l3m.sig"), h + 1)
                link(dve.tensor_scalar(sg, sg, 65536.0, MAGIC, ALU.mult, ALU.add))
                link(dve.tensor_scalar(sg, sg, MAGIC, 65535.0, ALU.subtract, ALU.min))
                dve.scalar_tensor_tensor(part, sg, 1.0 / 65536.0, part, ALU.mult, ALU.mult).then_inc(step("l3m.gs"), 1)
                dve.wait_ge(step("l3m.gs"), h + 1)
                last = largest(part_max[:, h:h + 1], part)
            link(last)
            largest(quant[:, 3, 0:1], part_max[:, 0:6]).then_inc(step("l3m.part_max"), 1)
            scale(3, 4)
            for h in range(6):
                part = big[:, 1024 * h:1024 * h + 1024]
                dve.wait_ge(step("l3m.round3"), h + 1)
                dve.wait_ge(step("l3m.u"), h + 1)
                link(dve.tensor_scalar(part, part, MAGIC, quant[:, 3, 2:3], ALU.subtract, ALU.mult))
                link(dve.tensor_tensor(part, part, U3[:, :, :].rearrange("p m t -> p (m t)")[:, 1024 * h:1024 * h + 1024], ALU.mult))
                last = largest(part_max[:, h:h + 1], part)
            link(last)
            largest(quant[:, 4, 0:1], part_max[:, 0:6]).then_inc(step("l3m.part_max"), 1)
            scale(4, 5)
            for h in range(6):
                part = big[:, 1024 * h:1024 * h + 1024]
                dve.wait_ge(step("l3m.round4"), h + 1)
                dve.tensor_scalar(part, part, MAGIC, quant[:, 4, 2:3], ALU.subtract, ALU.mult).then_inc(step("l3m.o"), 1)
            for g in range(4):
                r, k = front_use("l3m", 28 + g)
                dve.wait_ge(f_full[r], k + 1)
                dve.tensor_tensor(X[:, 4 * g:4 * g + 4, :], split(f_bank[r][:, :], 4), X[:, 4 * g:4 * g + 4, :], ALU.add)\
                    .then_inc(f_drained[r], 1)


def _layout(v):
    import numpy as np

    f = np.float32
    bf = v["L2_ffn_W1"].dtype
    D = P
    A = {}

    def arr(name):
        return np.asarray(v[name])

    A["x"], A["ctx"] = arr("x"), arr("ctx_1024")
    A["ctxT"] = arr("ctx_1024").transpose(0, 2, 1)
    A["pos"] = arr("pos_1xS2").astype(np.int32).reshape(1, P)
    A["mask"] = arr("mask_BxS2_bf1").view(np.uint8).reshape(1, B * P)

    def tiles(w):
        n = w.shape[0] // P
        return w.reshape(n, P, -1).transpose(1, 0, 2).reshape(P, -1)

    A["w0x"] = np.concatenate([arr("L0_xattn_Wq"), arr("L0_xattn_Wk"), arr("L0_xattn_Wv"), tiles(arr("L0_xattn_Wo"))], 1)

    def evens_odds(w, swap):
        w = w.reshape(w.shape[0], 16, 32, 2).transpose(0, 1, 3, 2)
        return (w[:, :, ::-1] if swap else w).reshape(w.shape[0], 1024)

    parts = [evens_odds(arr(n), s) for n in ("L0_ffn_q_w", "L0_ffn_k_w") for s in (0, 1)]
    A["w0f"] = np.concatenate(parts + [arr("L0_ffn_v_w"), tiles(arr("L0_ffn_o_w"))], 1)
    biases = [evens_odds(arr(n).reshape(1, -1), s).reshape(8, P).T for n in ("L0_ffn_q_b", "L0_ffn_k_b") for s in (0, 1)]

    def spread(w, head_of, count, order):
        out = np.zeros((D, count, 4, 32), w.dtype)
        for m in range(count):
            for g in range(4):
                h = head_of(m, g)
                out[:, m, g, 0:8] = w[:, 8 * h:8 * h + 8][:, order]
        return out.reshape(D, count * P)

    same, swapped = list(range(8)), [4, 5, 6, 7, 0, 1, 2, 3]
    head = lambda m, g: 4 * g + m
    A["w1x"] = np.concatenate([spread(arr("L1_xattn_Wq").T, head, 4, same), spread(arr("L1_xattn_Wk").T, head, 4, same),
                               arr("L1_xattn_Wv").T, arr("L1_xattn_Wo").T], 1)
    qkv = arr("L1_ffn_wqkv").T
    q, k, vv = qkv[:, 0:128], qkv[:, 128:160], qkv[:, 160:192]
    A["w1f"] = np.concatenate([spread(q, head, 4, same), spread(q, head, 4, swapped), spread(k, lambda m, g: g, 1, same),
                               spread(k, lambda m, g: g, 1, swapped), vv, arr("L1_ffn_wo").T], 1)
    A["wl2"] = np.concatenate([arr("L2_xattn_W")[:, 0:D].T, arr("L2_xattn_W")[:, D:].T], 1)
    A["w3"] = np.concatenate([tiles(arr("L3_ffn_w_gate")), tiles(arr("L3_ffn_w_up")), arr("L3_ffn_w_down")], 1)
    cols = [arr("L1_xattn_g1"), arr("L1_xattn_b1"), arr("L1_xattn_g2"), arr("L1_xattn_b2"), arr("L1_ffn_ln1_w"),
            arr("L1_ffn_ln2_w"), np.tile(arr("L0_ffn_theta"), 4), arr("L0_ffn_gamma2")]
    A["vec"] = np.concatenate([c.reshape(P, 1) for c in cols] + biases, 1)
    A["rows"] = np.concatenate([arr("L0_ffn_gamma1"), arr("L0_ffn_gamma2")]).reshape(1, -1)
    A["l0f_vb"] = arr("L0_ffn_v_b").reshape(1, -1)
    A["l0m_rb"] = arr("L0_ffn_router_b").reshape(1, -1)
    A["l2m_bias"] = arr("L2_ffn_bias").reshape(1, -1)
    A["brow"] = np.concatenate([arr("L0_xattn_bo"), arr("L0_ffn_o_b"), arr("L1_xattn_bo"), arr("L2_xattn_b")]).reshape(1, -1)
    A["b2"] = np.concatenate([arr("L0_ffn_re_b2"), arr("L0_ffn_sh_b2").reshape(1, D)], 0)
    A["rw"] = np.concatenate([arr("L0_ffn_router_w"), arr("L1_ffn_gate_w").T], 1)
    A["rwb"] = arr("L2_ffn_gate_w").T
    w1 = np.concatenate([arr("L0_ffn_re_w1"), arr("L0_ffn_sh_w1")[None]], 0)
    w2 = np.concatenate([arr("L0_ffn_re_w2"), arr("L0_ffn_sh_w2")[None]], 0)
    b1 = np.concatenate([arr("L0_ffn_re_b1"), arr("L0_ffn_sh_b1")[None]], 0)
    A["l0m"] = np.concatenate([w1, w2, b1[:, :, None]], 2)
    w2 = arr("L1_ffn_w2").transpose(0, 2, 1).reshape(8, 2, P, D).transpose(0, 2, 1, 3).reshape(8, P, 2 * D)
    A["l1m"] = np.concatenate([arr("L1_ffn_w13").transpose(0, 2, 1), w2], 2)
    sets = np.zeros((17, P, 3 * P), bf)
    sets[:16, :, 0:P] = arr("L2_ffn_W1").reshape(16, 2, D, 64).transpose(0, 2, 1, 3).reshape(16, D, P)
    sets[:16, :, P:2 * P] = arr("L2_ffn_W3").reshape(16, 2, D, 64).transpose(0, 2, 1, 3).reshape(16, D, P)
    sets[:16, :, 2 * P:] = arr("L2_ffn_W2").reshape(16, P, D)
    sets[16, :, 0:64] = arr("L2_ffn_sw1").T
    sets[16, :, P:P + 64] = arr("L2_ffn_sw3").T
    sets[16, 0:64, 2 * P:] = arr("L2_ffn_sw2").T
    A["l2m"] = sets

    n = np.arange(P)
    pos = np.arange(P, dtype=f)
    div = np.exp(np.arange(0, D, 2, dtype=f) * f(-(math.log(10000.0) / D))).astype(f)
    ang = pos[:, None] * div
    table = np.stack([np.sin(ang), np.cos(ang)], -1).reshape(P, D).astype(f)
    inv = (f(1.0) / f(10000.0) ** (np.arange(0, 8, 2, dtype=f) / f(8))).astype(f)
    freq = (pos[:, None] * inv[None, :]).astype(f)
    emb = np.concatenate([freq, freq], 1)
    cos1, sin1 = np.zeros((P, P), f), np.zeros((P, P), f)
    for g in range(4):
        for d in range(8):
            cos1[32 * g + d] = np.cos(emb[:, d])
            sin1[32 * g + d] = np.sin(emb[:, d]) * (-1 if d < 4 else 1)
    cols = np.stack([n.astype(f), (n % 32 == 8).astype(f), np.where(n // 32 % 2 == 0, -1, 1).astype(f), np.full(P, MAGIC, f)], 1)
    A["cf"] = np.concatenate([np.eye(P, dtype=f), (n[:, None] < n[None, :]).astype(f), np.tile(pos, (P, 1)), table, cos1, sin1,
                              cols, np.ones((P, P), f)], 1)
    causal = n[None, :] <= n[:, None]
    grouped = n[None, :] <= n[:, None] - 64
    hide = lambda keep: np.where(keep, 0.0, NEG).astype(bf)
    A["cb"] = np.concatenate([np.eye(P, dtype=bf)] + [hide(causal)] * HEADS + [hide(causal & ~grouped), hide(grouped)], 1)
    return A


def kernel(**inputs):
    import numpy as np
    import concourse.bacc as bacc
    from concourse.bass_utils import run_bass_kernel_spmd

    nc = bacc.Bacc("TRN2", target_bir_lowering=False, num_devices=1)
    arrays, aps = {}, {}
    for name, value in _layout(inputs).items():
        value = np.ascontiguousarray(value)
        arrays[f"in_{name}"] = value
        aps[name] = nc.dram_tensor(f"in_{name}", value.shape, mybir.dt.from_np(value.dtype), kind="ExternalInput").ap()
    out = nc.dram_tensor("out_x", (B, P, P), F32, kind="ExternalOutput").ap()
    build(nc, aps, out)
    r = run_bass_kernel_spmd(nc, [arrays], core_ids=[0])
    return r.results[0]["out_x"]
```

```python
from contextlib import ExitStack
import math

import concourse.bass as bass
from concourse import mybir
from concourse.alu_op_type import AluOpType as ALU

ACT = mybir.ActivationFunctionType
AX_X = mybir.AxisListType.X
F32 = mybir.dt.float32
BF16 = mybir.dt.bfloat16
F32R = mybir.dt.float32r
I32 = mybir.dt.int32
U32 = mybir.dt.uint32
U8 = mybir.dt.uint8

P = 128
B = 16
BANK = 512
PAIRS = B // 2
HEADS = 4
EPS = 1e-5
NEG = -1e30
HIDDEN_ORDER = [0, 2, 4, 1, 3, 5]
MAGIC = 1.5 * 2.0 ** 23
QMAX = 32767.0

LAYERS = [
    dict(name="l0x", units=2, heads=8, dim=64, scale=64 ** -0.5, jobs=[[0, 1], [2, 3]],
         back=["V0", "V1", "OT0", "OP0"]),
    dict(name="l0f", units=4, heads=16, dim=64, scale=64 ** -0.5, jobs=[[0, 1, 2], [3, 4, 5], [6, 7, 8], [9, 10]],
         back=["V0", "V1", "OT0", "V2", "V3", "OT1", "OP0"]),
    dict(name="l1x", units=4, heads=16, dim=8, scale=8 ** -0.5, jobs=[[0], [1], [2], [3]],
         back=["V0", "OB0", "OT0", "OP0"]),
    dict(name="l1f", units=4, heads=16, dim=8, scale=8 ** -0.5, jobs=[[0], [1], [2, 3], []],
         back=["V0", "OB0", "OT0", "OP0"]),
    dict(name="l3x", units=1, heads=1, dim=128, scale=1.0, jobs=[[0]], back=["V0"]),
]
for L in LAYERS:
    L["front"] = sum(len(slot) for slot in L["jobs"])
    L["turns"] = sum(use[:2] == "OT" for use in L["back"])


def schedule(L):
    units = L["units"]
    if units == 1:
        return [("Y", 0, "next"), ("S", 0, "own"), ("T", 0, "last"), ("E", 0, "own"), ("F", 0, "next"), ("V", 0, "last")]

    def unit(what, t):
        return (what, t, "own") if t >= 0 else (what, t + units, "last")

    parts = [("Y", 0, "next")]
    if L["dim"] == 8:
        before_jobs = [[], [("V", 3, "last")], [], [("OP", 0, "last"), ("V", 0, "own")]]
        at_end = [[("V", 2, "last")], [("OB", 0, "last")], [("OT", 0, "last")], [("V", 1, "own")]]
        for t in range(units):
            jobs = [("F", job, "next") for job in L["jobs"][t]]
            turn = [unit("T", t - 1)]
            parts += [("S", t, "own")] + before_jobs[t] + (turn + jobs if t == 0 else jobs + turn) + at_end[t] + [("E", t, "own")]
        return parts
    for t in range(units):
        jobs = [("F", job, "next") for job in L["jobs"][t]]
        parts.append(("S", t, "own"))
        if t == 2:
            parts.append(("OP", 0, "last"))
        parts += [unit("V", t - 2)] + jobs[:1] + [unit("T", t - 1)]
        if units == 2:
            parts += [("OT", 0, "last")] * (t == 1) + [("E", t, "own")] + jobs[1:] + [("OP", 0, "last")] * (t == 1)
        else:
            parts += [("E", t, "own")] + jobs[1:]
            if t == 1:
                parts.append(("OT", 1, "last"))
            if t == 3:
                parts.append(("OT", 0, "own"))
    return parts


EXPERTS = [
    dict(name="l0m", steps=32, halves=1, gated=False, up=P, wcols=2 * P + 1),
    dict(name="l1m", steps=8, halves=2, gated=True, up=4 * P, wcols=6 * P),
    dict(name="l2m", steps=17, halves=1, gated=True, up=2 * P, wcols=3 * P),
]
NORMS = {"l0x": ["r1"], "l0f": ["r12"], "l0m": ["rms"], "ctx": ["r1"], "l1x": ["r12"], "l1f": ["r12", "r1"],
         "l1m": ["rms"], "l2x": ["r1"], "l2m": ["r1"], "l3x": ["r1"], "l3m": ["r1"]}
PARTS = {n: {"l0x": [(0, 4), (4, B)], "l2m": [(0, 8), (8, B)], "ctx": [(0, B)]}.get(n, [(0, 12), (12, B)]) for n in NORMS}
AFTER = {"l0x": "l0f", "l0f": "l0m", "l0m": "l1x", "l1x": "l1f", "l1f": "l1m", "l1m": "l2x", "l2m": "l3x", "l3x": "l3m"}
CHUNKS = B * P // BANK
GCOLS = 34
CAPACITY = 2 * 512 * 4 // 32


def build(nc, a, out):
    ctx = ExitStack()
    with ctx:
        def sb(name, shape, dt=F32):
            return ctx.enter_context(nc.sbuf_tensor(name, shape, dt))

        def sem(name):
            return ctx.enter_context(nc.semaphore(name))

        def pair(name):
            return [sem(f"{name}{s}") for s in range(2)]

        def bank(name):
            return ctx.enter_context(nc.psum_tensor(name, [P, BANK], F32))

        def wide(ap, n, m):
            return ap.unsqueeze(2).to_broadcast([P, n, m])

        def over(ap, n):
            return ap.unsqueeze(1).to_broadcast([P, n, ap.shape[1]])

        def split(ap, n):
            return ap.rearrange("p (n m) -> p n m", n=n)

        s_bank = [bank(f"s_bank{s}") for s in range(2)]
        t_bank = [bank(f"t_bank{s}") for s in range(2)]
        v_bank = [bank(f"v_bank{s}") for s in range(2)]
        f_bank = [bank(f"f_bank{s}") for s in range(2)]

        router_bank = s_bank[0]
        l2x_bank = v_bank + t_bank

        X = sb("X", [P, B, P])
        AO = sb("AO", [P, B, P])
        Y = sb("Y", [P, B, P])
        YT = sb("YT", [P, B * P])
        CTX = sb("CTX", [P, B, P])
        with nc.sbuf_tensor("parts", [P, 6 * 8 * P], F32R) as parts:
            pass
        big = sb("big", [P, 6 * 8 * P])
        work = sb("work", [P, 6 * 8 * P])
        qT = [work[:, 1024 * s:1024 * s + 1024] for s in range(2)]
        kT = [work[:, 1024 * s + 2048:1024 * s + 3072] for s in range(2)]
        o_tok = [work[:, 1024 * s + 4096:1024 * s + 5120] for s in range(2)]
        GT = work[0:32, 0:B * P]
        U3 = work[:, :].rearrange("p (m t) -> p m t", m=3)
        W0X = sb("W0X", [P, 4, 4 * P])
        W1X = sb("W1X", [P, 10 * P])
        W1F = sb("W1F", [P, 8 * P + 2 * P + 32 + P])
        WL2 = sb("WL2", [P, 2 * P])
        W3N = work[:, 1024:1024 + 9 * P]
        POSF = work[:, 0:3 * P].rearrange("p (m s) -> p m s", m=3)
        HOT = work[:, 3 * P:6 * P].rearrange("p (m s) -> p m s", m=3)
        W3T = sb("W3T", [P, 9 * P])
        W3M = sb("W3M", [P, 36])
        W3S = sb("W3S", [P, 36])
        W3R = sb("W3R", [P, 36])
        VEC = sb("VEC", [P, a["vec"].shape[1]])
        ROWS = sb("ROWS", [P, 3 * P])
        RB = sb("RB", [P, 31])
        LB = sb("LB", [P, 32])
        RW = sb("RW", [P, 31 + 8 + 32])
        RWB = sb("RWB", [P, 32], BF16)
        BROW = sb("BROW", [1, 4 * P])
        VB = sb("VB", [P, 8 * P])
        MASK = sb("MASK", [P, B, P], BF16)
        MASKU = sb("MASKU", [P, B * P], U8)
        NANF = sb("NANF", [P, B])
        POSI = sb("POSI", [P, P], I32)
        POSG = sb("POSG", [P, P], I32)
        PET = sb("PET", [P, 3 * P])
        CF = sb("CF", [P, a["cf"].shape[1]])
        CB = sb("CB", [P, a["cb"].shape[1]], BF16)
        ones_row = sb("ones_row", [1, P])
        half_neg = sb("half_neg", [P, B])
        B2 = sb("B2", [32, P])
        GATES = sb("GATES", [P, B, GCOLS])

        y_tok = [sb(f"y_tok{s}", [P, P]) for s in range(2)]
        y_aux = [sb(f"y_aux{s}", [P, P]) for s in range(2)]
        yT = [sb(f"yT{s}", [P, P]) for s in range(2)]
        cT = [sb(f"cT{s}", [P, P]) for s in range(2)]
        V64 = [sb(f"V64_{s}", [P, 16, 65]) for s in range(2)]
        V8 = [W0X[:, 1 + s, :].rearrange("p (h c) -> p h c", c=32) for s in range(2)]
        spread_o = W0X[:, 0, :]
        V128 = [sb(f"V128_{s}", [P, P + 1]) for s in range(2)]
        rope_a = [sb(f"rope_a{s}", [P, BANK]) for s in range(2)]
        rope_b = [sb(f"rope_b{s}", [P, BANK]) for s in range(2)]
        shifted = [sb(f"shifted{s}", [P, BANK]) for s in range(2)]
        h_all = sb("h_all", [P, 4 * BANK])
        hT = [h_all[:, BANK * s:BANK * s + BANK] for s in range(4)]
        probs, probsT = hT[0:2], hT[2:4]
        row_max = [sb(f"row_max{s}", [P, HEADS]) for s in range(2)]
        recips = [sb(f"recips{s}", [P, 16]) for s in range(2)]
        oT = sb("oT", [P, 8 * P])
        wset = [sb(f"wset{s}", [P, 6 * P]) for s in range(2)]
        wraw = [sb(f"wraw{s}", [P, 3 * P], BF16) for s in range(2)]
        act_sb = shifted
        st = sb("st", [P, B, 6])
        small = sb("small", [P, 13, B])
        lg = sb("lg", [P, B, 32])
        ex = sb("ex", [P, B, 32])
        top8 = sb("top8", [P, B, 8])
        idx8 = sb("idx8", [P, B, 8], U32)
        idxf = sb("idxf", [P, B, 8])
        hits = work[:, 4096:6144].rearrange("p (b k e) -> p b k e", b=B, k=4)
        sel = sb("sel", [P, B, 32])
        run = [rope_a[s][:, :].rearrange("p (b e) -> p b e", b=B) for s in range(2)]
        quant = sb("quant", [P, 5, 4])
        part_max = sb("part_max", [P, 24])
        sig = [CTX[:, 8 * s:8 * s + 8, :].rearrange("p b d -> p (b d)") for s in range(2)]
        csum = sb("csum", [P, B])
        batch_rows = sb("batch_rows", [B, P])
        context_rows = AO[0:B, :, :].rearrange("p b d -> p (b d)")
        cstat = sb("cstat", [P, 4, B])
        waited = sb("waited", [P, 2])
        cst = sb("cst", [P, B, 6])
        tmpT = sb("tmpT", [P, 4, P])
        joined = [sb(f"joined{s}", [P, P]) for s in range(2)]

        mean, r1, r12, var, ve, t0, t1, ms = (small[:, n, :] for n in range(8))
        cmean, cr1, cvar, cve = (cstat[:, n, :] for n in range(4))
        srow0, srow1, srow2, srow3, ve12 = (small[:, n, :] for n in range(8, 13))
        ident = CF[:, 0:P]
        before = CF[:, P:2 * P]
        iota_row = CF[:, 2 * P:3 * P]
        pe = CF[:, 3 * P:4 * P]
        cos1 = CF[:, 4 * P:5 * P]
        sin1 = CF[:, 5 * P:6 * P]
        part_no = CF[:, 6 * P:6 * P + 1]
        ones_at = CF[:, 6 * P + 1:6 * P + 2]
        sin_sign = CF[:, 6 * P + 2:6 * P + 3]
        magic = CF[:, 6 * P + 3:6 * P + 4]
        ones_sq = CF[:, 6 * P + 4:7 * P + 4]
        part_one = CF[:, 6 * P + 4:6 * P + 5]
        ident_bf = CB[:, 0:P]
        causal_bf = CB[:, P:P + BANK]
        own_bf = CB[:, P + BANK:P + BANK + 2 * P]
        names = ["l1x_g1", "l1x_b1", "l1x_g2", "l1x_b2", "l1f_ln1", "l1f_ln2", "theta", "gamma2"]
        vec = {n: VEC[:, j:j + 1] for j, n in enumerate(names)}
        qb_a = VEC[:, 8:16]
        qb_b = VEC[:, 16:24]
        kb_a = VEC[:, 24:32]
        kb_b = VEC[:, 32:40]
        gamma1_row = ROWS[:, 0:P]
        gamma2_row = ROWS[:, P:2 * P]
        bo = {"l0x": BROW[:, 0:P], "l0f": BROW[:, P:2 * P], "l1x": BROW[:, 2 * P:3 * P], "l2x": BROW[:, 3 * P:4 * P]}
        w0f = {n: big[:, 1024 * j:1024 * j + 1024] for j, n in enumerate(["qa", "qb", "ka", "kb", "v", "o"])}
        w1f = {"qa": W1F[:, 0:512], "qb": W1F[:, 512:1024], "ka": W1F[:, 1024:1152], "kb": W1F[:, 1152:1280],
               "v": W1F[:, 1280:1312], "o": W1F[:, 1312:1440]}
        w1x = {"q": W1X[:, 0:512], "k": W1X[:, 512:1024], "v": W1X[:, 1024:1152], "o": W1X[:, 1152:1280]}
        TAB = sb("TAB", [P, 2 * P + 16 * P])
        cos0, sin0 = TAB[:, 0:P], TAB[:, P:2 * P]
        tbq, tbk = TAB[:, 2 * P:10 * P], TAB[:, 10 * P:18 * P]
        G3 = big[:, :].rearrange("p (m t) -> p m t", m=3)
        half_word = lambda lo, words: big[:, lo:lo + words].bitcast(BF16)
        y_part = [half_word(1024 * n, 1024) for n in range(3)]
        gates_turned, pick = half_word(3072, 1024), half_word(4096, 17 * P // 2)
        gate_part = [split(half_word(5184 + 256 * n, 256), B) for n in range(2)]
        rest = Y[:, :, :].rearrange("p b d -> p (b d)")
        gate_sum = h_all[:, :].rearrange("p (b e) -> p b e", b=B)

        y_high, y_low = parts[:, 0:2048], parts[:, 2048:4096]
        w_high = [parts[:, 4096 + 1024 * s:4608 + 1024 * s] for s in range(2)]
        w_low = [parts[:, 4608 + 1024 * s:5120 + 1024 * s] for s in range(2)]

        in_x, in_ctx, in_c, in_cb, in_w0x, in_w0f, in_w1, in_rows, in_w3 = (sem(n) for n in (
            "in_x", "in_ctx", "in_c", "in_cb", "in_w0x", "in_w0f", "in_w1", "in_rows", "in_w3"))
        tiles_measured = sem("tiles_measured")
        y_ready, aux_ready, cT_ready, v_dma = pair("y_ready"), pair("aux_ready"), pair("cT_ready"), pair("v_dma")
        f_full, f_drained = pair("f_full"), pair("f_drained")
        b_drained, turned, projected, regrouped = pair("b_drained"), sem("turned"), sem("projected"), sem("regrouped")
        s_full, shifted_ready, max_ready = pair("s_full"), pair("shifted_ready"), pair("max_ready")
        probs_ready, t_full, probsT_ready = pair("probs_ready"), pair("t_full"), pair("probsT_ready")
        pv_done, recip_ready = pair("pv_done"), pair("recip_ready")
        rope_sum, rope_done, k3_ready = pair("rope_sum"), pair("rope_done"), pair("k3_ready")
        grouped_ready, joined_ready = pair("grouped_ready"), pair("joined_ready")
        dve_chain, pool_chain = sem("dve_chain"), sem("pool_chain")
        w_loaded, w_cast, w_highs, w_split = pair("w_loaded"), pair("w_cast"), pair("w_highs"), pair("w_split")
        y_split = sem("y_split")
        spread_full, product_ready, in_pick = pair("spread_full"), pair("product_ready"), sem("in_pick")
        g_full, g_drained, u_full, h_ready = pair("g_full"), pair("g_drained"), pair("u_full"), pair("h_ready")
        d_full, d_drained = pair("d_full"), pair("d_drained")
        stored = sem("stored")
        step_sem = {}

        def step(name):
            if name not in step_sem:
                step_sem[name] = sem(name.replace(".", "_"))
            return step_sem[name]

        front_at, n = {}, 0
        for name, uses in [("l0x", 4 * B), ("l0f", 11 * B), ("l0m", 14), ("l1x", 4 * B), ("l1f", 4 * B),
                           ("l1m", 4), ("turn_w3", 4), ("l2x", 4), ("l2m", 9), ("l3x", B), ("l3m", 32)]:
            front_at[name] = n
            n += uses
        unit_at, back_at, turn_at, proj_at = {}, {}, {}, {}
        nu = nb = nt = npr = 0
        for j, L in enumerate(LAYERS):
            name = L["name"]
            L["no"] = j
            unit_at[name], back_at[name], turn_at[name], proj_at[name] = nu, nb, nt, npr
            nu, nb, nt = nu + L["units"] * B, nb + len(L["back"]) * B, nt + L["turns"] * B
            npr += B * (L["turns"] > 0)
        hid_at, sum_at, set_at = {}, {}, {}
        nh = nd = ns = 0
        for M in EXPERTS:
            hid_at[M["name"]], sum_at[M["name"]], set_at[M["name"]] = nh, nd, ns
            nh += M["steps"] * CHUNKS * M["halves"]
            nd += M["steps"] * CHUNKS
            ns += M["steps"]
        assert hid_at["l2m"] % 2 == 0
        ungated = hid_at["l1m"]
        ORDER = {L["name"]: schedule(L) for L in LAYERS}

        def place(at, per, i, s, c):
            c = at + per * s + c
            return c % 2, per * i + c // 2 + 1

        def front_use(name, c):
            c += front_at[name]
            return c % 2, c // 2 + 1

        def heads_of(L, u):
            if L["dim"] == 64:
                return [(8 * (u // 2) + u % 2 + 2 * m, 64 * (u % 2), 4 * (u // 2) + m, 4 * (u // 2) + m, 64,
                         8 * (u // 2) + u % 2 + 2 * m) for m in range(HEADS)]
            if L["name"] == "l1x":
                return [(4 * u + m, 32 * u, m, m, 32, 4 * u + m) for m in range(HEADS)]
            return [(4 * u + m, 32 * u, m, 0, 32, u) for m in range(HEADS)]

        regrouped_at = {"l1x": 0, "l1f": B}
        recips_at, nr = {}, 0
        for L in LAYERS:
            recips_at[L["name"]] = nr
            nr += L["units"] * PAIRS if L["dim"] == 64 else PAIRS

        def batches(eng, n, do, after_first=None, after_second=None, before_last=None):
            def step_of(i, own):
                for what, u, whose in ORDER[n]:
                    s = own + {"last": -1, "own": 0, "next": 1}[whose]
                    if isinstance(i, int):
                        if not 0 <= 2 * i + s < B:
                            continue
                        do(what, u, i + s // 2, s % 2)
                    else:
                        do(what, u, i, s)

            step_of(0, -1)
            if after_first:
                after_first()
            step_of(0, 0)
            if after_second:
                after_second()
            with eng.Fori(0, PAIRS - 1) as i:
                step_of(i, 1)
                step_of(i, 2)
            if before_last:
                before_last()
            step_of(PAIRS - 1, 1)
            step_of(PAIRS - 1, 2)

        def back_use(L, use, i, s):
            return place(back_at[L["name"]], len(L["back"]), i, s, L["back"].index(use))

        def pv_use(L, u):
            return f"V{u}" if L["dim"] == 64 else "V0"

        def sets(eng, M, chunk):
            pairs, odd = M["steps"] // 2, M["steps"] % 2
            with eng.Fori(0, pairs - 1 + odd) as i:
                for s in range(2):
                    for c in range(CHUNKS):
                        chunk(i, s, c, False)
            for s in range(1 if odd else 2):
                for c in range(CHUNKS):
                    chunk(pairs - 1 + odd, s, c, s == (0 if odd else 1) and c == CHUNKS - 1)

        def after(i, s, c):
            return (i, s, c + 1) if c + 1 < CHUNKS else (i, 1, 0) if s == 0 else (i + 1, 0, 0)

        def last_sum(M, i, s):
            return place(sum_at[M["name"]], CHUNKS, i, s, CHUNKS - 1)

        def col(ap, b):
            return ap[:, bass.ds(b, 1)]

        def tile(t, b):
            return t[:, bass.ds(b, 1), :].rearrange("p o d -> p (o d)")

        def rows_to_all(ap):
            return ap.partition_broadcast(P).rearrange("p o n -> p (o n)")

        block = ctx.enter_context(nc.Block())

        @block.sync
        def _(sp):
            def load(dst, src, s):
                sp.dma_start(dst, src).then_inc(s, 16)

            load(X[:, 0:4, :], a["x"][0:4].rearrange("b s d -> s b d"), in_x)
            load(X[:, 4:B, :], a["x"][4:B].rearrange("b s d -> s b d"), in_x)
            load(CF[:, :], a["cf"], in_c)
            load(VEC[:, :], a["vec"], in_c)
            load(BROW[:, :], a["brow"], in_c)
            def context0(i, s):
                sp.dma_start(cT[s][:, :], a["ctxT"][bass.ds(2 * i + s, 1), :, :].rearrange("o p n -> (o p) n")).then_inc(cT_ready[s], 16)

            for s in range(2):
                context0(0, s)
            load(W0X[:, :, :], split(a["w0x"], 4), in_w0x)
            load(CB[:, :], a["cb"], in_cb)
            load(ROWS[:, 0:2 * P], rows_to_all(a["rows"]), in_rows)
            load(VB[:, :], rows_to_all(a["l0f_vb"]), in_rows)
            load(RB[:, :], rows_to_all(a["l0m_rb"]), in_rows)
            load(LB[:, :], rows_to_all(a["l2m_bias"]), in_rows)
            load(B2[:, :], a["b2"], in_rows)
            load(RW[:, 0:39], a["rw"], in_rows)
            load(RWB[:, :], a["rwb"], in_rows)
            load(POSI[:, :], rows_to_all(a["pos"]), in_rows)
            load(MASKU[:, :], rows_to_all(a["mask"]), in_rows)
            load(big[:, :], a["w0f"], in_w0f)
            load(CTX[:, :, :], a["ctx"].rearrange("b s d -> s b d"), in_ctx)
            load(W1X[:, :], a["w1x"], in_w1)
            load(W1F[:, :], a["w1f"], in_w1)
            load(WL2[:, :], a["wl2"], in_w1)
            with sp.Fori(1, PAIRS) as i:
                for s in range(2):
                    for job in (2, 3):
                        r, k = place(front_at["l0x"], 4, i - 1, s, job)
                        sp.wait_ge(f_full[r], k + 1)
                    context0(i, s)

            def weights(M, dst, wait):
                def one(i, s):
                    wait(i, s)
                    sp.dma_start(dst[s][:, 0:M["wcols"]], a[M["name"]][bass.ds(2 * i + s, 1), :, :].rearrange("o p n -> (o p) n")).then_inc(w_loaded[s], 16)

                for s in range(2):
                    one(0, s)
                with sp.Fori(1, M["steps"] // 2) as i:
                    for s in range(2):
                        one(i, s)
                if M["steps"] % 2:
                    one(M["steps"] // 2, 0)

            def slot_free(M, prev):
                def wait(i, s):
                    if isinstance(i, int) and i == 0:
                        if prev is None:
                            return
                        r, k = last_sum(prev, prev["steps"] // 2 - 1, s)
                    else:
                        r, k = last_sum(M, i - 1, s)
                    sp.wait_ge(d_full[r], k + 1)
                return wait

            weights(EXPERTS[0], wset, slot_free(EXPERTS[0], None))
            weights(EXPERTS[1], wset, slot_free(EXPERTS[1], EXPERTS[0]))
            load(W3N[:, :], a["w3"], in_w3)
            r, k = last_sum(EXPERTS[1], EXPERTS[1]["steps"] // 2 - 1, 1)
            sp.wait_ge(d_full[r], k + 1)
            load(pick, a["pick"], in_pick)

            def raw_free(i, s):
                if isinstance(i, int) and i == 0:
                    sp.wait_ge(w_loaded[s], 16 * (set_at["l2m"] // 2))
                else:
                    r, k = last_sum(EXPERTS[2], i - 1, s)
                    sp.wait_ge(d_full[r], k + 1)

            weights(EXPERTS[2], wraw, raw_free)

            sp.wait_ge(step("l3x.begin"), 1)

            def context3(i, s):
                b = 2 * i + s
                if not (isinstance(i, int) and i == 0):
                    sp.wait_ge(k3_ready[s], 2 * i)
                sp.dma_start(cT[s][:, :], a["ctxT"][bass.ds(b, 1), :, :].rearrange("o p n -> (o p) n")).then_inc(cT_ready[s], 16)
                if not (isinstance(i, int) and i == 0):
                    r, k = place(unit_at["l3x"], 1, i - 1, s, 0)
                    sp.wait_ge(pv_done[r], k + 1)
                sp.dma_start(V128[s][:, 0:P], a["ctx"][bass.ds(b, 1), :, :].rearrange("o p n -> (o p) n")).then_inc(v_dma[s], 16)

            for s in range(2):
                context3(0, s)
            with sp.Fori(1, PAIRS) as i:
                for s in range(2):
                    context3(i, s)

            for g in range(4):
                r, k = front_use("l3m", 28 + g)
                sp.wait_ge(f_drained[r], k + 1)
                sp.dma_start(out[4 * g:4 * g + 4].rearrange("b s d -> s b d"), X[:, 4 * g:4 * g + 4, :]).then_inc(stored, 16)
            sp.wait_ge(stored, 4 * 16)

        @block.gpsimd
        def _(pool):
            links = [0]

            def link(ins):
                links[0] += 1
                ins.then_inc(pool_chain, 1)
                pool.wait_ge(pool_chain, links[0])

            for ring in (f_full, f_drained, b_drained, s_full, shifted_ready, max_ready, probs_ready, t_full, probsT_ready,
                         pv_done, rope_sum, rope_done, grouped_ready, joined_ready, g_full, g_drained, u_full, h_ready,
                         d_full, d_drained, spread_full, product_ready):
                for s in range(2):
                    pool.sem_inc(ring[s], 1)
            link(pool.memset(half_neg[:, :], -0.5))
            pool.memset(waited[:, :], 0.0)
            pool.memset(ones_row[:, :], 1.0)
            for s in range(2):
                pool.memset(V64[s][:, :, 64:65], 1.0)
                pool.memset(V128[s][:, P:P + 1], 1.0)
            pool.memset(ex[:, :, :], -1.0)
            link(pool.memset(GATES[:, :, :], 0.0))
            pool.memset(GATES[:, :, 32:33], 1.0)
            pool.memset(GATES[:, :, 31:32], 1.0).then_inc(step("setup.ones"), 1)

            def power(name):
                for part, (lo, hi) in enumerate(PARTS[name]):
                    pool.wait_ge(step(name + ".var"), part + 1)
                    for what in NORMS[name]:
                        src, dst = (ve12, r12) if what == "r12" else (cve, cr1) if name == "ctx" else (ve, r1)
                        last = pool.tensor_tensor(dst[:, lo:hi], src[:, lo:hi], half_neg[:, lo:hi], ALU.pow)
                    last.then_inc(step(name + ".r"), 1)

            def attention(L):
                n = L["name"]

                def do(what, u, i, s):
                    t = s % 2
                    if n == "l0f" and what == "Y":
                        pool.wait_ge(y_ready[t], PAIRS * L["no"] + s // 2 + 1 + i)
                        pool.tensor_tensor(y_aux[t][:, :], y_tok[t][:, :], gamma1_row, ALU.mult).then_inc(aux_ready[t], 1)
                    if n == "l0f" and what == "F" and u in (2, 4, 6, 8):
                        piece = u // 2 - 1
                        half = slice(BANK * (piece % 2), BANK * (piece % 2) + BANK)
                        r, k = place(front_at[n], L["front"], i, s, u)
                        pool.wait_ge(f_drained[r], k + 1)
                        r, k = place(0, 4, i, s, piece)
                        pool.tensor_tensor(rope_a[r][:, :], rope_a[r][:, :], rope_b[r][:, :], ALU.add).then_inc(rope_sum[r], 1)
                        pool.wait_ge(rope_sum[r], k + 1)
                        pool.tensor_tensor((qT if piece < 2 else kT)[t][:, half], rope_a[r][:, :],
                                           (tbq if piece < 2 else tbk)[:, half], ALU.add).then_inc(rope_done[r], 1)
                    if n == "l1f" and what == "F" and u in (2, 3):
                        r, k = place(front_at[n], L["front"], i, s, u)
                        pool.wait_ge(f_drained[r], k + 1)
                        r, k = place(4 * B, 2, i, s, u - 2)
                        cols = BANK if u == 2 else P
                        pool.tensor_tensor((qT if u == 2 else kT)[t][:, 0:cols], rope_a[r][:, 0:cols],
                                           rope_b[r][:, 0:cols], ALU.add).then_inc(rope_done[r], 1)
                    if n == "l3x" and what == "F":
                        pool.wait_ge(cT_ready[t], 16 * (PAIRS + s // 2 + 1) + 16 * i)
                        pool.wait_ge(y_ready[t], PAIRS * L["no"] + s // 2 + 1 + i)
                        pool.tensor_tensor(kT[t][:, 0:P], cT[t][:, :], PET[:, 0:P], ALU.add).then_inc(k3_ready[t], 1)
                        pool.tensor_tensor(kT[t][:, P:2 * P], cT[t][:, :], PET[:, 2 * P:3 * P], ALU.add).then_inc(k3_ready[t], 1)
                batches(pool, n, do)

            def residual(name):
                pool.wait_ge(step(name + ".y"), 4)
                link(pool.tensor_tensor(X[:, :, :], X[:, :, :], AO[:, :, :], ALU.add))
                if name == "l0m":
                    pool.wait_ge(step("l0m.an"), 4)
                    link(pool.tensor_tensor(X[:, :, :], X[:, :, :], Y[:, :, :], ALU.add))
                pool.sem_inc(step(name + ".x_ready"), 1)

            power("l0x")
            pool.wait_ge(in_c, 16 * 3)
            turns = [6.28125, 1.9340515136718750e-3, 1.2556659146e-6]
            link(pool.tensor_scalar(tmpT[:, 2, :], iota_row, vec["theta"], None, ALU.mult))
            for c, quarter in ((0, 0.0), (1, 0.25)):
                link(pool.tensor_scalar(tmpT[:, 3, :], tmpT[:, 2, :], 1.0 / (2.0 * math.pi), quarter, ALU.mult, ALU.add))
                link(pool.tensor_scalar(tmpT[:, 3, :], tmpT[:, 3, :], MAGIC, MAGIC, ALU.add, ALU.subtract))
                src = tmpT[:, 2, :]
                for turn in turns:
                    link(pool.tensor_scalar(cos0, tmpT[:, 3, :], -turn, None, ALU.mult))
                    link(pool.tensor_tensor(tmpT[:, c, :], src, cos0, ALU.add))
                    src = tmpT[:, c, :]
            link(pool.tensor_scalar(tmpT[:, 1, :], tmpT[:, 1, :], math.pi / 2, None, ALU.add))
            pool.tensor_scalar(tmpT[:, 0:2, :], tmpT[:, 0:2, :], 3.1415925, -3.1415925, ALU.min, ALU.max).then_inc(step("setup.angles"), 1)
            pool.wait_ge(step("setup.sin"), 1)
            link(pool.tensor_scalar(sin0, tmpT[:, 2, :], sin_sign, None, ALU.mult))
            link(pool.tensor_copy(cos0, tmpT[:, 3, :]))
            swapped = Y[:, 0:8, :]
            for dst, ba, bb in ((tbq, qb_a, qb_b), (tbk, kb_a, kb_b)):
                pool.tensor_tensor(split(dst, 8), over(cos0, 8), wide(ba, 8, P), ALU.mult)
                link(pool.tensor_tensor(swapped, over(sin0, 8), wide(bb, 8, P), ALU.mult))
                link(pool.tensor_tensor(split(dst, 8), split(dst, 8), swapped, ALU.add))
            pool.sem_inc(step("setup.tables"), 1)
            pool.wait_ge(in_rows, 16 * 9)
            power("l0f")
            for s in range(2):
                pool.memset(V8[s][:, :, 8:9], 1.0)
                pool.memset(V8[s][:, :, 9:32], 0.0)
            attention(LAYERS[1])
            power("l0m")
            residual("l0m")
            maskf = MASK[:, :, :].rearrange("p b s -> p (b s)")
            pool.tensor_copy(RW[:, 39:71], RWB[:, :])
            pool.tensor_copy(maskf, MASKU[:, :]).then_inc(step("setup.mask_read"), 1)
            pool.wait_ge(step("setup.keys"), 1)
            link(pool.tensor_tensor(srow3, NANF[:, :], half_neg[:, :], ALU.pow))
            link(pool.tensor_tensor(NANF[:, :], NANF[:, :], srow3, ALU.mult))
            pool.tensor_scalar(maskf, maskf, -1.0, -NEG, ALU.add, ALU.mult).then_inc(step("setup.mask"), 1)
            power("ctx")
            power("l1x")
            power("l1f")
            attention(LAYERS[3])
            power("l1m")
            residual("l1m")
            r, k = front_use("l0m", 5)
            pool.wait_ge(f_drained[r], k + 1)
            pool.tensor_tensor(AO[0:B, :, :], batch_rows[:, :].unsqueeze(1).to_broadcast([B, B, P]),
                               ident[0:B, 0:B].unsqueeze(2).to_broadcast([B, B, P]), ALU.mult).then_inc(step("l2x.spread"), 1)
            pool.wait_ge(in_w3, 16)
            pool.wait_ge(step("l3.groups"), 1)
            pool.tensor_copy(POSF[:, 0, :], POSI[:, :])
            link(pool.tensor_copy(POSF[:, 2, :], POSG[:, :]))
            link(pool.tensor_scalar(POSF[:, 1, :], POSF[:, 2, :], 60.0, None, ALU.add))
            link(pool.tensor_scalar(POSF[:, :, :], POSF[:, :, :], 0.0, P - 1.0, ALU.max, ALU.min))
            pool.tensor_scalar(HOT[:, :, :], POSF[:, :, :], part_no, None, ALU.is_equal).then_inc(step("l3.hot"), 1)
            w3 = W3N[:, :].rearrange("p (n m) -> p n m", m=32)
            pool.wait_ge(step("l3.w3_steps"), 1)
            link(pool.tensor_tensor(w3, w3, wide(W3R[:, :], 36, 32), ALU.mult))
            link(pool.tensor_scalar(W3N[:, :], W3N[:, :], MAGIC, None, ALU.add))
            link(pool.tensor_scalar(W3N[:, :], W3N[:, :], MAGIC, 7.0, ALU.subtract, ALU.min))
            link(pool.tensor_scalar(W3N[:, :], W3N[:, :], -8.0, None, ALU.max))
            pool.tensor_tensor(w3, w3, wide(W3S[:, :], 36, 32), ALU.mult).then_inc(step("l3.w3"), 1)
            power("l2x")
            power("l2m")
            for g in range(4):
                r, k = front_use("l2m", g)
                pool.wait_ge(f_drained[r], k + 1)
                c = slice(BANK * g, BANK * g + BANK)
                pool.tensor_tensor(rest[:, c], YT[:, c], y_part[0][:, c], ALU.subtract).then_inc(step("l2m.rest"), 1)
            for g in range(4):
                pool.wait_ge(step("l2m.second"), g + 1)
                c = slice(BANK * g, BANK * g + BANK)
                pool.tensor_tensor(y_part[2][:, c], rest[:, c], y_part[1][:, c], ALU.subtract).then_inc(step("l2m.third"), 1)
            power("l3x")
            attention(LAYERS[4])
            power("l3m")
            largest = 0
            for n, count in enumerate([1, 2, 1, 1]):
                pool.wait_ge(step("l3m.part_max"), n + 1)
                for c in range(count):
                    pool.partition_all_reduce(quant[:, largest, 1:2], quant[:, largest, 0:1], P,
                                              bass.bass_isa.ReduceOp.max).then_inc(step("l3m.all_max"), 1)
                    largest += 1
                if n == 1:
                    pool.wait_ge(step("l3m.scale"), 3)
                    for at, h in enumerate(HIDDEN_ORDER):
                        pool.wait_ge(step("l3m.u_round"), at + 1)
                        u = U3[:, :, :].rearrange("p m t -> p (m t)")[:, 1024 * h:1024 * h + 1024]
                        link(pool.tensor_tensor(u, u, magic.to_broadcast([P, 1024]), ALU.subtract))
                        pool.tensor_tensor(u, u, quant[:, 1, 2:3].to_broadcast([P, 1024]), ALU.mult).then_inc(step("l3m.u"), 1)

        @block.scalar
        def _(act):
            def attention(L, after_second=None):
                n, units = L["name"], L["units"]
                cols = BANK if units > 1 else P

                def do(what, u, i, s):
                    t = s % 2
                    if what == "E":
                        r, k = place(unit_at[n], units, i, s, u)
                        act.wait_ge(shifted_ready[r], k + 1)
                        act.wait_ge(t_full[r], k)
                        act.activation(probs[r][:, 0:cols], shifted[r][:, 0:cols], ACT.Exp, scale=L["scale"]).then_inc(probs_ready[r], 1)
                    if what == "T":
                        r, k = place(unit_at[n], units, i, s, u)
                        act.wait_ge(t_full[r], k + 1)
                        act.wait_ge(pv_done[r], k)
                        act.activation(probsT[r][:, 0:cols], t_bank[r][:, 0:cols], ACT.Copy).then_inc(probsT_ready[r], 1)
                    if what == "V" and u == units - 1 and L["dim"] == 8:
                        r, k = place(unit_at[n], units, i, s, u)
                        act.wait_ge(pv_done[r], k + 1)
                        r, k = back_use(L, "V0", i, s)
                        act.activation(spread_o[:, :], v_bank[r][:, :], ACT.Copy).then_inc(b_drained[r], 1)
                    if what == "OT":
                        r, k = back_use(L, f"OT{u}", i, s)
                        act.wait_ge(turned, turn_at[n] + L["turns"] * s + u + 1 + 2 * L["turns"] * i)
                        c = BANK if L["dim"] == 64 else P
                        act.activation(oT[:, BANK * u:BANK * u + c], v_bank[r][:, 0:c], ACT.Copy).then_inc(b_drained[r], 1)
                    if what != "F":
                        return
                    r, k = place(front_at[n], L["front"], i, s, u)
                    bk = f_bank[r]
                    if u == 0 and n != "l3x":
                        act.wait_ge(f_full[r], k + 1)
                        if n == "l1x":
                            act.activation(yT[t][:, :], bk[:, 0:P], ACT.Identity, scale=vec["l1x_g1"], bias=vec["l1x_b1"])
                            act.activation(cT[t][:, :], bk[:, P:2 * P], ACT.Identity, scale=vec["l1x_g2"],
                                           bias=vec["l1x_b2"]).then_inc(f_drained[r], 1)
                        elif n == "l1f":
                            act.activation(yT[t][:, :], bk[:, 0:P], ACT.Copy, scale=vec["l1f_ln1"]).then_inc(f_drained[r], 1)
                        else:
                            act.activation(yT[t][:, :], bk[:, 0:P], ACT.Copy).then_inc(f_drained[r], 1)
                    if n == "l0x" and u in (1, 2):
                        act.wait_ge(f_full[r], k + 1)
                        act.activation((qT if u == 1 else kT)[t][:, 0:BANK], bk[:, :], ACT.Copy).then_inc(f_drained[r], 1)
                    if n == "l1x" and u == 1:
                        act.wait_ge(f_full[r], k + 1)
                        act.activation(qT[t][:, 0:BANK], bk[:, :], ACT.Identity, bias=ones_at).then_inc(f_drained[r], 1)
                    if n == "l1x" and u == 3:
                        act.wait_ge(f_full[r], k + 1)
                        act.activation(V8[t][:, :, 0:8], split(bk[:, 0:P], 16), ACT.Copy).then_inc(f_drained[r], 1)
                batches(act, n, do, after_second=after_second)

            def turned_stream(n, part=None, **how):
                for g in range(4):
                    r, k = front_use(n, g)
                    act.wait_ge(f_full[r], k + 1)
                    if part is not None:
                        act.activation(part[:, BANK * g:BANK * g + BANK], f_bank[r][:, :], ACT.Copy)
                    act.activation(YT[:, BANK * g:BANK * g + BANK], f_bank[r][:, :], ACT.Copy, **how).then_inc(f_drained[r], 1)

            def experts(M):
                n, H = M["name"], M["halves"]

                def chunk(i, s, c, last):
                    if n == "l0m" and isinstance(i, int) and s == c == 0:
                        for g in range(4):
                            r, k = front_use("l0m", 6 + g)
                            act.wait_ge(f_full[r], k + 1)
                            act.activation(GT[:, BANK * g:BANK * g + BANK], f_bank[r][0:32, :], ACT.Copy).then_inc(f_drained[r], 1)
                    for h in range(H):
                        r, k = place(hid_at[n], CHUNKS * H, i, s, c * H + h)
                        act.wait_ge(g_full[r], k + 1)
                        if M["gated"]:
                            act.wait_ge(h_ready[r], k)
                            act.activation(act_sb[r][:, :], s_bank[r][:, :], ACT.Silu).then_inc(g_drained[r], 1)
                        else:
                            act.activation(hT[(c * H + h) % 4][:, :], s_bank[r][:, :], ACT.Gelu,
                                           bias=wset[s][:, 2 * P:2 * P + 1]).then_inc(h_ready[r], 1)
                sets(act, M, chunk)

            def sines():
                act.wait_ge(step("setup.angles"), 1)
                act.activation(tmpT[:, 2:4, :], tmpT[:, 0:2, :], ACT.Sin).then_inc(step("setup.sin"), 1)

            attention(LAYERS[0], after_second=sines)
            attention(LAYERS[1])
            turned_stream("l0m", scale=vec["gamma2"])
            act.wait_ge(step("l0m.logits"), 1)
            act.activation(ex[:, :, 0:31], lg[:, :, 0:31], ACT.Exp).then_inc(step("l0m.exp"), 1)
            r, k = front_use("l0m", 4)
            act.wait_ge(f_full[r], k + 1)
            act.activation(csum[:, :], f_bank[r][:, 0:B], ACT.Copy, scale=1.0 / P).then_inc(f_drained[r], 1)
            r, k = front_use("l0m", 5)
            act.wait_ge(f_full[r], k + 1)
            act.activation(batch_rows[:, :], f_bank[r][0:B, 0:P], ACT.Copy).then_inc(f_drained[r], 1)
            experts(EXPERTS[0])
            attention(LAYERS[2])
            attention(LAYERS[3])
            turned_stream("l1m", scale=vec["l1f_ln2"])
            act.wait_ge(step("l1m.logits"), 1)
            act.activation(ex[:, :, 0:8], lg[:, :, 0:8], ACT.Exp).then_inc(step("l1m.exp"), 1)
            experts(EXPERTS[1])
            for g, dst in enumerate([PET[:, 0:3 * P], W3T[:, 0:BANK], W3T[:, BANK:2 * BANK], W3T[:, 2 * BANK:9 * P]]):
                r, k = front_use("turn_w3", g)
                act.wait_ge(f_full[r], k + 1)
                act.activation(dst, f_bank[r][:, 0:dst.shape[1]], ACT.Copy).then_inc(f_drained[r], 1)
            turned_stream("l2x")
            turned_stream("l2m", y_part[0])
            act.wait_ge(step("l2m.routed"), 1)
            act.activation(ex[:, :, :], split(router_bank[:, :], B), ACT.Sigmoid).then_inc(step("l2m.router_read"), 1)
            for g in range(4):
                act.wait_ge(step("l2m.rest"), g + 1)
                c = slice(BANK * g, BANK * g + BANK)
                act.activation(y_part[1][:, c], rest[:, c], ACT.Copy).then_inc(step("l2m.second"), 1)
            for g in range(4):
                r, k = front_use("l2m", 5 + g)
                act.wait_ge(f_full[r], k + 1)
                act.activation(gates_turned[:, BANK * g:BANK * g + BANK], f_bank[r][:, :], ACT.Copy).then_inc(f_drained[r], 1)
            experts(EXPERTS[2])
            attention(LAYERS[4])

            act.wait_ge(step("l3m.scale"), 1)
            for g in range(4):
                r, k = front_use("l3m", g)
                act.wait_ge(f_full[r], k + 1)
                act.activation(YT[:, BANK * g:BANK * g + BANK], f_bank[r][:, :], ACT.Identity, scale=quant[:, 0, 3:4],
                               bias=magic).then_inc(f_drained[r], 1)
            for e in range(24):
                r, k = front_use("l3m", 4 + e)
                c, w, m = e // 6, e % 6 // 3, e % 3
                act.wait_ge(f_full[r], k + 1)
                act.activation((U3, G3)[w][:, m, BANK * c:BANK * c + BANK], f_bank[r][:, :], ACT.Copy).then_inc(f_drained[r], 1)
            Uf = U3[:, :, :].rearrange("p m t -> p (m t)")
            act.wait_ge(step("l3m.scale"), 3)

            def rounded(part, n, signal):
                act.activation(part, part, ACT.Identity, scale=quant[:, n, 3:4], bias=magic).then_inc(step(signal), 1)

            def sigmoid(at):
                h = HIDDEN_ORDER[at]
                act.wait_ge(step("l3m.g"), at + 1)
                if at >= 2:
                    act.wait_ge(step("l3m.gs"), at - 1)
                act.activation(sig[at % 2][:, :], big[:, 1024 * h:1024 * h + 1024], ACT.Sigmoid, scale=quant[:, 2, 2:3])\
                    .then_inc(step("l3m.sig"), 1)

            for at, h in enumerate(HIDDEN_ORDER):
                rounded(big[:, 1024 * h:1024 * h + 1024], 2, "l3m.g_round")
                if at:
                    sigmoid(at - 1)
                rounded(Uf[:, 1024 * h:1024 * h + 1024], 1, "l3m.u_round")
            sigmoid(5)
            act.wait_ge(step("l3m.scale"), 4)
            for h in HIDDEN_ORDER:
                rounded(big[:, 1024 * h:1024 * h + 1024], 3, "l3m.round3")
            act.wait_ge(step("l3m.scale"), 5)
            for h in HIDDEN_ORDER[1::2]:
                rounded(big[:, 1024 * h:1024 * h + 1024], 4, "l3m.round4")

        @block.tensor
        def _(pe_):
            def front_begin(n, c):
                r, k = front_use(n, c)
                pe_.wait_ge(f_drained[r], k)
                return f_bank[r], f_full[r]

            def attention(L):
                n, units, F = L["name"], L["units"], L["front"]
                causal = n in ("l0f", "l1f")

                def drained(i, s, job):
                    r, k = place(front_at[n], F, i, s, job)
                    pe_.wait_ge(f_drained[r], k + 1)

                def roped(i, s, piece):
                    at, per = (0, 4) if n == "l0f" else (4 * B, 2)
                    r, k = place(at, per, i, s, piece)
                    pe_.wait_ge(rope_done[r], k + 1)

                def front_job(i, s, u):
                    t = s % 2
                    r, k = place(front_at[n], F, i, s, u)
                    pe_.wait_ge(f_drained[r], k)
                    bk = f_bank[r]

                    def product(cols, w, m, count, x):
                        for q in range(count):
                            last = pe_.matmul(bk[:, cols + P * q:cols + P * q + P], w[:, P * (m + q):P * (m + q) + P], x[:, :],
                                              start=True, stop=True)
                        return last

                    if u == 0:
                        if n == "l0f":
                            pe_.wait_ge(aux_ready[t], s // 2 + 1 + i)
                            last = pe_.transpose(bk[:, 0:P], y_aux[t][:, :], ident)
                        else:
                            pe_.wait_ge(y_ready[t], PAIRS * L["no"] + s // 2 + 1 + i)
                            last = pe_.transpose(bk[:, 0:P], y_tok[t][:, :], ident)
                            if n == "l1x":
                                last = pe_.transpose(bk[:, P:2 * P], y_aux[t][:, :], ident)
                    elif n == "l0x":
                        if u == 1:
                            drained(i, s, 0)
                            last = product(0, W0X[:, 0, :], 0, 4, yT[t])
                        if u == 2:
                            pe_.wait_ge(cT_ready[t], 16 * (s // 2 + 1) + 16 * i)
                            last = product(0, W0X[:, 1, :], 0, 4, cT[t])
                        if u == 3:
                            last = pe_.matmul(bk[:, :], cT[t][:, :], W0X[:, 2, :], start=True, stop=True)
                    elif n == "l0f":
                        if u == 1:
                            drained(i, s, 0)
                        if u < 9:
                            piece = (u - 1) // 2
                            w = w0f[["qa", "qb", "ka", "kb"][2 * (piece // 2) + (u - 1) % 2]]
                            last = product(0, w, 4 * (piece % 2), 4, yT[t])
                        else:
                            last = pe_.matmul(bk[:, :], yT[t][:, :], w0f["v"][:, BANK * (u - 9):BANK * (u - 9) + BANK], start=True, stop=True)
                    elif n == "l1x":
                        if u == 1:
                            drained(i, s, 0)
                            last = product(0, w1x["q"], 0, 4, yT[t])
                        if u == 2:
                            last = product(0, w1x["k"], 0, 4, cT[t])
                        if u == 3:
                            last = pe_.matmul(bk[:, 0:P], cT[t][:, :], w1x["v"], start=True, stop=True)
                    elif n == "l1f":
                        if u == 1:
                            drained(i, s, 0)
                        if u < 3:
                            last = product(0, w1f[("qa", "qb")[u - 1]], 0, 4, yT[t])
                        else:
                            product(0, w1f["ka"], 0, 1, yT[t])
                            product(P, w1f["kb"], 0, 1, yT[t])
                            last = pe_.matmul(bk[:, 2 * P:2 * P + 32], yT[t][:, :], w1f["v"], start=True, stop=True)
                    last.then_inc(f_full[r], 1)

                def uses_drained(i, s, uses):
                    last_of = {}
                    for c in sorted(uses):
                        r, k = place(back_at[n], len(L["back"]), i, s, c)
                        last_of[r] = k
                    for r, k in last_of.items():
                        pe_.wait_ge(b_drained[r], k + 1)

                def operands_ready(i, s, u):
                    if n in ("l0x", "l1x") and u == 0:
                        drained(i, s, 1)
                        drained(i, s, 2)
                    if n == "l0f" and u % 2 == 0:
                        roped(i, s, 2 + u // 2)
                    if n == "l1f" and u == 0:
                        roped(i, s, 0)
                        roped(i, s, 1)
                    if n == "l3x":
                        drained(i, s, 0)
                        pe_.wait_ge(k3_ready[s % 2], 2 * (s // 2) + 2 + 2 * i)

                def do(what, u, i, s):
                    slot = s % 2
                    if what == "F":
                        front_job(i, s, u)
                    if what in ("S", "T", "V"):
                        r, k = place(unit_at[n], units, i, s, u)
                    if what == "S":
                        pe_.wait_ge(shifted_ready[r], k)
                        operands_ready(i, s, u)
                        bk = s_bank[r]
                        if causal:
                            pe_.matmul(bk[:, :], ident_bf, causal_bf, start=True, stop=False, skip_group_check=True)
                        if n == "l3x":
                            pe_.matmul(bk[:, 0:2 * P], ident_bf, own_bf, start=True, stop=False, skip_group_check=True)
                            for m in range(2):
                                last = pe_.matmul(bk[:, P * m:P * m + P], qT[slot][:, P * m:P * m + P], kT[slot][:, P * m:P * m + P],
                                                  start=False, stop=True, skip_group_check=True)
                        else:
                            for m, (_, row, tq, tk, rows, _) in enumerate(heads_of(L, u)):
                                last = pe_.matmul(bk[:, P * m:P * m + P], qT[slot][row:row + rows, P * tq:P * tq + P],
                                                  kT[slot][row:row + rows, P * tk:P * tk + P],
                                                  start=not causal, stop=True, skip_group_check=causal)
                        last.then_inc(s_full[r], 1)
                    if what == "T":
                        pe_.wait_ge(probs_ready[r], k + 1)
                        pe_.wait_ge(probsT_ready[r], k)
                        for m in range(HEADS if units > 1 else 1):
                            last = pe_.transpose(t_bank[r][:, P * m:P * m + P], probs[r][:, P * m:P * m + P], ident)
                        last.then_inc(t_full[r], 1)
                    if what == "V":
                        pe_.wait_ge(probsT_ready[r], k + 1)
                        rb, kb = back_use(L, pv_use(L, u), i, s)
                        if L["dim"] == 64 or u == 0:
                            pe_.wait_ge(b_drained[rb], kb)
                        if n == "l0x" and u == 0:
                            drained(i, s, 3)
                        if n == "l0f" and u % 2 == 0:
                            drained(i, s, 9 + u // 2)
                        if n in ("l1x", "l1f") and u == 0:
                            drained(i, s, 3)
                        bk = v_bank[rb]
                        if n == "l3x":
                            pe_.wait_ge(v_dma[slot], 16 * (s // 2 + 1) + 16 * i)
                            last = pe_.matmul(bk[:, 0:P + 1], probsT[r][:, 0:P], V128[slot][:, :], start=True, stop=True)
                        else:
                            for m, (h, _, _, _, _, hv) in enumerate(heads_of(L, u)):
                                turned_probs = probsT[r][:, P * m:P * m + P]
                                if L["dim"] == 64:
                                    last = pe_.matmul(bk[:, 65 * m:65 * m + 65], turned_probs, V64[slot][:, hv, :], start=True, stop=True)
                                else:
                                    last = pe_.matmul(bk[32 * m:32 * m + 32, P * u:P * u + P], V8[slot][:, hv, :], turned_probs,
                                                      start=True, stop=True)
                        last.then_inc(pv_done[r], 1)
                    if what == "OB":
                        uses_drained(i, s, [0, -1])
                        rb, kb = back_use(L, "OB0", i, s)
                        for v in range(units):
                            last = pe_.transpose(v_bank[rb][:, P * v:P * v + P], spread_o[:, P * v:P * v + P], ident)
                        last.then_inc(regrouped, 1)
                    if what == "OT":
                        c = L["back"].index(f"OT{u}")
                        mine = [L["back"].index(v) for v in ((f"V{2 * u}", f"V{2 * u + 1}") if L["dim"] == 64 else ("OB0",))]
                        uses_drained(i, s, mine + [c - 2])
                        rb, kb = back_use(L, f"OT{u}", i, s)
                        for m in range(4 if L["dim"] == 64 else 1):
                            c = BANK * u + P * m
                            last = pe_.transpose(v_bank[rb][:, P * m:P * m + P], o_tok[slot][:, c:c + P], ident)
                        last.then_inc(turned, 1)
                    if what == "OP":
                        c = L["back"].index("OP0")
                        uses_drained(i, s, [L["back"].index(f"OT{v}") for v in range(L["turns"])] + [c - 2])
                        rb, kb = back_use(L, "OP0", i, s)
                        count = {"l0x": 4, "l0f": 8, "l1x": 1, "l1f": 1}[n]
                        w = {"l0x": W0X[:, 3, :], "l0f": w0f["o"], "l1x": w1x["o"], "l1f": w1f["o"]}[n]
                        for m in range(count):
                            last = pe_.matmul(v_bank[rb][:, 0:P], oT[:, P * m:P * m + P], w[:, P * m:P * m + P],
                                              start=(m == 0), stop=(m == count - 1 and n == "l1f"))
                        if n != "l1f":
                            last = pe_.matmul(v_bank[rb][:, 0:P], ones_row[:, :], bo[n], start=False, stop=True)
                        last.then_inc(projected, 1)
                batches(pe_, n, do)

            def turn_tiles(n, g):
                bk, full = front_begin(n, g)
                pe_.wait_ge(step(n + ".y"), g + 1)
                for m in range(4):
                    last = pe_.transpose(bk[:, P * m:P * m + P], Y[:, 4 * g + m, :], ident)
                last.then_inc(full, 1)

            def tiles_turned(n, g):
                r, k = front_use(n, g)
                pe_.wait_ge(f_drained[r], k + 1)

            def router(n, w):
                for g in range(5):
                    if g < 4:
                        turn_tiles(n, g)
                    if g > 0:
                        tiles_turned(n, g - 1)
                        for b in range(4 * g - 4, 4 * g):
                            last = pe_.matmul(router_bank[:, 32 * b:32 * b + w.shape[1]], YT[:, P * b:P * b + P], w, start=True, stop=True)
                last.then_inc(step(n + ".routed"), 1)

            def experts(M):
                n, H = M["name"], M["halves"]

                def gated_biases():
                    pe_.wait_ge(step("l0m.gates"), 1)
                    for g in range(4):
                        bk, full = front_begin("l0m", 6 + g)
                        for m in range(4):
                            last = pe_.transpose(bk[0:32, P * m:P * m + P], GATES[:, 4 * g + m, 0:32], ident)
                        last.then_inc(full, 1)
                    for g in range(4):
                        r, k = front_use("l0m", 6 + g)
                        pe_.wait_ge(f_drained[r], k + 1)
                    for g in range(4):
                        bk, full = front_begin("l0m", 10 + g)
                        for m in range(4):
                            b = 4 * g + m
                            last = pe_.matmul(bk[:, P * m:P * m + P], GT[:, P * b:P * b + P], B2[:, :], start=True, stop=True)
                        last.then_inc(full, 1)

                def spread_gates(i, s, c):
                    r, k = place(hid_at[n], CHUNKS, i, s, c)
                    pe_.matmul(f_bank[r][:, :], pick[:, bass.ds(P * s + 2 * P * i, P)], gates_turned[:, BANK * c:BANK * c + BANK],
                               start=True, stop=True).then_inc(spread_full[r], 1)

                def hidden(i, s, c):
                    if c == 0 and n == "l2m":
                        pe_.wait_ge(w_loaded[s], 16 * (set_at[n] // 2 + i + 1))
                    elif c == 0:
                        pe_.wait_ge(w_split[s], set_at[n] // 2 + i + 1)
                    if n != "l2m" and isinstance(i, int) and i == s == 0:
                        pe_.wait_ge(y_split, 4 * (n == "l1m") + c + 1)
                    x = slice(BANK * c, BANK * c + BANK)

                    def product(dst, at):
                        if n != "l2m":
                            for part, (wt, y) in enumerate([(w_high, y_high), (w_low, y_high), (w_high, y_low)]):
                                last = pe_.matmul(dst, wt[s][:, at:at + P], y[:, x],
                                                  start=(part == 0), stop=(part == 2))
                            return last
                        for part in range(3):
                            last = pe_.matmul(dst, wraw[s][:, at:at + P], y_part[part][:, x],
                                              start=(part == 0), stop=(part == 2))
                        return last

                    for h in range(H):
                        r, k = place(hid_at[n], CHUNKS * H, i, s, c * H + h)
                        if M["gated"]:
                            pe_.wait_ge(g_drained[r], k - ungated // 2)
                        pe_.wait_ge(h_ready[r], k)
                        product(s_bank[r][:, :], P * h).then_inc(g_full[r], 1)
                        if M["gated"]:
                            product(t_bank[r][:, :], (M["up"] // 2) + P * h).then_inc(u_full[r], 1)
                    if n == "l2m":
                        spread_gates(i, s, c)

                def sums(i, s, c):
                    if n == "l2m" and c == 0:
                        pe_.wait_ge(w_cast[s], i + 1)
                    for h in range(H):
                        r, k = place(hid_at[n], CHUNKS * H, i, s, c * H + h)
                        pe_.wait_ge(h_ready[r], k + 1)
                    r, k = place(sum_at[n], CHUNKS, i, s, c)
                    pe_.wait_ge(d_drained[r], k)
                    for q in range(4):
                        for h in range(H):
                            last = pe_.matmul(v_bank[r][:, P * q:P * q + P], hT[(c * H + h) % 4][:, P * q:P * q + P],
                                              wset[s][:, (M["up"] + P * h):(M["up"] + P * h) + P],
                                              start=(h == 0), stop=(h == H - 1))
                    last.then_inc(d_full[r], 1)

                def chunk(i, s, c, last):
                    if n == "l0m" and isinstance(i, int) and s == c == 0:
                        gated_biases()
                    if not last:
                        hidden(*after(i, s, c))
                    sums(i, s, c)

                if n != "l2m":
                    pe_.wait_ge(step(n + ".router_read"), 1)
                hidden(0, 0, 0)
                sets(pe_, M, chunk)

            pe_.wait_ge(in_c, 16 * 3)
            pe_.wait_ge(in_w0x, 16)
            pe_.wait_ge(step("setup.ones"), 1)
            attention(LAYERS[0])
            pe_.wait_ge(in_w0f, 16)
            pe_.wait_ge(in_cb, 16)
            attention(LAYERS[1])
            pe_.wait_ge(in_rows, 16 * 9)
            router("l0m", RW[:, 0:31])
            pe_.wait_ge(in_w1, 16 * 3)
            pe_.wait_ge(in_ctx, 16)
            bk, full = front_begin("l0m", 4)
            for b in range(B):
                last = pe_.matmul(bk[:, b:b + 1], CTX[:, b, :], part_one, start=True, stop=True)
            last.then_inc(full, 1)
            tiles_turned("l0m", 4)
            bk, full = front_begin("l0m", 5)
            pe_.matmul(bk[0:B, 0:P], csum[:, 0:B], WL2[:, P:2 * P], start=True, stop=False)
            pe_.matmul(bk[0:B, 0:P], ones_row[:, 0:B], bo["l2x"], start=False, stop=True).then_inc(full, 1)
            experts(EXPERTS[0])
            attention(LAYERS[2])
            attention(LAYERS[3])
            router("l1m", RW[:, 31:39])
            experts(EXPERTS[1])

            pe_.wait_ge(step("l3.hot"), 1)
            bk, full = front_begin("turn_w3", 0)
            pe_.matmul(bk[:, 0:3 * P], pe, HOT[:, :, :].rearrange("p m s -> p (m s)"), start=True, stop=True).then_inc(full, 1)
            pe_.wait_ge(step("l3.w3"), 1)
            for g in range(3):
                bk, full = front_begin("turn_w3", 1 + g)
                for m in range(4 * g, min(4 * g + 4, 9)):
                    last = pe_.transpose(bk[:, P * (m - 4 * g):P * (m - 4 * g) + P], W3N[:, P * m:P * m + P], ident)
                last.then_inc(full, 1)

            pe_.wait_ge(step("l2x.spread"), 1)
            for g in range(4):
                if g < 2:
                    r, k = place(sum_at["l1m"], CHUNKS, EXPERTS[1]["steps"] // 2 - 1, 1, 2 + g)
                    pe_.wait_ge(d_drained[r], k + 1)
                pe_.matmul(l2x_bank[g][:, :], ones_sq[0:B, :], context_rows[:, BANK * g:BANK * g + BANK], start=True, stop=False)
            for g in range(5):
                if g < 4:
                    turn_tiles("l2x", g)
                if g > 0:
                    tiles_turned("l2x", g - 1)
                    for m in range(4):
                        b = 4 * (g - 1) + m
                        last = pe_.matmul(l2x_bank[g - 1][:, P * m:P * m + P], YT[:, P * b:P * b + P], WL2[:, 0:P], start=False, stop=(m == 3))
                    last.then_inc(step("l2x.sums"), 1)

            router("l2m", RW[:, 39:71])
            pe_.wait_ge(step("l2m.run"), 1)
            bk, full = front_begin("l2m", 4)
            pe_.matmul(bk[:, :], before, sel[:, :, :].rearrange("p b e -> p (b e)"), start=True, stop=False)
            pe_.matmul(bk[:, :], ones_sq, run[0][:, :, :].rearrange("p b e -> p (b e)"), start=False, stop=True).then_inc(full, 1)
            pe_.wait_ge(step("l2m.gates"), 1)
            for g in range(4):
                bk, full = front_begin("l2m", 5 + g)
                for m in range(4):
                    last = pe_.transpose(bk[:, P * m:P * m + P], gate_sum[:, 4 * g + m, :], ident)
                last.then_inc(full, 1)
            for g in range(2, 4):
                r, k = front_use("l2m", 5 + g)
                pe_.wait_ge(f_drained[r], k + 1)
            pe_.wait_ge(in_pick, 16)
            pe_.wait_ge(step("l2m.third"), 4)
            experts(EXPERTS[2])
            attention(LAYERS[4])

            for g in range(4):
                turn_tiles("l3m", g)
            for c in range(4):
                pe_.wait_ge(step("l3m.yq"), c + 1)
                for e in range(6):
                    w, m = e // 3, e % 3
                    bk, full = front_begin("l3m", 4 + 6 * c + e)
                    wt = W3T[:, P * (3 * (1 - w) + m):P * (3 * (1 - w) + m) + P]
                    pe_.matmul(bk[:, :], wt, YT[:, BANK * c:BANK * c + BANK], start=True, stop=True).then_inc(full, 1)
            for g in range(4):
                pe_.wait_ge(step("l3m.o"), 3 if g < 2 else 6)
                bk, full = front_begin("l3m", 28 + g)
                for q in range(4):
                    b = 4 * g + q
                    for m in range(3):
                        last = pe_.matmul(bk[:, P * q:P * q + P], G3[:, m, P * b:P * b + P], W3T[:, P * (6 + m):P * (6 + m) + P],
                                          start=(m == 0), stop=(m == 2))
                last.then_inc(full, 1)

        @block.vector
        def _(dve):
            links = [0]

            def link(ins):
                links[0] += 1
                ins.then_inc(dve_chain, 1)
                dve.wait_ge(dve_chain, links[0])

            def measure(src, b, stats=None):
                stats = st if stats is None else stats
                dve.bn_stats(stats[:, bass.ds(b, 1), :].rearrange("p o d -> p (o d)"), tile(src, b)).then_inc(tiles_measured, 1)

            def variances(name, part):
                lo, hi = PARTS[name][part]
                dve.wait_ge(tiles_measured, B * list(NORMS).index(name) + hi)
                u, d, m, sq = (x[:, lo:hi] for x in (t0, t1, ms, srow2))
                stats, mu, v, v1 = (cst, cmean, cvar, cve) if name == "ctx" else (st, mean, var, ve)
                stats, mu, v, v1 = stats[:, lo:hi, :], mu[:, lo:hi], v[:, lo:hi], v1[:, lo:hi]
                dve.tensor_tensor(u, stats[:, :, 1], stats[:, :, 4], ALU.add)
                dve.tensor_tensor(d, stats[:, :, 1], stats[:, :, 4], ALU.subtract)
                link(dve.tensor_tensor(m, stats[:, :, 2], stats[:, :, 5], ALU.add))
                dve.tensor_scalar(mu, u, 0.5, None, ALU.mult)
                link(dve.tensor_tensor(sq, d, d, ALU.mult))
                link(dve.scalar_tensor_tensor(v, sq, 32.0, m, ALU.mult, ALU.add))
                for what in NORMS[name]:
                    if what == "rms":
                        link(dve.tensor_tensor(u, mu, mu, ALU.mult))
                        link(dve.scalar_tensor_tensor(u, v, 1.0 / P, u, ALU.mult, ALU.add))
                        last = dve.tensor_scalar(v1, u, EPS, None, ALU.add)
                    elif what == "r12":
                        last = dve.tensor_scalar(ve12[:, lo:hi], v, (1.0 + EPS) / P, EPS * EPS, ALU.mult, ALU.add)
                    else:
                        last = dve.tensor_scalar(v1, v, 1.0 / P, EPS, ALU.mult, ALU.add)
                last.then_inc(step(name + ".var"), 1)

            def powered(name, part):
                dve.wait_ge(step(name + ".r"), part + 1)

            def normalise(n, src, centred):
                part = 0
                for g in range(4):
                    if g == 0 or PARTS[n][part][1] < 4 * g + 4:
                        part += g > 0
                        powered(n, part)
                    for b in range(4 * g, 4 * g + 4):
                        if centred:
                            last = dve.tensor_scalar(Y[:, b, :], src[:, b, :], mean[:, b:b + 1], r1[:, b:b + 1], ALU.subtract, ALU.mult)
                        else:
                            last = dve.tensor_scalar(Y[:, b, :], src[:, b, :], r1[:, b:b + 1], None, ALU.mult)
                    last.then_inc(step(n + ".y"), 1)

            def attention(L):
                n, units = L["name"], L["units"]

                def do(what, u, i, s):
                    b, slot = 2 * i + s, s % 2
                    if what == "Y":
                        last = dve.tensor_scalar(y_tok[slot][:, :], tile(X, b), col(mean, b),
                                                 col(r12 if n in ("l0f", "l1x", "l1f") else r1, b), ALU.subtract, ALU.mult)
                        if n == "l1x":
                            last = dve.tensor_scalar(y_aux[slot][:, :], tile(CTX, b), col(cmean, b),
                                                     col(cr1, b), ALU.subtract, ALU.mult)
                        if n == "l1f":
                            last = dve.tensor_scalar(tile(AO, b), tile(X, b), col(mean, b), col(r1, b), ALU.subtract, ALU.mult)
                        last.then_inc(y_ready[slot], 1)
                        if n == "l0f":
                            dve.wait_ge(y_ready[slot], PAIRS * L["no"] + s // 2 + 1 + i)
                            dve.tensor_tensor(tile(AO, b), y_tok[slot][:, :], gamma1_row, ALU.mult)
                    if what == "F":
                        front_job(i, s, u, b)
                    if what in ("S", "V"):
                        r, k = place(unit_at[n], units, i, s, u)
                    if what == "S":
                        src = split(s_bank[r][:, :], HEADS)
                        heads = HEADS
                        dve.wait_ge(s_full[r], k + 1)
                        if n == "l3x":
                            k3 = place(0, 1, i, s, 0)[1]
                            heads = 1
                            dve.tensor_copy(joined[r][:, :], s_bank[r][:, P:2 * P]).then_inc(grouped_ready[r], 1)
                            dve.wait_ge(grouped_ready[r], k3 + 1)
                            dve.tensor_tensor(joined[r][:, :], s_bank[r][:, 0:P], joined[r][:, :], ALU.max).then_inc(joined_ready[r], 1)
                            dve.wait_ge(joined_ready[r], k3 + 1)
                            src = split(joined[r][:, :], 1)
                        dve.tensor_reduce(row_max[r][:, 0:heads], src, AX_X, ALU.max).then_inc(max_ready[r], 1)
                        dve.wait_ge(max_ready[r], k + 1)
                        dve.wait_ge(probs_ready[r], k)
                        dve.tensor_tensor(split(shifted[r][:, 0:P * heads], heads), src, wide(row_max[r][:, 0:heads], heads, P),
                                          ALU.subtract).then_inc(shifted_ready[r], 1)
                    if what == "V" and L["dim"] != 8:
                        dve.wait_ge(pv_done[r], k + 1)
                        rb, kb = back_use(L, pv_use(L, u), i, s)
                        kr = recips_at[n] + ((units * s + u) // 2 + 1 + units * i if L["dim"] == 64 else s // 2 + 1 + i)
                        rr = r if L["dim"] == 64 else slot
                        bk = v_bank[rb]
                        if L["dim"] == 64:
                            o = split(bk[:, 0:260], HEADS)
                            dve.reciprocal(recips[rr][:, 0:HEADS], o[:, :, 64]).then_inc(recip_ready[rr], 1)
                            dve.wait_ge(recip_ready[rr], kr)
                            h0 = 8 * (u // 2) + u % 2
                            dst = o_tok[slot][:, :].rearrange("p (h d) -> p h d", d=64)[:, h0:h0 + 7:2, :]
                            dve.tensor_tensor(dst, o[:, :, 0:64], wide(recips[rr][:, 0:HEADS], HEADS, 64), ALU.mult).then_inc(b_drained[rb], 1)
                        else:
                            dve.reciprocal(recips[rr][:, 0:1], bk[:, P:P + 1]).then_inc(recip_ready[rr], 1)
                            dve.wait_ge(recip_ready[rr], kr)
                            dve.scalar_tensor_tensor(tile(X, b), bk[:, 0:P], recips[rr][:, 0:1], tile(X, b), ALU.mult, ALU.add)\
                                .then_inc(b_drained[rb], 1)
                            measure_residual(rb, kb, b)
                    if what == "OB":
                        rb, kb = back_use(L, "OB0", i, s)
                        dve.wait_ge(regrouped, regrouped_at[n] + s + 1 + 2 * i)
                        o = split(v_bank[rb][:, :], 16)
                        dve.reciprocal(recips[slot][:, :], o[:, :, 8]).then_inc(recip_ready[slot], 1)
                        dve.wait_ge(recip_ready[slot], recips_at[n] + s // 2 + 1 + i)
                        dst = split(o_tok[slot][:, 0:P], 16)
                        by = wide(recips[slot][:, :], 16, 8)
                        if n == "l1x":
                            dve.scalar_tensor_tensor(dst, o[:, :, 0:8], col(NANF, b), by, ALU.mult, ALU.mult).then_inc(b_drained[rb], 1)
                        else:
                            dve.tensor_tensor(dst, o[:, :, 0:8], by, ALU.mult).then_inc(b_drained[rb], 1)
                    if what == "OP":
                        rb, kb = back_use(L, "OP0", i, s)
                        dve.wait_ge(projected, proj_at[n] + s + 1 + 2 * i)
                        if n in ("l0x", "l1x"):
                            dve.tensor_tensor(tile(X, b), v_bank[rb][:, 0:P], tile(X, b), ALU.add).then_inc(b_drained[rb], 1)
                        else:
                            dve.tensor_tensor(tile(AO, b), v_bank[rb][:, 0:P], tile(AO, b), ALU.add).then_inc(b_drained[rb], 1)
                        measure_residual(rb, kb, b)

                def measure_residual(rb, kb, b):
                    dve.wait_ge(b_drained[rb], kb + 1)
                    dve.tensor_copy(waited[:, 1:2], waited[:, 0:1])
                    measure(AO if n in ("l0f", "l1f") else X, b)

                def front_job(i, s, u, b):
                    t = s % 2
                    r, k = place(front_at[n], L["front"], i, s, u)
                    bk = f_bank[r]
                    four = split(bk[:, :], 4)
                    if n == "l0x" and u == 3:
                        dve.wait_ge(f_full[r], k + 1)
                        dve.tensor_copy(V64[t][:, 0:8, 0:64], split(bk[:, :], 8)).then_inc(f_drained[r], 1)
                    if n == "l0f" and 1 <= u <= 8 or n == "l1f" and u in (1, 2):
                        piece = (u - 1) // 2
                        at, per = (0, 4) if n == "l0f" else (4 * B, 2)
                        q, kq = place(at, per, i, s, piece)
                        dve.wait_ge(f_full[r], k + 1)
                        dve.wait_ge(rope_done[q], kq)
                        odd = (u - 1) % 2
                        table = (sin0 if odd else cos0) if n == "l0f" else (sin1 if odd else cos1)
                        dve.tensor_tensor(split((rope_b if odd else rope_a)[q][:, :], 4), four, over(table, 4), ALU.mult).then_inc(f_drained[r], 1)
                    if n == "l0f" and u >= 9:
                        h0 = 8 * (u - 9)
                        dve.wait_ge(f_full[r], k + 1)
                        dve.tensor_tensor(V64[t][:, h0:h0 + 8, 0:64], split(bk[:, :], 8), split(VB[:, BANK * (u - 9):BANK * (u - 9) + BANK], 8),
                                          ALU.add).then_inc(f_drained[r], 1)
                    if n == "l1x" and u == 2:
                        dve.wait_ge(f_full[r], k + 1)
                        dve.scalar_tensor_tensor(split(kT[t][:, 0:BANK], 4), tile(MASK, b).unsqueeze(1).to_broadcast([P, 4, P]), ones_at,
                                                 four, ALU.mult, ALU.add).then_inc(f_drained[r], 1)
                    if n == "l1f" and u == 3:
                        q, kq = place(4 * B, 2, i, s, 1)
                        dve.wait_ge(f_full[r], k + 1)
                        dve.wait_ge(rope_done[q], kq)
                        dve.tensor_tensor(rope_a[q][:, 0:P], bk[:, 0:P], cos1, ALU.mult)
                        dve.tensor_tensor(rope_b[q][:, 0:P], bk[:, P:2 * P], sin1, ALU.mult)
                        dve.tensor_copy(V8[t][:, 0:4, 0:8], split(bk[:, 2 * P:2 * P + 32], 4)).then_inc(f_drained[r], 1)
                    if n == "l3x":
                        dve.wait_ge(f_full[r], k + 1)
                        dve.tensor_tensor(qT[t][:, 0:P], bk[:, 0:P], PET[:, 0:P], ALU.add)
                        dve.tensor_tensor(qT[t][:, P:2 * P], bk[:, 0:P], PET[:, P:2 * P], ALU.add).then_inc(f_drained[r], 1)
                powered(n, 0)
                batches(dve, n, do, after_first=lambda: powered(n, 1), before_last=lambda: variances(AFTER[n], 0))
                variances(AFTER[n], 1)

            def high_part(dst, src):
                return dve.tensor_scalar(dst.bitcast(I32), src.bitcast(I32), 12, 12, ALU.logical_shift_right, ALU.logical_shift_left)

            def two_parts(high, low, src, first):
                dve.tensor_copy(high, first)
                return dve.tensor_tensor(low, src, first, ALU.subtract)

            def split_stream(n):
                for g in range(4):
                    r, k = front_use(n, g)
                    dve.wait_ge(f_drained[r], k + 1)
                    c = slice(BANK * g, BANK * g + BANK)
                    link(high_part(rope_a[g % 2][:, :], YT[:, c]))
                    two_parts(y_high[:, c], y_low[:, c], YT[:, c], rope_a[g % 2][:, :]).then_inc(y_split, 1)

            def top(n, k, E):
                for b in range(B):
                    last = dve.max(top8[:, b, :], ex[:, b, 0:E])
                link(last)
                for b in range(B):
                    last = dve.max_index(idx8[:, b, :], top8[:, b, :], ex[:, b, 0:E])
                link(last)
                link(dve.tensor_copy(idxf[:, :, :], idx8[:, :, :]))
                iota = iota_row[:, 0:E].unsqueeze(1).unsqueeze(1).to_broadcast([P, B, k, E])
                link(dve.tensor_tensor(hits[:, :, 0:k, 0:E], iota, idxf[:, :, 0:k].unsqueeze(3).to_broadcast([P, B, k, E]), ALU.is_equal))
                link(dve.tensor_reduce(sel[:, :, 0:E], hits[:, :, 0:k, 0:E].rearrange("p b k e -> p b e k"), AX_X, ALU.add))

            def row_scale(dst, src, by, E):
                return dve.tensor_tensor(dst, src, wide(by, B, E), ALU.mult)

            def softmax_gates(n, E, k, bias, exact):
                dve.wait_ge(step(n + ".routed"), 1)
                logits = split(router_bank[:, :], B)[:, :, 0:E]
                if bias is not None:
                    link(dve.tensor_tensor(lg[:, :, 0:E], logits, over(bias, B), ALU.add))
                else:
                    link(dve.tensor_copy(lg[:, :, 0:E], logits))
                dve.sem_inc(step(n + ".router_read"), 1)
                link(dve.tensor_reduce(srow0, lg[:, :, 0:E], AX_X, ALU.max))
                dve.tensor_tensor(lg[:, :, 0:E], lg[:, :, 0:E], wide(srow0, B, E), ALU.subtract).then_inc(step(n + ".logits"), 1)
                dve.wait_ge(step(n + ".exp"), 1)
                link(dve.tensor_reduce(srow0, ex[:, :, 0:E], AX_X, ALU.add))
                link(dve.reciprocal(srow1, srow0))
                link(row_scale(ex[:, :, 0:E], ex[:, :, 0:E], srow1, E))
                top(n, k, max(E, 8) + (E == 31))
                if exact:
                    link(dve.tensor_tensor(lg[:, :, 0:E], ex[:, :, 0:E], sel[:, :, 0:E], ALU.mult))
                    link(dve.tensor_reduce(srow0, lg[:, :, 0:E], AX_X, ALU.add))
                    link(dve.reciprocal(srow1, srow0))
                    link(row_scale(GATES[:, :, 0:E], lg[:, :, 0:E], srow1, E))
                else:
                    link(dve.tensor_tensor(GATES[:, :, 0:E], ex[:, :, 0:E], sel[:, :, 0:E], ALU.mult))
                dve.sem_inc(step(n + ".gates"), 1)

            def halve(M, i, s):
                dve.wait_ge(w_loaded[s], 16 * (set_at[M["name"]] // 2 + i + 1))
                cols, first = slice(0, M["up"]), rope_b[s][:, 0:M["up"]]
                high_part(first, wset[s][:, cols]).then_inc(w_highs[s], 1)
                dve.wait_ge(w_highs[s], set_at[M["name"]] // 2 + i + 1)
                two_parts(w_high[s][:, cols], w_low[s][:, cols], wset[s][:, cols], first).then_inc(w_split[s], 1)

            def experts(M):
                n, H = M["name"], M["halves"]

                def hidden(i, s, c):
                    if not M["gated"]:
                        return
                    for h in range(H):
                        r, k = place(hid_at[n], CHUNKS * H, i, s, c * H + h)
                        dve.wait_ge(g_drained[r], k - ungated // 2 + 1)
                        dve.wait_ge(u_full[r], k - ungated // 2 + 1)
                        dst = hT[(c * H + h) % 4]
                        if n == "l2m":
                            dve.tensor_tensor(act_sb[r][:, :], t_bank[r][:, :], act_sb[r][:, :], ALU.mult).then_inc(product_ready[r], 1)
                            kc = place(0, CHUNKS, i, s, c)[1]
                            dve.wait_ge(product_ready[r], kc + 1)
                            dve.wait_ge(spread_full[r], kc + 1)
                            dve.tensor_tensor(dst[:, :], f_bank[r][:, :], act_sb[r][:, :], ALU.mult).then_inc(h_ready[r], 1)
                        else:
                            dve.tensor_tensor(dst[:, :], t_bank[r][:, :], act_sb[r][:, :], ALU.mult).then_inc(h_ready[r], 1)

                def chunk(i, s, c, last):
                    if n == "l0m" and isinstance(i, int) and s == c == 0:
                        for g in range(4):
                            r, k = front_use("l0m", 10 + g)
                            dve.wait_ge(f_full[r], k + 1)
                            last = dve.tensor_tensor(X[:, 4 * g:4 * g + 4, :], split(f_bank[r][:, :], 4), X[:, 4 * g:4 * g + 4, :], ALU.add)
                            last.then_inc(f_drained[r], 1)
                            dve.wait_ge(f_drained[r], k + 1)
                    if not last:
                        hidden(*after(i, s, c))
                    r, k = place(sum_at[n], CHUNKS, i, s, c)
                    dve.wait_ge(d_full[r], k + 1)
                    if n != "l2m" and c == 1 and not last_set(i, s):
                        halve(M, i + s, 1 - s)
                    if n == "l2m":
                        tiles = X[:, 4 * c:4 * c + 4, :]
                        dve.tensor_tensor(tiles, split(v_bank[r][:, :], 4), tiles, ALU.add).then_inc(d_drained[r], 1)
                    else:
                        for q in range(4):
                            tok = 4 * c + q
                            ins = dve.scalar_tensor_tensor(X[:, tok, :], v_bank[r][:, P * q:P * q + P],
                                                           GATES[:, tok, bass.ds(2 * i + s, 1)], X[:, tok, :], ALU.mult, ALU.add)
                        ins.then_inc(d_drained[r], 1)
                    if last_set(i, s):
                        dve.wait_ge(d_drained[r], k + 1)
                        for tok in range(4 * c, 4 * c + 4):
                            measure(X, tok)
                        if c == 2:
                            variances(AFTER[n], 0)
                    if n == "l0m" and isinstance(i, int) and s == 0:
                        if c == 0:
                            dve.wait_ge(in_ctx, 16)
                        for tok in range(4 * c, 4 * c + 4):
                            measure(CTX, tok, cst)
                        if c == CHUNKS - 1:
                            variances("ctx", 0)
                            dve.wait_ge(in_rows, 16 * 9)
                            dve.tensor_scalar(POSG[:, :], POSI[:, :], 4, None, ALU.arith_shift_right).then_inc(step("l3.groups"), 1)
                            dve.wait_ge(step("setup.mask_read"), 1)
                            dve.tensor_reduce(NANF[:, :], MASK[:, :, :], AX_X, ALU.max).then_inc(step("setup.keys"), 1)
                    if n == "l1m" and isinstance(i, int) and s == 0 and c == 0:
                        dve.wait_ge(in_w3, 16)
                        link(dve.tensor_reduce(W3M[:, :], W3N[:, :].rearrange("p (n m) -> p n m", m=32), AX_X, ALU.max,
                                               apply_absolute_value=True))
                        link(dve.tensor_scalar(W3S[:, :], W3M[:, :], 1.0 / 7.0, 1e-12, ALU.mult, ALU.max))
                        dve.reciprocal(W3R[:, :], W3S[:, :]).then_inc(step("l3.w3_steps"), 1)
                    if n == "l2m" and c == 0 and not last_set(i, s):
                        cast(i + s, 1 - s)

                def last_set(i, s):
                    return isinstance(i, int) and 2 * i + s == M["steps"] - 1

                def cast(i, s):
                    dve.wait_ge(w_loaded[s], 16 * (set_at[n] // 2 + i + 1))
                    dve.tensor_copy(wset[s][:, M["up"]:M["wcols"]], wraw[s][:, M["up"]:M["wcols"]]).then_inc(w_cast[s], 1)

                if n == "l2m":
                    cast(0, 0)
                hidden(0, 0, 0)
                sets(dve, M, chunk)
                variances(AFTER[n], 1)

            dve.wait_ge(in_x, 16 * 2)
            for b in range(B):
                measure(X, b)
            variances("l0x", 0)
            variances("l0x", 1)
            attention(LAYERS[0])
            dve.wait_ge(step("setup.tables"), 1)
            dve.wait_ge(in_rows, 16 * 9)
            attention(LAYERS[1])

            normalise("l0m", AO, False)
            for g in range(4):
                r, k = front_use("l0m", g)
                dve.wait_ge(f_full[r], k + 1)
                dve.tensor_tensor(Y[:, 4 * g:4 * g + 4, :], Y[:, 4 * g:4 * g + 4, :], over(gamma2_row, 4), ALU.mult).then_inc(step("l0m.an"), 1)
            split_stream("l0m")
            halve(EXPERTS[0], 0, 0)
            softmax_gates("l0m", 31, 3, RB[:, :], False)
            dve.wait_ge(step("l0m.x_ready"), 1)
            experts(EXPERTS[0])
            dve.wait_ge(step("setup.mask"), 1)
            powered("ctx", 0)
            attention(LAYERS[2])
            attention(LAYERS[3])
            normalise("l1m", AO, False)
            split_stream("l1m")
            halve(EXPERTS[1], 0, 0)
            softmax_gates("l1m", 8, 2, None, True)
            dve.wait_ge(step("l1m.x_ready"), 1)
            experts(EXPERTS[1])
            normalise("l2x", X, True)
            for g in range(4):
                dve.wait_ge(step("l2x.sums"), g + 1)
                link(dve.tensor_tensor(X[:, 4 * g:4 * g + 4, :], split(l2x_bank[g][:, :], 4), X[:, 4 * g:4 * g + 4, :], ALU.add))
                for b in range(4 * g, 4 * g + 4):
                    measure(X, b)
                if g % 2:
                    variances("l2m", g // 2)
            normalise("l2m", X, True)
            dve.wait_ge(step("l2m.router_read"), 1)
            link(dve.tensor_copy(lg[:, :, :], ex[:, :, :]))
            link(dve.tensor_tensor(ex[:, :, :], ex[:, :, :], over(LB[:, :], B), ALU.add))
            top("l2m", 4, 32)
            link(dve.memset(run[0][:, 0:1, :], 0.0))
            link(dve.tensor_copy(run[0][:, 1:B, :], sel[:, 0:B - 1, :]))
            src = 0
            for hop in (1, 2, 4, 8):
                dve.tensor_copy(run[1 - src][:, 0:hop, :], run[src][:, 0:hop, :])
                link(dve.tensor_tensor(run[1 - src][:, hop:B, :], run[src][:, hop:B, :], run[src][:, 0:B - hop, :], ALU.add))
                src = 1 - src
            dve.sem_inc(step("l2m.run"), 1)
            link(dve.tensor_tensor(lg[:, :, :], lg[:, :, :], sel[:, :, :], ALU.mult))
            link(dve.tensor_reduce(srow0, lg[:, :, :], AX_X, ALU.add))
            link(dve.tensor_scalar(srow0, srow0, 1e-12, None, ALU.max))
            link(dve.reciprocal(srow1, srow0))
            link(row_scale(lg[:, :, :], lg[:, :, :], srow1, 32))
            r, k = front_use("l2m", 4)
            dve.wait_ge(f_full[r], k + 1)
            link(dve.tensor_scalar(ex[:, :, :], split(f_bank[r][:, :], B), float(CAPACITY), None, ALU.is_lt))
            dve.sem_inc(f_drained[r], 1)
            gates = GATES[:, :, 0:32]
            link(dve.tensor_tensor(gates, lg[:, :, :], ex[:, :, :], ALU.mult))
            dve.memset(gate_sum[:, :, 96:P], 1.0)
            link(dve.tensor_copy(gate_part[0], gates))
            link(dve.tensor_tensor(lg[:, :, :], gates, gate_part[0], ALU.subtract))
            link(dve.tensor_copy(gate_part[1], lg[:, :, :]))
            for part in range(2):
                dve.tensor_copy(gate_sum[:, :, 32 * part:32 * part + 32], gate_part[part])
            dve.tensor_tensor(gate_sum[:, :, 64:96], lg[:, :, :], gate_part[1], ALU.subtract).then_inc(step("l2m.gates"), 1)
            experts(EXPERTS[2])
            dve.sem_inc(step("l3x.begin"), 1)
            attention(LAYERS[4])

            normalise("l3m", X, True)
            dve.wait_ge(step("l3m.y"), 4)

            def scale(n, waits, unit=None):
                dve.wait_ge(step("l3m.all_max"), waits)
                if unit is None:
                    link(dve.tensor_scalar(quant[:, n, 2:3], quant[:, n, 1:2], 1.0 / QMAX, 1e-12, ALU.mult, ALU.max))
                    dve.reciprocal(quant[:, n, 3:4], quant[:, n, 2:3]).then_inc(step("l3m.scale"), 1)
                else:
                    held = quant[:, unit, 2:3]
                    link(dve.tensor_scalar(quant[:, n, 1:2], quant[:, n, 1:2], held, None, ALU.mult))
                    link(dve.tensor_scalar(quant[:, n, 2:3], quant[:, n, 1:2], 1.0 / QMAX, 1e-12, ALU.mult, ALU.max))
                    link(dve.reciprocal(quant[:, n, 3:4], quant[:, n, 2:3]))
                    dve.tensor_scalar(quant[:, n, 3:4], quant[:, n, 3:4], held, None, ALU.mult).then_inc(step("l3m.scale"), 1)

            def largest(dst, src):
                return dve.tensor_reduce(dst, src, AX_X, ALU.max, apply_absolute_value=True)

            largest(quant[:, 0, 0:1], Y[:, :, :].rearrange("p b d -> p (b d)")).then_inc(step("l3m.part_max"), 1)
            scale(0, 1)
            for g in range(4):
                r, k = front_use("l3m", g)
                dve.wait_ge(f_drained[r], k + 1)
                part = YT[:, BANK * g:BANK * g + BANK]
                dve.tensor_scalar(part, part, MAGIC, quant[:, 0, 2:3], ALU.subtract, ALU.mult).then_inc(step("l3m.yq"), 1)
            for e in range(24):
                r, k = front_use("l3m", 4 + e)
                c, w, m = e // 6, e % 6 // 3, e % 3
                dve.wait_ge(f_drained[r], k + 1)
                last = largest(part_max[:, 12 * w + 3 * c + m:12 * w + 3 * c + m + 1], (U3, G3)[w][:, m, BANK * c:BANK * c + BANK])
            link(last)
            link(largest(quant[:, 1, 0:1], part_max[:, 0:12]))
            largest(quant[:, 2, 0:1], part_max[:, 12:24]).then_inc(step("l3m.part_max"), 1)
            scale(1, 2)
            scale(2, 3)
            def product_max(last, n):
                link(last)
                largest(quant[:, n, 0:1], part_max[:, 0:6]).then_inc(step("l3m.part_max"), 1)

            def gate_steps(at):
                part = big[:, 1024 * HIDDEN_ORDER[at]:1024 * HIDDEN_ORDER[at] + 1024]
                dve.wait_ge(step("l3m.g_round"), at + 1)
                dve.tensor_scalar(part, part, MAGIC, None, ALU.subtract).then_inc(step("l3m.g"), 1)

            gate_steps(0)
            for at, h in enumerate(HIDDEN_ORDER):
                part, sg = big[:, 1024 * h:1024 * h + 1024], sig[at % 2][:, :]
                if at < 5:
                    gate_steps(at + 1)
                dve.wait_ge(step("l3m.sig"), at + 1)
                link(dve.tensor_scalar(sg, sg, 65535.0 / 65536.0, MAGIC / 65536.0, ALU.min, ALU.add))
                dve.scalar_tensor_tensor(part, sg, MAGIC / 65536.0, part, ALU.subtract, ALU.mult).then_inc(step("l3m.gs"), 1)
                dve.wait_ge(step("l3m.gs"), at + 1)
                last = largest(part_max[:, at:at + 1], part)
            product_max(last, 3)
            scale(3, 4, 2)
            for at, h in enumerate(HIDDEN_ORDER):
                part = big[:, 1024 * h:1024 * h + 1024]
                dve.wait_ge(step("l3m.round3"), at + 1)
                dve.wait_ge(step("l3m.u"), at + 1)
                link(dve.scalar_tensor_tensor(part, part, MAGIC, U3[:, :, :].rearrange("p m t -> p (m t)")[:, 1024 * h:1024 * h + 1024],
                                              ALU.subtract, ALU.mult))
                last = largest(part_max[:, h:h + 1], part)
            product_max(last, 4)
            scale(4, 5, 3)
            dve.wait_ge(step("l3m.scale"), 5)
            for at, h in enumerate(HIDDEN_ORDER):
                part = big[:, 1024 * h:1024 * h + 1024]
                if at % 2:
                    dve.wait_ge(step("l3m.round4"), at // 2 + 1)
                else:
                    link(dve.tensor_scalar(part, part, quant[:, 4, 3:4], MAGIC, ALU.mult, ALU.add))
                dve.tensor_scalar(part, part, MAGIC, quant[:, 4, 2:3], ALU.subtract, ALU.mult).then_inc(step("l3m.o"), 1)
            for g in range(4):
                r, k = front_use("l3m", 28 + g)
                dve.wait_ge(f_full[r], k + 1)
                dve.tensor_tensor(X[:, 4 * g:4 * g + 4, :], split(f_bank[r][:, :], 4), X[:, 4 * g:4 * g + 4, :], ALU.add)\
                    .then_inc(f_drained[r], 1)


def _layout(v):
    import numpy as np

    f = np.float32
    bf = v["L2_ffn_W1"].dtype
    D = P
    A = {}

    def arr(name):
        return np.asarray(v[name])

    A["x"], A["ctx"] = arr("x"), arr("ctx_1024")
    A["ctxT"] = arr("ctx_1024").transpose(0, 2, 1)
    A["pos"] = arr("pos_1xS2").astype(np.int32).reshape(1, P)
    A["mask"] = arr("mask_BxS2_bf1").view(np.uint8).reshape(1, B * P)

    def tiles(w):
        n = w.shape[0] // P
        return w.reshape(n, P, -1).transpose(1, 0, 2).reshape(P, -1)

    A["w0x"] = np.concatenate([arr("L0_xattn_Wq"), arr("L0_xattn_Wk"), arr("L0_xattn_Wv"), tiles(arr("L0_xattn_Wo"))], 1)

    def evens_odds(w, swap):
        w = w.reshape(w.shape[0], 16, 32, 2).transpose(0, 1, 3, 2)
        return (w[:, :, ::-1] if swap else w).reshape(w.shape[0], 1024)

    parts = [evens_odds(arr(n), s) for n in ("L0_ffn_q_w", "L0_ffn_k_w") for s in (0, 1)]
    A["w0f"] = np.concatenate(parts + [arr("L0_ffn_v_w"), tiles(arr("L0_ffn_o_w"))], 1)
    biases = [evens_odds(arr(n).reshape(1, -1), s).reshape(8, P).T for n in ("L0_ffn_q_b", "L0_ffn_k_b") for s in (0, 1)]

    def spread(w, head_of, count, order):
        out = np.zeros((D, count, 4, 32), w.dtype)
        for m in range(count):
            for g in range(4):
                h = head_of(m, g)
                out[:, m, g, 0:8] = w[:, 8 * h:8 * h + 8][:, order]
        return out.reshape(D, count * P)

    same, swapped = list(range(8)), [4, 5, 6, 7, 0, 1, 2, 3]
    head = lambda m, g: 4 * g + m
    A["w1x"] = np.concatenate([spread(arr("L1_xattn_Wq").T, head, 4, same), spread(arr("L1_xattn_Wk").T, head, 4, same),
                               arr("L1_xattn_Wv").T, arr("L1_xattn_Wo").T], 1)
    qkv = arr("L1_ffn_wqkv").T
    q, k, vv = qkv[:, 0:128], qkv[:, 128:160], qkv[:, 160:192]
    A["w1f"] = np.concatenate([spread(q, head, 4, same), spread(q, head, 4, swapped), spread(k, lambda m, g: g, 1, same),
                               spread(k, lambda m, g: g, 1, swapped), vv, arr("L1_ffn_wo").T], 1)
    A["wl2"] = np.concatenate([arr("L2_xattn_W")[:, 0:D].T, arr("L2_xattn_W")[:, D:].T], 1)
    A["w3"] = np.concatenate([tiles(arr("L3_ffn_w_gate")), tiles(arr("L3_ffn_w_up")), arr("L3_ffn_w_down")], 1)
    cols = [arr("L1_xattn_g1"), arr("L1_xattn_b1"), arr("L1_xattn_g2"), arr("L1_xattn_b2"), arr("L1_ffn_ln1_w"),
            arr("L1_ffn_ln2_w"), np.tile(arr("L0_ffn_theta"), 4), arr("L0_ffn_gamma2")]
    A["vec"] = np.concatenate([c.reshape(P, 1) for c in cols] + biases, 1)
    A["rows"] = np.concatenate([arr("L0_ffn_gamma1"), arr("L0_ffn_gamma2")]).reshape(1, -1)
    A["l0f_vb"] = arr("L0_ffn_v_b").reshape(1, -1)
    A["l0m_rb"] = arr("L0_ffn_router_b").reshape(1, -1)
    A["l2m_bias"] = arr("L2_ffn_bias").reshape(1, -1)
    A["brow"] = np.concatenate([arr("L0_xattn_bo"), arr("L0_ffn_o_b"), arr("L1_xattn_bo"), arr("L2_xattn_b")]).reshape(1, -1)
    A["b2"] = np.concatenate([arr("L0_ffn_re_b2"), arr("L0_ffn_sh_b2").reshape(1, D)], 0)
    A["rw"] = np.concatenate([arr("L0_ffn_router_w"), arr("L1_ffn_gate_w").T], 1)
    A["rwb"] = arr("L2_ffn_gate_w").T
    w1 = np.concatenate([arr("L0_ffn_re_w1"), arr("L0_ffn_sh_w1")[None]], 0)
    w2 = np.concatenate([arr("L0_ffn_re_w2"), arr("L0_ffn_sh_w2")[None]], 0)
    b1 = np.concatenate([arr("L0_ffn_re_b1"), arr("L0_ffn_sh_b1")[None]], 0)
    A["l0m"] = np.concatenate([w1, w2, b1[:, :, None]], 2)
    w2 = arr("L1_ffn_w2").transpose(0, 2, 1).reshape(8, 2, P, D).transpose(0, 2, 1, 3).reshape(8, P, 2 * D)
    A["l1m"] = np.concatenate([arr("L1_ffn_w13").transpose(0, 2, 1), w2], 2)
    sets = np.zeros((17, P, 3 * P), bf)
    sets[:16, :, 0:P] = arr("L2_ffn_W1").reshape(16, 2, D, 64).transpose(0, 2, 1, 3).reshape(16, D, P)
    sets[:16, :, P:2 * P] = arr("L2_ffn_W3").reshape(16, 2, D, 64).transpose(0, 2, 1, 3).reshape(16, D, P)
    sets[:16, :, 2 * P:] = arr("L2_ffn_W2").reshape(16, P, D)
    sets[16, :, 0:64] = arr("L2_ffn_sw1").T
    sets[16, :, P:P + 64] = arr("L2_ffn_sw3").T
    sets[16, 0:64, 2 * P:] = arr("L2_ffn_sw2").T
    A["l2m"] = sets

    n = np.arange(P)
    pos = np.arange(P, dtype=f)
    div = np.exp(np.arange(0, D, 2, dtype=f) * f(-(math.log(10000.0) / D))).astype(f)
    ang = pos[:, None] * div
    table = np.stack([np.sin(ang), np.cos(ang)], -1).reshape(P, D).astype(f)
    inv = (f(1.0) / f(10000.0) ** (np.arange(0, 8, 2, dtype=f) / f(8))).astype(f)
    freq = (pos[:, None] * inv[None, :]).astype(f)
    emb = np.concatenate([freq, freq], 1)
    cos1, sin1 = np.zeros((P, P), f), np.zeros((P, P), f)
    for g in range(4):
        for d in range(8):
            cos1[32 * g + d] = np.cos(emb[:, d])
            sin1[32 * g + d] = np.sin(emb[:, d]) * (-1 if d < 4 else 1)
    cols = np.stack([n.astype(f), (n % 32 == 8).astype(f), np.where(n // 32 % 2 == 0, -1, 1).astype(f), np.full(P, MAGIC, f)], 1)
    A["cf"] = np.concatenate([np.eye(P, dtype=f), (n[:, None] < n[None, :]).astype(f), np.tile(pos, (P, 1)), table, cos1, sin1,
                              cols, np.ones((P, P), f)], 1)
    pick = np.zeros((4, 32, 17, 2, 64), bf)
    for e in range(32):
        pick[0:3, e, e // 2, e % 2, :] = 1
    pick[3, 0, 16] = 1
    A["pick"] = pick.reshape(P, 17 * P)
    causal = n[None, :] <= n[:, None]
    grouped = n[None, :] <= n[:, None] - 64
    hide = lambda keep: np.where(keep, 0.0, NEG).astype(bf)
    A["cb"] = np.concatenate([np.eye(P, dtype=bf)] + [hide(causal)] * HEADS + [hide(causal & ~grouped), hide(grouped)], 1)
    return A


def kernel(**inputs):
    import numpy as np
    import concourse.bacc as bacc
    from concourse.bass_utils import run_bass_kernel_spmd

    nc = bacc.Bacc("TRN2", target_bir_lowering=False, num_devices=1)
    arrays, aps = {}, {}
    for name, value in _layout(inputs).items():
        value = np.ascontiguousarray(value)
        arrays[f"in_{name}"] = value
        aps[name] = nc.dram_tensor(f"in_{name}", value.shape, mybir.dt.from_np(value.dtype), kind="ExternalInput").ap()
    out = nc.dram_tensor("out_x", (B, P, P), F32, kind="ExternalOutput").ap()
    build(nc, aps, out)
    r = run_bass_kernel_spmd(nc, [arrays], core_ids=[0])
    return r.results[0]["out_x"]
```
